# Optimizing a Trainium2 kernel written in Bass

```python
import numpy as np
import jax
import jax.numpy as jnp

def _softmax(x, axis=-1):
    return jax.nn.softmax(x, axis=axis)

def _gelu(x):
    return jax.nn.gelu(x, approximate=True)

def _silu(x):
    return jax.nn.silu(x)

def _sigmoid(x):
    return jax.nn.sigmoid(x)

def _layernorm(x, axis=-1, eps=1e-05):
    m = jnp.mean(x, axis=axis, keepdims=True)
    v = jnp.var(x, axis=axis, keepdims=True)
    return (x - m) / jnp.sqrt(v + eps)

def _scatter_add(tgt, idx, src, axis=0):
    return tgt.at[idx].add(src)

def _segment_sum(src, seg, n):
    return jax.ops.segment_sum(src, seg, n)
kernel_name = 'mk_gnn_resnorm_d2_gnn_r8_73b5a0'

def setup_inputs(seed: int=0):
    np.random.seed(seed)
    _w = jnp.asarray

    def _rec_inputs():
        import jax
        import jax.numpy as jnp
        _gk = jax.random.key(seed)
        x = -0.000202 + 1 * jax.random.normal(jax.random.fold_in(_gk, 1), (12500, 128), jnp.float32)
        src = jax.random.randint(jax.random.fold_in(_gk, 2), (200000,), 0, 12500, jnp.int32)
        dst = jax.random.randint(jax.random.fold_in(_gk, 3), (200000,), 0, 12500, jnp.int32)
        _o = jnp.argsort(dst, stable=True)
        src = src[_o]
        dst = dst[_o]
        return (x, src, dst)
    x, src, dst = _rec_inputs()

    def _L0_gnn_setup():
        import jax, jax.numpy as jnp
        import numpy as np
        ALPHA = 0.2
        BN_EPS = 1e-05
        N_NODES = 6250
        N_EDGES = 200000
        DIM_IN = 128
        DIM_HID = 64
        DIM_OUT = 128
        NUM_HEADS = 8

        def gat_layer(feat, src, dst, W, a, gamma, beta):
            n = feat.shape[0]
            dh = W.shape[1]
            msg = feat @ W
            attn_src = msg @ a[:dh]
            attn_dst = msg @ a[dh:]
            scores = jax.nn.leaky_relu(attn_src[src] + attn_dst[dst], ALPHA)
            scores = scores - scores.max()
            e = jnp.exp(scores)
            denom = jax.ops.segment_sum(e, dst, num_segments=n) + 1e-10
            coef = e / denom[dst]
            out = jax.ops.segment_sum(msg[src] * coef[:, None], dst, num_segments=n)
            mean = out.mean(axis=0)
            var = out.var(axis=0)
            out = (out - mean) * jax.lax.rsqrt(var + BN_EPS) * gamma + beta
            return out
        key = jax.random.key(seed)
        ks = jax.random.split(key, 10)
        feat = jax.random.normal(ks[0], (N_NODES, DIM_IN), dtype=jnp.float32)
        edges = jax.random.randint(ks[1], (2, N_EDGES), 0, N_NODES)

        def xavier(k, shape):
            fan_in, fan_out = (shape[0], shape[-1])
            lim = np.sqrt(6.0 / (fan_in + fan_out)).astype(np.float32)
            return jax.random.uniform(k, shape, jnp.float32, -lim, lim)
        W_heads = xavier(ks[2], (NUM_HEADS, DIM_IN, DIM_HID))
        a_heads = xavier(ks[3], (NUM_HEADS, 2 * DIM_HID))
        gamma_h = jnp.ones((NUM_HEADS, DIM_HID), jnp.float32)
        beta_h = jnp.zeros((NUM_HEADS, DIM_HID), jnp.float32)
        W_out = xavier(ks[4], (NUM_HEADS * DIM_HID, DIM_OUT))
        a_out = xavier(ks[5], (2 * DIM_OUT,))
        gamma_o = jnp.ones((DIM_OUT,), jnp.float32)
        beta_o = jnp.zeros((DIM_OUT,), jnp.float32)
        W_res = xavier(ks[6], (DIM_IN, DIM_OUT))
        b_res = jnp.zeros((DIM_OUT,), jnp.float32)
        return {'feat': feat, 'edges': edges, 'W_heads': W_heads, 'a_heads': a_heads, 'gamma_h': gamma_h, 'beta_h': beta_h, 'W_out': W_out, 'a_out': a_out, 'gamma_o': gamma_o, 'beta_o': beta_o, 'W_res': W_res, 'b_res': b_res}
    _L0_gnn_all = _L0_gnn_setup()
    _L0_gnn_in = {k: v for k, v in _L0_gnn_all.items() if k in ('W_heads', 'a_heads', 'gamma_h', 'beta_h', 'W_out', 'a_out', 'gamma_o', 'beta_o', 'W_res', 'b_res')}
    del _L0_gnn_all

    def _L1_gnn_setup():
        import jax, jax.numpy as jnp
        import numpy as np
        N, E, D = (6250, 100000, 128)
        BN_EPS = 1e-05

        def _sage_conv(x, src, dst, Wl, Wr, b):
            n = x.shape[0]
            msg = x[src]
            agg = jax.ops.segment_sum(msg, dst, num_segments=n)
            cnt = jax.ops.segment_sum(jnp.ones((src.shape[0],), x.dtype), dst, num_segments=n)
            agg = agg / jnp.maximum(cnt, 1.0)[:, None]
            return agg @ Wl.T + x @ Wr.T + b

        def _bn_eval(x, gamma, beta, rmean, rvar):
            return (x - rmean) * (gamma / jnp.sqrt(rvar + BN_EPS)) + beta
        key = jax.random.key(seed)
        ks = jax.random.split(key, 12)
        s = 1.0 / np.sqrt(D)
        inp = {'x': jax.random.normal(ks[0], (N, D), jnp.float32), 'edge_index': jax.random.randint(ks[1], (2, E), 0, N, jnp.int32), 'Wl0': jax.random.normal(ks[2], (D, D), jnp.float32) * s, 'Wr0': jax.random.normal(ks[3], (D, D), jnp.float32) * s, 'b0': jnp.zeros((D,), jnp.float32), 'g0': jnp.ones((D,), jnp.float32), 'be0': jnp.zeros((D,), jnp.float32), 'rm0': jax.random.normal(ks[4], (D,), jnp.float32) * 0.1, 'rv0': jax.random.uniform(ks[5], (D,), jnp.float32, 0.5, 1.5), 'Wl1': jax.random.normal(ks[6], (D, D), jnp.float32) * s, 'Wr1': jax.random.normal(ks[7], (D, D), jnp.float32) * s, 'b1': jnp.zeros((D,), jnp.float32), 'g1': jnp.ones((D,), jnp.float32), 'be1': jnp.zeros((D,), jnp.float32), 'rm1': jax.random.normal(ks[8], (D,), jnp.float32) * 0.1, 'rv1': jax.random.uniform(ks[9], (D,), jnp.float32, 0.5, 1.5)}
        return inp
    _L1_gnn_all = _L1_gnn_setup()
    _L1_gnn_in = {k: v for k, v in _L1_gnn_all.items() if k in ('Wl0', 'Wr0', 'b0', 'g0', 'be0', 'rm0', 'rv0', 'Wl1', 'Wr1', 'b1', 'g1', 'be1', 'rm1', 'rv1')}
    del _L1_gnn_all
    return {'x': x, 'src': src, 'dst': dst, 'L0_gnn_W_heads': _L0_gnn_in['W_heads'], 'L0_gnn_a_heads': _L0_gnn_in['a_heads'], 'L0_gnn_gamma_h': _L0_gnn_in['gamma_h'], 'L0_gnn_beta_h': _L0_gnn_in['beta_h'], 'L0_gnn_W_out': _L0_gnn_in['W_out'], 'L0_gnn_a_out': _L0_gnn_in['a_out'], 'L0_gnn_gamma_o': _L0_gnn_in['gamma_o'], 'L0_gnn_beta_o': _L0_gnn_in['beta_o'], 'L0_gnn_W_res': _L0_gnn_in['W_res'], 'L0_gnn_b_res': _L0_gnn_in['b_res'], 'L1_gnn_Wl0': _L1_gnn_in['Wl0'], 'L1_gnn_Wr0': _L1_gnn_in['Wr0'], 'L1_gnn_b0': _L1_gnn_in['b0'], 'L1_gnn_g0': _L1_gnn_in['g0'], 'L1_gnn_be0': _L1_gnn_in['be0'], 'L1_gnn_rm0': _L1_gnn_in['rm0'], 'L1_gnn_rv0': _L1_gnn_in['rv0'], 'L1_gnn_Wl1': _L1_gnn_in['Wl1'], 'L1_gnn_Wr1': _L1_gnn_in['Wr1'], 'L1_gnn_b1': _L1_gnn_in['b1'], 'L1_gnn_g1': _L1_gnn_in['g1'], 'L1_gnn_be1': _L1_gnn_in['be1'], 'L1_gnn_rm1': _L1_gnn_in['rm1'], 'L1_gnn_rv1': _L1_gnn_in['rv1']}

def reference(x, src, dst, L0_gnn_W_heads, L0_gnn_a_heads, L0_gnn_gamma_h, L0_gnn_beta_h, L0_gnn_W_out, L0_gnn_a_out, L0_gnn_gamma_o, L0_gnn_beta_o, L0_gnn_W_res, L0_gnn_b_res, L1_gnn_Wl0, L1_gnn_Wr0, L1_gnn_b0, L1_gnn_g0, L1_gnn_be0, L1_gnn_rm0, L1_gnn_rv0, L1_gnn_Wl1, L1_gnn_Wr1, L1_gnn_b1, L1_gnn_g1, L1_gnn_be1, L1_gnn_rm1, L1_gnn_rv1):
    import jax
    import jax.numpy as jnp

    def _L0_gnn_ref(feat, edges, W_heads, a_heads, gamma_h, beta_h, W_out, a_out, gamma_o, beta_o, W_res, b_res):
        import jax, jax.numpy as jnp
        import numpy as np
        ALPHA = 0.2
        BN_EPS = 1e-05
        N_NODES = 6250
        N_EDGES = 200000
        DIM_IN = 128
        DIM_HID = 64
        DIM_OUT = 128
        NUM_HEADS = 8

        def gat_layer(feat, src, dst, W, a, gamma, beta):
            n = feat.shape[0]
            dh = W.shape[1]
            msg = feat @ W
            attn_src = msg @ a[:dh]
            attn_dst = msg @ a[dh:]
            scores = jax.nn.leaky_relu(attn_src[src] + attn_dst[dst], ALPHA)
            scores = scores - scores.max()
            e = jnp.exp(scores)
            denom = jax.ops.segment_sum(e, dst, num_segments=n) + 1e-10
            coef = e / denom[dst]
            out = jax.ops.segment_sum(msg[src] * coef[:, None], dst, num_segments=n)
            mean = out.mean(axis=0)
            var = out.var(axis=0)
            out = (out - mean) * jax.lax.rsqrt(var + BN_EPS) * gamma + beta
            return out
        src, dst = (edges[0], edges[1])
        head_outs = [gat_layer(feat, src, dst, W_heads[h], a_heads[h], gamma_h[h], beta_h[h]) for h in range(NUM_HEADS)]
        x = jnp.concatenate(head_outs, axis=-1)
        x = gat_layer(x, src, dst, W_out, a_out, gamma_o, beta_o)
        x = x + feat @ W_res + b_res
        return x

    def _L1_gnn_ref(x, edge_index, Wl0, Wr0, b0, g0, be0, rm0, rv0, Wl1, Wr1, b1, g1, be1, rm1, rv1):
        import jax, jax.numpy as jnp
        import numpy as np
        N, E, D = (6250, 100000, 128)
        BN_EPS = 1e-05

        def _sage_conv(x, src, dst, Wl, Wr, b):
            n = x.shape[0]
            msg = x[src]
            agg = jax.ops.segment_sum(msg, dst, num_segments=n)
            cnt = jax.ops.segment_sum(jnp.ones((src.shape[0],), x.dtype), dst, num_segments=n)
            agg = agg / jnp.maximum(cnt, 1.0)[:, None]
            return agg @ Wl.T + x @ Wr.T + b

        def _bn_eval(x, gamma, beta, rmean, rvar):
            return (x - rmean) * (gamma / jnp.sqrt(rvar + BN_EPS)) + beta
        src, dst = (edge_index[0], edge_index[1])
        h = _sage_conv(x, src, dst, Wl0, Wr0, b0)
        h = jax.nn.relu(_bn_eval(h, g0, be0, rm0, rv0))
        h = _sage_conv(h, src, dst, Wl1, Wr1, b1)
        return _bn_eval(h, g1, be1, rm1, rv1)
    edge_index = jnp.stack([src, dst])
    x = _layernorm(x + _L0_gnn_ref(x, edge_index, L0_gnn_W_heads, L0_gnn_a_heads, L0_gnn_gamma_h, L0_gnn_beta_h, L0_gnn_W_out, L0_gnn_a_out, L0_gnn_gamma_o, L0_gnn_beta_o, L0_gnn_W_res, L0_gnn_b_res), axis=-1)
    x = _layernorm(x + _L1_gnn_ref(x, edge_index, L1_gnn_Wl0, L1_gnn_Wr0, L1_gnn_b0, L1_gnn_g0, L1_gnn_be0, L1_gnn_rm0, L1_gnn_rv0, L1_gnn_Wl1, L1_gnn_Wr1, L1_gnn_b1, L1_gnn_g1, L1_gnn_be1, L1_gnn_rm1, L1_gnn_rv1), axis=-1)
    return x

_drawn_inputs = setup_inputs


def setup_inputs(seed=0):
    import zlib

    import numpy as np

    out = dict(_drawn_inputs(seed))
    spreads = {'L0_gnn_gamma_h': (1.0, 0.2),
     'L0_gnn_beta_h': (0.0, 0.724),
     'L0_gnn_gamma_o': (1.0, 0.2),
     'L0_gnn_beta_o': (0.0, 0.1),
     'L0_gnn_b_res': (0.0, 0.1),
     'L1_gnn_b0': (0.0, 0.1),
     'L1_gnn_g0': (1.0, 0.2),
     'L1_gnn_be0': (0.0, 0.1),
     'L1_gnn_b1': (0.0, 0.1),
     'L1_gnn_g1': (1.0, 0.2),
     'L1_gnn_be1': (0.0, 0.1)}
    factors = {}
    for name, (base, spread) in spreads.items():
        noise = np.random.default_rng([zlib.crc32(name.encode()), seed]).standard_normal(out[name].shape)
        drawn = base * np.exp(spread * noise) if base else spread * noise
        out[name] = jnp.asarray(drawn.astype(out[name].dtype))
    for name, factor in factors.items():
        out[name] = (out[name] * factor).astype(out[name].dtype)
    return out
```

```python
from contextlib import ExitStack, contextmanager

import numpy as np
import concourse.bass as bass
from concourse import mybir

F32 = mybir.dt.float32
I32 = mybir.dt.int32
I16 = mybir.dt.int16
ALU = mybir.AluOpType
ACT = mybir.ActivationFunctionType
AX = mybir.AxisListType.X
ds = bass.ds

N = 12500
E = 200000
D = 128
H = 8
DH = 64
NP_ = 125
NT = N // NP_
CH = 2 * NP_
NC = N // CH
EP = 125
ET = E // EP
TH = 8
PAIRS = TH // 2
SB = ET // (2 * TH)
NPAIR = ET // 2
WIN = 24
NS = 5
SN = N // NS
NV = NS + 1
WHOLE = NS
SW = SN + WIN
NW = N + WIN
HP = H // 2
FC = 500
NFC = SN // FC
ROW0 = D + H
ROW1 = D + 1
SLOPE = 0.2
BN_EPS = 1e-5
LN_EPS = 1e-5
DEN_EPS = 1e-10
TINY = 1.2e-38
BIG = 1e30


class Links:

    def __init__(self, eng, sem, base=0):
        self.eng, self.sem, self.base, self.k = eng, sem, base, 0

    def __call__(self, ins):
        self.k += 1
        ins.then_inc(self.sem, 1)
        self.eng.wait_ge(self.sem, self.base + self.k)


@contextmanager
def by_two(eng, n):
    with eng.Fori(0, n // 2) as i:
        yield i * 2


def gnn_kernel(nc, x, src_t, dst_t, dst, W_heads, a_heads, gamma_h, beta_h, W_out, a_out, gamma_o, beta_o,
               W_res, b_res, Wl0, Wr0, b0, g0, be0, rm0, rv0, Wl1, Wr1, b1, g1, be1, rm1, rv1, out):
    ctx = ExitStack()
    with ctx:
        def sb(name, shape, dt=F32):
            return ctx.enter_context(nc.sbuf_tensor(name, shape, dt))

        def psb(name, shape):
            return ctx.enter_context(nc.psum_tensor(name, shape, F32))

        def sem(name):
            return ctx.enter_context(nc.semaphore(name))

        def dram(name, shape, dt=F32):
            return nc.dram_tensor(name, shape, dt).ap()

        t_gat0 = dram("t_gat0", (N, ROW0))
        t_gat1 = dram("t_gat1", (N, ROW1))
        t_sage0 = dram("t_sage0", (N, D))
        t_sage1 = dram("t_sage1", (N, D))
        win0_d = dram("win0_d", (NW, 2 * H + 1))
        win1_d = dram("win1_d", (NW, 3))
        dsc0_d = dram("dsc0_d", (H, N))
        dsc1_d = dram("dsc1_d", (1, N))
        den0_d = dram("den0_d", (H, N))
        y1_d = dram("y1_d", (HP, D, N))
        base_d = dram("base_d", (NV, NPAIR), I32)
        baser_d = dram("baser_d", (NV, NPAIR), I32)
        span_d = dram("span_d", (NV, 2 * SB), I32)

        acc = sb("acc", [128, H * SW])
        den = sb("den", [H, NW])
        acc8 = acc[:, :].rearrange("p (h n) -> p h n", h=H)
        dstf = sb("dstf", [EP, ET], I16)
        dsti = acc[0:EP, 0:ET].bitcast(I32)
        basef = sb("basef", [EP, NV, NPAIR], I16)
        basei = acc[0:EP, 2048:2048 + NV * NPAIR].bitcast(I32)
        baser = sb("baser", [1, NV * NPAIR], I32)
        spanr = sb("spanr", [1, NV * 2 * SB], I32)
        lohi = sb("lohi", [1, 2 * NS], I32)
        rows_all = sb("rows", [EP, 2 * TH * ROW0])
        rows = rows_all[:, :].rearrange("p (t k) -> p t k", t=2 * TH)
        idx = sb("idx", [EP, 2 * TH], I32)
        adw = sb("adw", [WIN, PAIRS, 2 * H + 1])
        cur = sb("cur", [EP, PAIRS])
        rel = sb("rel", [EP, TH])
        oh = sb("oh", [EP, TH, WIN])
        oht = sb("oht", [WIN, TH * EP])
        s_t = sb("s_t", [EP, TH, H])
        s_l = sb("s_l", [EP, TH, H])
        s_m = sb("s_m", [EP, TH, H])
        s_d = sb("s_d", [EP, TH, H])
        pen = sb("pen", [EP, TH])
        smax = sb("smax", [EP, TH, H])
        wgt = sb("wgt", [EP, TH, H])
        rhs_all = sb("rhs", [128, TH * H * WIN])
        rhs = rhs_all[0:EP, :].rearrange("p (t k) -> p t k", t=TH)
        s1col = sb("s1col", [EP, 1])
        ident = sb("ident", [128, 128])
        iota_w = sb("iota_w", [EP, WIN])
        ones = sb("ones", [128, CH])
        sel = sb("sel", [H, HP, 128])
        w_sb = acc[:, 14400:14400 + H * DH].rearrange("p (h j) -> p h j", h=H)
        wz = sb("wz", [128, H, 128])
        a_bc = acc[:, 16384:16384 + 2 * H * DH].rearrange("p (h j) -> p h j", h=H)
        wa = sb("wa", [128, 2 * H])
        prod = acc[:, 0:HP * D]
        woa = sb("woa", [128, HP, D + 2])
        wob = sb("wob", [128, HP, D + 2])
        ao_bc = acc[:, 17500:17500 + 2 * D].rearrange("p (r j) -> p r j", r=2)
        gh = sb("gh", [128, HP])
        bh = sb("bh", [128, HP])
        stats = acc[:, H * SW - HP * NC * 6:].rearrange("p (h c k) -> p h c k", h=HP, c=NC)
        mv = sb("mv", [128, HP, 2])
        scl = sb("scl", [128, HP])
        shf = sb("shf", [128, HP])
        go = sb("go", [128, 1])
        bo = sb("bo", [128, 1])
        brow = sb("brow", [1, D + 2])
        bres = sb("bres", [1, D])
        w_a = sb("w_a", [128, D])
        w_b = sb("w_b", [128, D])
        stg = sb("stg", [128, 2, FC])
        vrow = stg[:, :, :].rearrange("p u n -> p (u n)")[:, 0:5 * D].rearrange("p (i n) -> p i n", i=5)
        col1 = sb("col1", [128, 2 * H])
        amax = sb("amax", [128, H])
        a8 = sb("a8", [H, 1])
        m8 = sb("m8", [H, 1])
        t8 = sb("t8", [H, H])
        big8 = sb("big8", [H, 128])
        nsc = acc[0:NP_, 0:NT * 2 * H].rearrange("p (t k) -> p t k", t=NT)
        nwin = acc[0:NP_, 2048:2048 + NT * (2 * H + 1)].rearrange("p (t k) -> p t k", t=NT)
        nlr = acc[0:NP_, 4096:4096 + NT * H].rearrange("p (t k) -> p t k", t=NT)
        pairs_i = acc[0:SB, 8192:8192 + 2 * TH * EP].bitcast(I32)
        pairs_f = acc[0:SB, 12288:12288 + 2 * TH * EP]
        gmin = sb("gmin", [SB, 2 * PAIRS])
        gmax = sb("gmax", [SB, 2 * PAIRS])
        tb_b = sb("tb_b", [SB, NV, 2 * PAIRS])
        tb_r = sb("tb_r", [SB, NV, 2 * PAIRS])
        tb_e = sb("tb_e", [SB, NV, 2 * PAIRS])
        tb_s = sb("tb_s", [SB, NV, 2])
        tb_bi = sb("tb_bi", [SB, NV, 2 * PAIRS], I32)
        tb_ri = sb("tb_ri", [SB, NV, 2 * PAIRS], I32)
        tb_si = sb("tb_si", [SB, NV, 2], I32)
        bmn = sb("bmn", [SB, 2])
        tch = sb("tch", [SB, 3])
        pidx = sb("pidx", [SB, 2])
        cand = sb("cand", [SB, 2 * NS])
        c10 = sb("c10", [2 * NS, 1])
        lh = sb("lh", [1, 2 * NS])
        def two(buf, p, at, width):
            return buf[0:p, at:at + 2 * width].rearrange("p (u n) -> p u n", u=2)

        xt = two(rhs_all, NP_, 0, D)
        ht = two(rhs_all, NP_, 2 * D, D)
        xT = two(rhs_all, 128, 4 * D, NP_)
        aT = two(rhs_all, 128, 6 * D, NP_)
        rowb = sb("rowb", [NP_, 2, ROW0])
        zt = two(rhs_all, NP_, 8 * D, D)
        lnst = sb("lnst", [NP_, 2, 6])
        lnmv = sb("lnmv", [NP_, 2, 2])
        lnr = sb("lnr", [NP_, 2])
        y1 = acc[:, 8192:8192 + 2 * HP * CH].rearrange("p (u c n) -> p u c n", u=2, c=HP)
        d8, q8, e8, r8 = (two(rows_all, H, 2 * CH * i, CH) for i in range(4))

        bank = [psb(f"bank{i}", [128, 512]) for i in range(2)]
        p_oht = psb("p_oht", [128, 2, 512])
        p_adx = psb("p_adx", [128, 512])
        p_den = psb("p_den", [128, 512])
        p_big = psb("p_big", [128, 2, 512])

        cst = sem("cst")
        cst_l = sem("cst_l")
        alone = sem("alone")
        phase = sem("phase")
        sp_in = sem("sp_in")
        sp_out = sem("sp_out")
        dve_l = sem("dve_l")
        cand_ready = sem("cand_ready")
        cand_t = sem("cand_t")
        lh_col = sem("lh_col")
        lh_row = sem("lh_row")
        tables = sem("tables")
        mx_part = sem("mx_part")
        mx_t = sem("mx_t")
        mx_diag = sem("mx_diag")
        mx_bc = sem("mx_bc")
        win_ready = sem("win_ready")
        sqrt_arg = sem("sqrt_arg")
        sqrt_done = sem("sqrt_done")
        m_ready = sem("m_ready")
        bn_ready = sem("bn_ready")
        bias_ps = sem("bias_ps")
        bias_sb = sem("bias_sb")
        idx_in = [sem(f"idx_in{i}") for i in range(2)]
        rows_in = [sem(f"rows_in{i}") for i in range(2)]
        rows_used = [sem(f"rows_used{i}") for i in range(2)]
        adw_in = sem("adw_in")
        oh_ready = sem("oh_ready")
        oht_ps = sem("oht_ps")
        oht_sb = sem("oht_sb")
        adx_ready = sem("adx_ready")
        exp_arg = sem("exp_arg")
        wgt_ready = sem("wgt_ready")
        rhs_ready = sem("rhs_ready")
        sums_ps = sem("sums_ps")
        dve_w = sem("dve_w")
        dve_b = sem("dve_b")
        dve_r = sem("dve_r")
        fl_ps = sem("fl_ps")
        fl_sb = sem("fl_sb")
        fl_out = [sem(f"fl_out{i}") for i in range(2)]
        fl_free = sem("fl_free")
        rng_done = sem("rng_done")
        den_out = sem("den_out")

        def phase_sems(name, plain, primed=()):
            S = {k: sem(f"{name}_{k}") for k in tuple(plain) + tuple(primed)}
            S["primed"] = [S[k] for k in primed]
            return S

        n_x = phase_sems("n_x", ("in0", "in1", "xps", "row", "out0", "out1"), ("xsb", "mps", "msb", "asb", "stored"))
        n_bn = phase_sems("n_bn", ("in0", "in1", "add", "bound", "expd", "rec", "bc", "row", "stat", "own", "out0", "out1"))
        n_msg = phase_sems("n_msg", ("in0", "in1", "mps", "out0", "out1"), ("used", "row", "msb", "dsb", "stored"))
        n_gn = phase_sems("n_gn", ("in0", "in1", "add", "bound", "expd", "rec", "bc", "own"), ("row",))
        n_c = [phase_sems(f"n_c{k}", ("rec", "bc", "own")) for k in range(2)]
        n_fin = [phase_sems(f"n_f{k}", ("in0", "in1", "xps", "acp", "var", "std", "row", "own", "out0", "out1"),
                            ("xsb", "mps", "msb", "stored"))
                 for k in range(3)]

        block = ctx.enter_context(nc.Block())
        ENGINES = 5

        def phase_end(eng, k):
            eng.drain().then_inc(phase, 1)
            eng.wait_ge(phase, ENGINES * k)

        def node_ranges(eng, spec, body, after=None, before=None, last=None):
            if spec["parts"]:
                with eng.Fori(0, NS) as s:
                    lo = eng.value_load(lohi[0:1, ds(s + NS, 1)], min_val=0, max_val=SB - 1)
                    hi = eng.value_load(lohi[0:1, ds(s, 1)], min_val=1, max_val=SB)
                    if before:
                        before(lo)
                    with eng.Fori(lo, hi) as b:
                        body(s * SN, s, b)
                    if last:
                        last()
                    if after:
                        after(s)
            else:
                if before:
                    before(0)
                with eng.Fori(0, SB) as b:
                    body(0, WHOLE, b)
                if last:
                    last()

        def load_span(eng, v, b, half):
            return eng.value_load(spanr[0:1, ds(v * (2 * SB) + b * 2 + half, 1)], min_val=1, max_val=N)

        MAX_BLOCKS = (NS + 3) * SB
        MAX_WINDOWS = 2 * SB * (NS * (SN // WIN + 1) + 3 * (N // WIN + 1))

        def count(eng, reg, most):
            eng.reg_add(reg, reg, 1)
            return eng.snap(reg, min_val=1, max_val=most)

        G0 = dict(table=t_gat0, width=ROW0, heads=H, weighted=True, parts=True, window=win0_d, cols=SN, count=True)
        G1 = dict(table=t_gat1, width=ROW1, heads=1, weighted=True, parts=False, window=win1_d, cols=N, count=True)
        S0 = dict(table=t_sage0, width=D, heads=1, weighted=False, parts=False, cols=N, count=True)
        S1 = dict(table=t_sage1, width=D, heads=1, weighted=False, parts=False, cols=N, count=False)

        def acc_view(spec):
            return acc8 if spec["heads"] == H else acc[:, 0:NW].rearrange("p (h n) -> p h n", h=1)

        def sums(q, h):
            return (bank[q][:, 0:h * WIN] if q < 2 else p_big[:, q - 2, 0:h * WIN])

        NCHUNK = HP * NFC

        def pool_pass(eng, spec, nb, ni):
            def body(s0, v, b):
                c = count(eng, nb, MAX_BLOCKS)
                i = count(eng, ni, 2 * MAX_BLOCKS)
                for half in range(2):
                    eng.wait_ge(idx_in[half], i * 16)
                    eng.wait_ge(rows_used[half], c)
                    eng.sem_inc(alone, 1)
                    for j in range(half * TH, half * TH + TH):
                        eng.indirect_dma_start(rows[:, j, 0:spec["width"]], None, spec["table"],
                                               bass.IndirectOffsetOnAxis(ap=idx[:, j:j + 1], axis=0)
                                               ).then_inc(rows_in[half], 16)
            node_ranges(eng, spec, body, last=lambda: eng.reg_add(ni, ni, 1))

        def pool_store(eng, S, primed, src, table, width):
            with by_two(eng, NT) as t:
                for u in range(2):
                    eng.wait_ge(S["row"], t + (u + 1 + primed))
                    eng.dma_start(table[ds((t + u) * NP_, NP_), :], src[:, u, 0:width]).then_inc(S[f"out{u}"], 16)
                for u in range(2):
                    eng.wait_ge(S[f"out{u}"], t * 8 + 16)
                    eng.sem_inc(S["stored"], 1)

        @block.gpsimd
        def _(eng):
            nb = eng.alloc_register("nb_pool")
            ni = eng.alloc_register("ni_pool")
            eng.reg_mov(nb, 0)
            eng.reg_mov(ni, 0)
            link = Links(eng, cst_l)
            eng.memset(ones[:, :], 1.0).then_inc(cst, 1)
            link(eng.memset(ident[:, :], 0.0))
            link(eng.memset(sel[:, :, :], 0.0))
            eng.affine_select(out=ident[:, :], in_=ident[:, :], compare_op=ALU.not_equal, fill=1.0, base=0,
                              pattern=[[-1, 128]], channel_multiplier=1).then_inc(cst, 1)
            for r in range(2):
                v = sel[:, :, r * DH:(r + 1) * DH]
                eng.affine_select(out=v, in_=v, compare_op=ALU.not_equal, fill=1.0, base=-r,
                                  pattern=[[-2, HP], [0, DH]], channel_multiplier=1).then_inc(cst, 1)
            eng.iota(iota_w[:, :], pattern=[[1, WIN]], base=0, channel_multiplier=0,
                     allow_small_or_imprecise_dtypes=True).then_inc(cst, 1)
            eng.iota(pidx[:, 0:1], pattern=[[0, 1]], base=1, channel_multiplier=1,
                     allow_small_or_imprecise_dtypes=True).then_inc(cst, 1)
            eng.iota(pidx[:, 1:2], pattern=[[0, 1]], base=SB, channel_multiplier=-1,
                     allow_small_or_imprecise_dtypes=True).then_inc(cst, 1)
            for i in range(2):
                eng.sem_inc(rows_used[i], 1)
            eng.sem_inc(adx_ready, 1)
            eng.sem_inc(sums_ps, PAIRS)
            eng.sem_inc(rhs_ready, PAIRS)
            eng.sem_inc(fl_sb, 2)
            eng.sem_inc(fl_free, 2)
            for S in (n_x, n_bn, n_msg, n_gn, *n_fin):
                for s_ in S["primed"]:
                    eng.sem_inc(s_, 2)
            phase_end(eng, 1)
            pool_store(eng, n_x, 0, rowb, t_gat0, ROW0)
            phase_end(eng, 2)
            pool_pass(eng, G0, nb, ni)
            phase_end(eng, 3)
            phase_end(eng, 4)
            pool_store(eng, n_msg, 2, rowb, t_gat1, ROW1)
            phase_end(eng, 5)
            pool_pass(eng, G1, nb, ni)
            phase_end(eng, 6)
            phase_end(eng, 7)
            pool_store(eng, n_fin[0], 0, zt, t_sage0, D)
            phase_end(eng, 8)
            pool_pass(eng, S0, nb, ni)
            phase_end(eng, 9)
            phase_end(eng, 10)
            pool_store(eng, n_fin[1], 0, zt, t_sage1, D)
            phase_end(eng, 11)
            pool_pass(eng, S1, nb, ni)
            phase_end(eng, 12)
            phase_end(eng, 13)
            pool_store(eng, n_fin[2], 0, zt, out, D)
            phase_end(eng, 14)

        def sp_pass(eng, spec, nb, ni, nw, nxt, bases):
            def load_idx(half, block_):
                eng.dma_start(idx[:, half * TH:half * TH + TH],
                              src_t[:, ds(block_ * (2 * TH) + half * TH, TH)]).then_inc(idx_in[half], 16)

            def before(lo):
                eng.reg_add(ni, ni, 1)
                for half in range(2):
                    load_idx(half, lo)

            def last():
                i = eng.snap(ni, min_val=1, max_val=2 * MAX_BLOCKS)
                for half in range(2):
                    eng.wait_ge(idx_in[half], i * 16)
                eng.sem_inc(alone, 1)

            def body(s0, v, b):
                c = count(eng, nb, MAX_BLOCKS)
                eng.reg_add(ni, ni, 1)
                for half in range(2):
                    if spec["weighted"]:
                        windows(s0, v, b, half)
                    eng.reg_mov(nxt, b + 1)
                    eng.reg_alu(nxt, nxt, SB - 1, ALU.min)
                    eng.wait_ge(rows_in[half], c * (16 * TH))
                    load_idx(half, eng.snap(nxt, min_val=0, max_val=SB - 1))

            def windows(s0, v, b, half):
                span = load_span(eng, v, b, half)
                eng.load(bases, baser[0:1, ds(v * NPAIR + b * (2 * PAIRS) + half * PAIRS, PAIRS)])
                with eng.Fori(0, span, WIN):
                    w = count(eng, nw, MAX_WINDOWS)
                    eng.wait_ge(adx_ready, w)
                    for q in range(PAIRS):
                        at = eng.snap(bases[q], min_val=0, max_val=spec["cols"])
                        eng.dma_start(adw[:, q, 0:2 * spec["heads"] + 1],
                                      spec["window"][ds(at + s0, WIN), :]).then_inc(adw_in, 16)
                    for q in range(PAIRS):
                        eng.reg_add(bases[q], bases[q], WIN)
                        eng.reg_alu(bases[q], bases[q], spec["cols"], ALU.min)

            def after(s):
                eng.wait_ge(rng_done, s + 1)
                eng.dma_start(den0_d[:, ds(s * SN, SN)], den[:, 0:SN]).then_inc(den_out, 16)
                for i in range(NCHUNK):
                    p, ck, u = i % HP, i // HP, i % 2
                    eng.wait_ge(fl_sb, s * NCHUNK + (i + 1 + 2))
                    eng.dma_start(y1_d[p, :, ds(s * SN + ck * FC, FC)], stg[:, u, :]).then_inc(fl_out[u], 16)
                    for k in ([i - 1] if i else []) + ([i] if i == NCHUNK - 1 else []):
                        eng.wait_ge(fl_out[k % 2], s * (16 * NCHUNK // 2) + 16 * (k // 2 + 1))
                        eng.sem_inc(fl_free, 1)
            node_ranges(eng, spec, body, after if spec["parts"] else None, before, last)

        def sp_node(eng, S, first, second=None):
            with by_two(eng, NT) as t:
                for u in range(2):
                    eng.wait_ge(S["stored"], t + (u + 1))
                    eng.dma_start(xt[:, u, :], first[ds((t + u) * NP_, NP_), :]).then_inc(S[f"in{u}"], 16)
                    if second is not None:
                        eng.dma_start(ht[:, u, :], second[ds((t + u) * NP_, NP_), :]).then_inc(S[f"in{u}"], 16)

        def chunk(src, at):
            return src[:, :, ds(at, CH)].rearrange("c p n -> p c n")

        @block.sync
        def _(eng):
            nb = eng.alloc_register("nb_sp")
            ni = eng.alloc_register("ni_sp")
            nxt = eng.alloc_register("nxt_sp")
            eng.reg_mov(ni, 0)
            nw = eng.alloc_register("nw_sp")
            bases = [eng.alloc_register(f"base_sp{q}") for q in range(PAIRS)]
            eng.reg_mov(nb, 0)
            eng.reg_mov(nw, 0)
            n_in, n_out = [0], [0]

            def load(dst_, src_, **kw):
                eng.dma_start(dst_, src_, **kw).then_inc(sp_in, 16)
                n_in[0] += 1

            def store(dst_, src_):
                eng.dma_start(dst_, src_).then_inc(sp_out, 16)
                n_out[0] += 1

            load(pairs_i, dst.rearrange("(p n) -> p n", p=SB))
            load(dsti, dst_t)
            load(w_sb[:, :, :], W_heads.rearrange("h k j -> k h j"))
            load(a_bc[:, :, :], a_heads.rearrange("(o h) j -> o h j", o=1).to_broadcast([128, H, 2 * DH]))
            load(woa[:, :, 0:D], W_out.rearrange("(c p) n -> p c n", p=128))
            load(ao_bc[:, :, :], a_out.rearrange("(o r j) -> o r j", o=1, r=2).to_broadcast([128, 2, D]))
            load(gh[:, :], gamma_h.rearrange("(c a) j -> (a j) c", a=2), allow_slow_non_contiguous=True)
            load(bh[:, :], beta_h.rearrange("(c a) j -> (a j) c", a=2), allow_slow_non_contiguous=True)
            load(go[:, :], gamma_o.rearrange("(p o) -> p o", o=1))
            load(bo[:, :], beta_o.rearrange("(p o) -> p o", o=1))
            load(bres[:, :], b_res.rearrange("(o n) -> o n", o=1))
            eng.wait_ge(tables, 1)
            store(base_d.rearrange("v (p q) -> p v q", p=SB), tb_bi[:, :, :])
            store(baser_d.rearrange("v (p q) -> p v q", p=SB), tb_ri[:, :, :])
            store(span_d.rearrange("v (p q) -> p v q", p=SB), tb_si[:, :, :])
            eng.wait_ge(sp_out, 16 * n_out[0])
            load(basei, base_d.rearrange("(o v) q -> o (v q)", o=1).to_broadcast([EP, NV * NPAIR]))
            load(baser[:, :], baser_d.rearrange("(o v) q -> o (v q)", o=1))
            load(spanr[:, :], span_d.rearrange("(o v) q -> o (v q)", o=1))
            eng.wait_ge(sp_in, 16 * n_in[0])
            phase_end(eng, 1)
            sp_node(eng, n_x, x)
            eng.wait_ge(win_ready, 1)
            store(win0_d[0:N, :].rearrange("(t p) c -> p t c", p=NP_), nwin[:, :, :])
            store(win0_d[N:NW, :], nwin[0:WIN, 0, :])
            eng.wait_ge(n_x["asb"], NT + 2)
            store(dsc0_d, den[:, 0:N])
            eng.wait_ge(sp_out, 16 * n_out[0])
            phase_end(eng, 2)
            sp_pass(eng, G0, nb, ni, nw, nxt, bases)
            eng.wait_ge(den_out, 16 * NS)
            phase_end(eng, 3)
            S = n_bn
            with by_two(eng, NC) as c:
                for u in range(2):
                    eng.dma_start(y1[:, u, :, :], chunk(y1_d, (c + u) * CH)).then_inc(S[f"in{u}"], 16)
                    eng.dma_start(d8[:, u, :], den0_d[:, ds((c + u) * CH, CH)]).then_inc(S[f"in{u}"], 16)
                    eng.dma_start(q8[:, u, :], dsc0_d[:, ds((c + u) * CH, CH)]).then_inc(S[f"in{u}"], 16)
                for u in range(2):
                    eng.wait_ge(S["row"], c + (u + 1))
                    eng.dma_start(chunk(y1_d, (c + u) * CH), y1[:, u, :, :]).then_inc(S[f"out{u}"], 16)
                for u in range(2):
                    eng.wait_ge(S["stat"], c + (u + 1))
                    eng.wait_ge(S[f"out{u}"], c * 8 + 16)
                    eng.sem_inc(alone, 1)
            phase_end(eng, 4)
            S = n_msg
            with by_two(eng, NC) as c:
                for u in range(2):
                    eng.wait_ge(S["used"], c + (u + 1))
                    eng.dma_start(y1[:, u, :, :], chunk(y1_d, (c + u) * CH)).then_inc(S[f"in{u}"], 16)
            eng.wait_ge(win_ready, 2)
            store(win1_d[0:N, :].rearrange("(t p) c -> p t c", p=NP_), nwin[:, :, 0:3])
            store(win1_d[N:NW, :], nwin[0:WIN, 0, 0:3])
            store(dsc1_d, den[0:1, 0:N])
            eng.wait_ge(sp_out, 16 * n_out[0])
            phase_end(eng, 5)
            sp_pass(eng, G1, nb, ni, nw, nxt, bases)
            phase_end(eng, 6)
            load(w_a[:, :], W_res)
            S = n_gn
            with by_two(eng, NC) as c:
                for u in range(2):
                    eng.wait_ge(S["row"], c + (u + 1))
                    eng.dma_start(q8[0:1, u, :], dsc1_d[:, ds((c + u) * CH, CH)]).then_inc(S[f"in{u}"], 16)
            eng.wait_ge(sp_in, 16 * n_in[0])
            phase_end(eng, 7)
            sp_node(eng, n_fin[0], x)
            phase_end(eng, 8)
            sp_pass(eng, S0, nb, ni, nw, nxt, bases)
            phase_end(eng, 9)

            def sage_weights(Wl, Wr, vectors):
                load(w_a[:, :], Wl)
                load(w_b[:, :], Wr)
                for i, vec in enumerate(vectors):
                    load(vrow[:, i, :], vec.rearrange("(o n) -> o n", o=1).to_broadcast([128, D]))
                eng.wait_ge(sp_in, 16 * n_in[0])
            sage_weights(Wl0, Wr0, (b0, g0, be0, rm0, rv0))
            phase_end(eng, 10)
            sp_node(eng, n_fin[1], t_sage0)
            phase_end(eng, 11)
            sp_pass(eng, S1, nb, ni, nw, nxt, bases)
            phase_end(eng, 12)
            sage_weights(Wl1, Wr1, (b1, g1, be1, rm1, rv1))
            phase_end(eng, 13)
            sp_node(eng, n_fin[2], t_sage0, t_sage1)
            phase_end(eng, 14)

        LOADS_1 = 16 * 11
        LOADS_T = 16 * 14
        LOADS_10 = LOADS_T + 16 + 16 * 7
        LOADS_13 = LOADS_10 + 16 * 7

        def act_pass(eng, spec, nw):
            h = spec["heads"]

            def body(s0, v, b):
                for half in range(2):
                    span = load_span(eng, v, b, half)
                    with eng.Fori(0, span, WIN):
                        w = count(eng, nw, MAX_WINDOWS)
                        eng.wait_ge(oht_ps, w)
                        eng.activation(oht[:, :].rearrange("p (a n) -> p a n", a=2), p_oht[0:WIN, :, 0:4 * EP],
                                       ACT.Copy).then_inc(oht_sb, 1)
                        eng.wait_ge(exp_arg, w)
                        eng.activation(wgt[:, :, 0:h], s_d[:, :, 0:h], ACT.Exp).then_inc(wgt_ready, 1)

            def after(s):
                for i in range(NCHUNK):
                    u = i % 2
                    eng.wait_ge(fl_ps, s * NCHUNK + (i + 1))
                    eng.wait_ge(fl_free, s * NCHUNK + (i + 1))
                    eng.activation(stg[:, u, :], p_big[:, u, 0:FC], ACT.Copy).then_inc(fl_sb, 1)
            node_ranges(eng, spec, body, after)

        def act_bound(eng, S, h, loads):
            eng.wait_ge(m_ready, 1 if h == H else 2)
            with by_two(eng, NC) as c:
                for u in range(2):
                    eng.wait_ge(S[f"in{u}"], c * (8 * loads) + 16 * loads)
                    eng.activation(e8[0:h, u, :], q8[0:h, u, :], ACT.Identity, bias=a8[0:h, 0:1]).then_inc(S["add"], 1)
                for u in range(2):
                    eng.wait_ge(S["bound"], c + (u + 1))
                    eng.activation(e8[0:h, u, :], r8[0:h, u, :], ACT.Exp, bias=m8[0:h, 0:1], scale=-1.0).then_inc(S["expd"], 1)

        def act_node(eng, S, affine, norm):
            with by_two(eng, NT) as t:
                for u in range(2):
                    eng.wait_ge(S["mps"], t + (u + 1))
                    cols = acc[:, ds((t + u) * NP_, NP_)]
                    if affine:
                        ins = eng.activation(aT[:, u, :], cols, ACT.Identity, bias=shf[:, 0:1], scale=scl[:, 0:1])
                    else:
                        ins = eng.activation(aT[:, u, :], cols, ACT.Copy)
                    ins.then_inc(S["acp"], 1)
                    eng.wait_ge(S["xps"], t + (u + 1))
                    eng.activation(xT[:, u, :], bank[u][:, 0:NP_], ACT.Copy).then_inc(S["xsb"], 1)
                for u in range(2 if norm else 0):
                    eng.wait_ge(S["var"], t + (u + 1))
                    eng.activation(lnr[:, u:u + 1], lnr[:, u:u + 1], ACT.Sqrt).then_inc(S["std"], 1)

        def act_sqrt(eng, ap, k):
            eng.wait_ge(sqrt_arg, k)
            eng.activation(ap, ap, ACT.Sqrt).then_inc(sqrt_done, 1)

        @block.scalar
        def _(eng):
            nw = eng.alloc_register("nw_act")
            eng.reg_mov(nw, 0)
            phase_end(eng, 1)
            S = n_x
            with by_two(eng, NT) as t:
                for u in range(2):
                    eng.wait_ge(S["mps"], t + (u + 1))
                    eng.wait_ge(S["xps"], t + (u + 1))
                    eng.activation(xT[:, u, :], bank[u][:, 0:NP_], ACT.Copy).then_inc(S["xsb"], 1)
                for u in range(2):
                    eng.wait_ge(S["mps"], t + (u + 3))
                    eng.activation(den[:, ds((t + u) * NP_, NP_)], p_oht[0:H, u, 0:NP_], ACT.Copy).then_inc(S["asb"], 1)
            phase_end(eng, 2)
            act_pass(eng, G0, nw)
            phase_end(eng, 3)
            act_bound(eng, n_bn, H, 3)
            act_sqrt(eng, scl[:, :], 1)
            phase_end(eng, 4)
            S = n_msg
            with eng.Fori(0, NC) as c:
                for i in range(2):
                    eng.wait_ge(S["mps"], c * 2 + (i + 1))
                    eng.wait_ge(S["stored"], c * 2 + (i + 1))
                    eng.activation(rowb[:, i, 0:D + 2], p_big[0:NP_, i, 0:D + 2], ACT.Copy).then_inc(S["row"], 1)
            phase_end(eng, 5)
            act_pass(eng, G1, nw)
            phase_end(eng, 6)
            act_bound(eng, n_gn, 1, 1)
            act_sqrt(eng, scl[:, 0:1], 2)
            phase_end(eng, 7)
            act_node(eng, n_fin[0], True, True)
            phase_end(eng, 8)
            phase_end(eng, 9)
            act_sqrt(eng, vrow[:, 4, :], 3)
            phase_end(eng, 10)
            act_node(eng, n_fin[1], False, False)
            phase_end(eng, 11)
            phase_end(eng, 12)
            act_sqrt(eng, vrow[:, 4, :], 4)
            phase_end(eng, 13)
            act_node(eng, n_fin[2], False, True)
            phase_end(eng, 14)

        def pe_pass(eng, spec, nb, nw):
            h = spec["heads"]

            def body(s0, v, b):
                c = count(eng, nb, MAX_BLOCKS)
                for half in range(2):
                    span = load_span(eng, v, b, half)
                    with eng.Fori(0, span, WIN):
                        w = count(eng, nw, MAX_WINDOWS)
                        if not spec["weighted"]:
                            eng.wait_ge(rows_in[half], c * (16 * TH))
                        eng.wait_ge(oh_ready, w)
                        if spec["weighted"]:
                            for j in range(TH):
                                last = eng.transpose(p_oht[0:WIN, j // 4, (j % 4) * EP:(j % 4 + 1) * EP], oh[:, j, :],
                                                     ident[0:EP, 0:EP])
                            last.then_inc(oht_ps, 1)
                            eng.wait_ge(adw_in, w * (16 * PAIRS))
                            eng.wait_ge(oht_sb, w)
                            k = 2 * h + 1
                            for j in range(TH):
                                last = eng.matmul(p_adx[0:EP, j * k:(j + 1) * k], oht[:, j * EP:(j + 1) * EP],
                                                  adw[:, j // 2, 0:k], start=True, stop=True)
                            last.then_inc(adx_ready, 1)
                            eng.wait_ge(rows_in[half], c * (16 * TH))
                            eng.wait_ge(wgt_ready, w)
                        for j in range(TH if spec["count"] else 0):
                            left = wgt[:, j, 0:h] if spec["weighted"] else ones[0:EP, 0:1]
                            eng.matmul(p_den[0:h, (j // 2) * WIN:(j // 2 + 1) * WIN], left, oh[:, j, :],
                                       start=(j % 2 == 0), stop=(j % 2 == 1))
                        for q in range(PAIRS):
                            if spec["weighted"]:
                                eng.wait_ge(rhs_ready, w * PAIRS + (q + 1))
                            for j in (2 * q, 2 * q + 1):
                                right = rhs[:, j, 0:h * WIN] if spec["weighted"] else oh[:, j, :]
                                last = eng.matmul(sums(q, h), rows[:, half * TH + j, 0:D], right,
                                                  start=(j == 2 * q), stop=(j == 2 * q + 1))
                            last.then_inc(sums_ps, 1)
                    eng.drain().then_inc(rows_used[half], 1)

            def after(s):
                eng.wait_ge(rng_done, s + 1)
                for i in range(NCHUNK):
                    p, ck, u = i % HP, i // HP, i % 2
                    eng.wait_ge(fl_sb, s * NCHUNK + (i + 1))
                    for r in range(2):
                        last = eng.matmul(p_big[:, u, 0:FC], wz[:, 2 * p + r, :],
                                          acc8[:, 2 * p + r, ck * FC:(ck + 1) * FC], start=(r == 0), stop=(r == 1))
                    last.then_inc(fl_ps, 1)
                eng.wait_ge(fl_sb, (s + 1) * NCHUNK + 2)
            node_ranges(eng, spec, body, after)

        def pe_max(eng, h, k, spread):
            eng.wait_ge(mx_part, k)
            eng.transpose(p_den[0:h, 0:EP], col1[0:EP, 0:h], ident[0:EP, 0:EP]).then_inc(mx_t, 1)
            if spread:
                eng.wait_ge(mx_diag, spread)
                eng.matmul(p_adx[:, 0:h], ones[0:h, 0:128], t8[0:h, 0:h], start=True, stop=True).then_inc(mx_bc, 1)

        def pe_node(eng, S, tile, loads, left_w, right_w, bias):
            with by_two(eng, NT) as t:
                for u in range(2):
                    eng.wait_ge(S[f"in{u}"], t * (8 * loads) + 16 * loads)
                    eng.wait_ge(S["xsb"], t + (u + 1))
                    eng.transpose(bank[u][:, 0:NP_], tile[:, u, :], ident[0:NP_, 0:NP_]).then_inc(S["xps"], 1)
                for u in range(2):
                    eng.wait_ge(S["msb"], t + (u + 1))
                    eng.wait_ge(S["acp"], t + (u + 1))
                    eng.wait_ge(S["xsb"], t + (u + 3))
                    o = p_big[0:NP_, u, 0:D]
                    eng.matmul(o, aT[:, u, :], left_w, start=True, stop=False)
                    eng.matmul(o, xT[:, u, :], right_w, start=False, stop=False)
                    eng.matmul(o, ones[0:1, 0:NP_], bias, start=False, stop=True).then_inc(S["mps"], 1)

        @block.tensor
        def _(eng):
            nb = eng.alloc_register("nb_pe")
            nw = eng.alloc_register("nw_pe")
            eng.reg_mov(nb, 0)
            eng.reg_mov(nw, 0)
            eng.wait_ge(cst, 7)
            eng.wait_ge(cand_ready, 1)
            eng.transpose(p_den[0:2 * NS, 0:SB], cand[:, :], ident[0:SB, 0:SB]).then_inc(cand_t, 1)
            eng.wait_ge(lh_col, 1)
            eng.matmul(p_adx[0:1, 0:2 * NS], c10[:, 0:1], ident[0:2 * NS, 0:2 * NS], start=True, stop=True).then_inc(lh_row, 1)
            phase_end(eng, 1)
            S = n_x
            with by_two(eng, NT) as t:
                for u in range(2):
                    eng.wait_ge(S[f"in{u}"], t * 8 + 16)
                    eng.wait_ge(S["xsb"], t + (u + 1))
                    eng.transpose(bank[u][:, 0:NP_], xt[:, u, :], ident[0:NP_, 0:NP_]).then_inc(S["xps"], 1)
                for u in range(2):
                    eng.wait_ge(S["msb"], t + (u + 1))
                    eng.wait_ge(S["asb"], t + (u + 1))
                    eng.wait_ge(S["xsb"], t + (u + 3))
                    eng.matmul(p_big[0:NP_, u, 0:2 * H], xT[:, u, :], wa[:, :], start=True, stop=True)
                    eng.matmul(p_oht[0:H, u, 0:NP_], wa[:, H:2 * H], xT[:, u, :],
                               start=True, stop=True).then_inc(S["mps"], 1)
            pe_max(eng, H, 1, 1)
            phase_end(eng, 2)
            pe_pass(eng, G0, nb, nw)
            phase_end(eng, 3)
            pe_max(eng, H, 2, 0)
            S = n_bn
            with by_two(eng, NC) as c:
                for u in range(2):
                    eng.wait_ge(S["rec"], c + (u + 1))
                    for p in range(HP):
                        o = (p_big, p_oht)[u][:, p // 2, (p % 2) * CH:(p % 2 + 1) * CH]
                        last = eng.matmul(o, sel[:, p, :], r8[:, u, :], start=True, stop=True)
                    last.then_inc(S["bc"], 1)
            eng.wait_ge(bn_ready, 1)
            for p in range(HP):
                last = eng.matmul(p_den[0:1, 0:D + 2], shf[:, p:p + 1], woa[:, p, :], start=(p == 0), stop=(p == HP - 1))
            last.then_inc(bias_ps, 1)
            phase_end(eng, 4)
            S = n_msg
            with by_two(eng, NC) as c:
                for u in range(2):
                    eng.wait_ge(S[f"in{u}"], c * 8 + 16)
                    for i in range(2):
                        eng.wait_ge(S["row"], c * 2 + (2 * u + i + 1))
                        eng.wait_ge(S["msb"], c * 2 + (2 * u + i + 1))
                        o = p_big[0:NP_, i, 0:D + 2]
                        for p in range(HP):
                            eng.matmul(o, y1[:, u, p, i * NP_:(i + 1) * NP_], wob[:, p, :], start=(p == 0), stop=False)
                        eng.matmul(o, ones[0:1, 0:NP_], brow[:, :], start=False, stop=True).then_inc(S["mps"], 1)
                    eng.wait_ge(S["dsb"], c + (u + 1))
                    o = bank[u][0:1, 0:CH]
                    for p in range(HP):
                        eng.matmul(o, wob[:, p, D + 1:D + 2], y1[:, u, p, :], start=(p == 0), stop=False)
                    eng.matmul(o, brow[:, D + 1:D + 2], ones[0:1, 0:CH], start=False, stop=True).then_inc(S["used"], 1)
            pe_max(eng, 1, 3, 2)
            phase_end(eng, 5)
            pe_pass(eng, G1, nb, nw)
            phase_end(eng, 6)
            pe_max(eng, 1, 4, 0)

            def spread_row(S):
                with by_two(eng, NC) as c:
                    for u in range(2):
                        eng.wait_ge(S["rec"], c + (u + 1))
                        eng.matmul(p_big[:, u, 0:CH], ones[0:1, 0:128], r8[0:1, u, :], start=True, stop=True).then_inc(S["bc"], 1)
            spread_row(n_gn)
            phase_end(eng, 7)
            pe_node(eng, n_fin[0], xt, 1, ident[:, :], w_a[:, :], bres[:, :])
            phase_end(eng, 8)
            pe_pass(eng, S0, nb, nw)
            phase_end(eng, 9)
            spread_row(n_c[0])
            phase_end(eng, 10)
            pe_node(eng, n_fin[1], xt, 1, w_a[:, :], w_b[:, :], brow[:, 0:D])
            phase_end(eng, 11)
            pe_pass(eng, S1, nb, nw)
            phase_end(eng, 12)
            spread_row(n_c[1])
            phase_end(eng, 13)
            pe_node(eng, n_fin[2], ht, 2, w_a[:, :], w_b[:, :], brow[:, 0:D])
            phase_end(eng, 14)

        class DynLinks:

            def __init__(self, eng, sem_, reg):
                self.eng, self.sem, self.reg, self.k = eng, sem_, reg, 0
                self.base = eng.snap(reg, min_val=0, max_val=16 * MAX_WINDOWS)

            def __call__(self, ins):
                self.k += 1
                ins.then_inc(self.sem, 1)
                self.eng.wait_ge(self.sem, self.base + self.k)

            def end(self):
                self.eng.reg_add(self.reg, self.reg, self.k)

        def dve_pass(eng, spec, nb, nw, nl, bases):
            h, acc_v, weighted = spec["heads"], acc_view(spec), spec["weighted"]
            basef_v = basef[:, :, :].rearrange("p v q -> p (v q)")

            def pairs(ap):
                return ap.rearrange("p (q i) -> p q i", i=2)

            def body(s0, v, b):
                c = count(eng, nb, MAX_BLOCKS)
                for half in range(2):
                    span = load_span(eng, v, b, half)
                    eng.load(bases, baser[0:1, ds(v * NPAIR + b * (2 * PAIRS) + half * PAIRS, PAIRS)])
                    link = DynLinks(eng, dve_w, nl)
                    link(eng.tensor_scalar(cur[:, :], basef_v[:, ds(v * NPAIR + b * (2 * PAIRS) + half * PAIRS, PAIRS)],
                                           1.0, None, ALU.mult))
                    link.end()
                    with eng.Fori(0, span, WIN):
                        w = count(eng, nw, MAX_WINDOWS)
                        link = DynLinks(eng, dve_w, nl)
                        link(eng.tensor_tensor(pairs(rel[:, :]), pairs(dstf[:, ds(b * (2 * TH) + half * TH, TH)]),
                                               cur[:, :].unsqueeze(2).to_broadcast([EP, PAIRS, 2]), ALU.subtract))
                        eng.tensor_tensor(oh[:, :, :], iota_w[:, :].unsqueeze(1).to_broadcast([EP, TH, WIN]),
                                          rel[:, :].unsqueeze(2).to_broadcast([EP, TH, WIN]),
                                          ALU.is_equal).then_inc(oh_ready, 1)
                        eng.tensor_scalar(cur[:, :], cur[:, :], float(WIN), s1col[:, 0:1], ALU.add,
                                          ALU.min).then_inc(dve_w, 1)
                        link.k += 1
                        if weighted:
                            eng.wait_ge(rows_in[half], c * (16 * TH))
                            eng.wait_ge(adx_ready, w + 1)
                            adx = p_adx[0:EP, 0:TH * (2 * h + 1)].rearrange("p (t k) -> p t k", t=TH)
                            t_, l_, m_, d_ = (a[:, :, 0:h] for a in (s_t, s_l, s_m, s_d))
                            eng.tensor_scalar(pen[:, :], adx[:, :, 2 * h], -1.0, BIG, ALU.add, ALU.mult)
                            link(eng.tensor_tensor(t_, rows[:, half * TH:half * TH + TH, D:D + h], adx[:, :, 0:h], ALU.add))
                            link(eng.scalar_tensor_tensor(l_, t_, SLOPE, t_, ALU.mult, ALU.max))
                            link(eng.tensor_tensor(m_, l_, pen[:, :].unsqueeze(2).to_broadcast([EP, TH, h]), ALU.add))
                            eng.tensor_tensor(d_, m_, adx[:, :, h:2 * h], ALU.subtract).then_inc(exp_arg, 1)
                            link(eng.tensor_tensor(smax[:, :, 0:h], smax[:, :, 0:h], m_, ALU.max))
                            eng.wait_ge(wgt_ready, w)
                            for q in range(PAIRS):
                                two = slice(2 * q, 2 * q + 2)
                                eng.tensor_tensor(rhs[:, two, 0:h * WIN].rearrange("p t (h j) -> p t h j", h=h),
                                                  oh[:, two, :].unsqueeze(2).to_broadcast([EP, 2, h, WIN]),
                                                  wgt[:, two, 0:h].unsqueeze(3).to_broadcast([EP, 2, h, WIN]),
                                                  ALU.mult).then_inc(rhs_ready, 1)
                        for q in range(PAIRS):
                            eng.wait_ge(sums_ps, w * PAIRS + (q + 1))
                            at = eng.snap(bases[q], min_val=0, max_val=spec["cols"])
                            a = acc_v[:, :, ds(at, WIN)]
                            if spec["count"]:
                                dn = den[0:h, ds(at, WIN)]
                                eng.tensor_tensor(dn, dn, p_den[0:h, q * WIN:(q + 1) * WIN], ALU.add).then_inc(dve_w, 1)
                                link.k += 1
                            link(eng.tensor_tensor(a, a, sums(q, h).rearrange("p (h j) -> p h j", h=h), ALU.add))
                            eng.reg_add(bases[q], bases[q], WIN)
                            eng.reg_alu(bases[q], bases[q], spec["cols"], ALU.min)
                        link.end()

            def after(s):
                link = Links(eng, dve_r, s * (NCHUNK + 2))
                link(eng.tensor_scalar(s1col[:, :], s1col[:, :], float(SN), None, ALU.add))
                eng.sem_inc(rng_done, 1)
                for i in range(NCHUNK):
                    p, ck = i % HP, i // HP
                    eng.wait_ge(fl_ps, s * NCHUNK + (i + 1))
                    end = SW if ck == NFC - 1 else (ck + 1) * FC
                    link(eng.memset(acc8[:, 2 * p:2 * p + 2, ck * FC:end], 0.0))
                eng.wait_ge(den_out, s * 16 + 16)
                link(eng.memset(den[:, 0:SW], 0.0))
            node_ranges(eng, spec, body, after)

        @block.vector
        def _(eng):
            nb = eng.alloc_register("nb_dve")
            nw = eng.alloc_register("nw_dve")
            nl = eng.alloc_register("nl_dve")
            bases = [eng.alloc_register(f"base_dve{q}") for q in range(PAIRS)]
            for r in (nb, nw, nl):
                eng.reg_mov(r, 0)
            link = Links(eng, dve_l)
            ts, tt = eng.tensor_scalar, eng.tensor_tensor

            def dve_max(h, src, k, spread):
                eng.tensor_reduce(col1[0:EP, 0:h], src.rearrange("p m h -> p h m"), axis=AX, op=ALU.max).then_inc(mx_part, 1)
                eng.wait_ge(mx_t, k)
                top = a8 if spread else m8
                link(eng.tensor_reduce(top[0:h, :], p_den[0:h, 0:EP], axis=AX, op=ALU.max))
                if spread:
                    ts(t8[0:h, 0:h], ident[0:h, 0:h], a8[0:h, 0:1], None, ALU.mult).then_inc(mx_diag, 1)
                    eng.wait_ge(mx_bc, spread)
                    link(eng.tensor_copy(amax[:, 0:h], p_adx[:, 0:h]))

            def window_rows(h):
                sc = nsc[:, :, h:2 * h]
                link(tt(nlr[:, :, 0:h], sc, amax[0:NP_, 0:h].unsqueeze(1).to_broadcast([NP_, NT, h]), ALU.add))
                link(eng.scalar_tensor_tensor(nwin[:, :, h:2 * h], nlr[:, :, 0:h], SLOPE, nlr[:, :, 0:h], ALU.mult, ALU.max))
                link(eng.tensor_copy(nwin[:, :, 0:h], sc))
                link(eng.memset(nwin[:, :, 2 * h:2 * h + 1], 1.0))
                eng.sem_inc(win_ready, 1)

            def clear_sums(cols_den):
                link(eng.memset(acc[:, :], 0.0))
                if cols_den:
                    link(eng.memset(den[:, :], 0.0))

            eng.wait_ge(cst, 7)
            eng.wait_ge(sp_in, LOADS_1)
            link(eng.tensor_copy(dstf[:, :], dsti))
            link(eng.tensor_copy(pairs_f, pairs_i))
            by_pair = pairs_f.rearrange("p (q n) -> p q n", n=2 * EP)
            link(eng.tensor_reduce(gmin[:, :], by_pair, axis=AX, op=ALU.min))
            link(eng.tensor_reduce(gmax[:, :], by_pair, axis=AX, op=ALU.max))
            for v in range(NV):
                s0, s1 = (0, N) if v == WHOLE else (v * SN, (v + 1) * SN)
                link(ts(tb_b[:, v, :], gmin[:, :], float(s0), float(s1), ALU.max, ALU.min))
                link(ts(tb_r[:, v, :], tb_b[:, v, :], float(-s0), None, ALU.add))
                link(ts(tb_e[:, v, :], gmax[:, :], float(s1 - 1), None, ALU.min))
                link(tt(tb_e[:, v, :], tb_e[:, v, :], tb_b[:, v, :], ALU.subtract))
                link(eng.tensor_reduce(tb_s[:, v, :], tb_e[:, v, :].rearrange("p (a q) -> p a q", a=2), axis=AX, op=ALU.max))
                link(ts(tb_s[:, v, :], tb_s[:, v, :], 1.0, 1.0, ALU.add, ALU.max))
            link(eng.tensor_copy(tb_bi[:, :, :], tb_b[:, :, :]))
            link(eng.tensor_copy(tb_ri[:, :, :], tb_r[:, :, :]))
            link(eng.tensor_copy(tb_si[:, :, :], tb_s[:, :, :]))
            eng.sem_inc(tables, 1)
            link(eng.tensor_reduce(bmn[:, 0:1], gmin[:, :], axis=AX, op=ALU.min))
            link(eng.tensor_reduce(bmn[:, 1:2], gmax[:, :], axis=AX, op=ALU.max))
            for s in range(NS):
                link(ts(tch[:, 0:1], bmn[:, 1:2], float(s * SN), None, ALU.is_ge))
                link(ts(tch[:, 1:2], bmn[:, 0:1], float((s + 1) * SN), None, ALU.is_lt))
                link(tt(tch[:, 2:3], tch[:, 0:1], tch[:, 1:2], ALU.mult))
                for i in range(2):
                    link(tt(cand[:, i * NS + s:i * NS + s + 1], tch[:, 2:3], pidx[:, i:i + 1], ALU.mult))
            eng.sem_inc(cand_ready, 1)
            eng.wait_ge(cand_t, 1)
            eng.tensor_reduce(c10[:, :], p_den[0:2 * NS, 0:SB], axis=AX, op=ALU.max).then_inc(lh_col, 1)
            eng.wait_ge(lh_row, 1)
            link(eng.tensor_copy(lh[:, :], p_adx[0:1, 0:2 * NS]))
            link(ts(lh[:, NS:], lh[:, NS:], -1.0, float(SB), ALU.mult, ALU.add))
            link(ts(lh[:, NS:], lh[:, NS:], float(SB - 1), None, ALU.min))
            link(eng.scalar_tensor_tensor(lh[:, 0:NS], lh[:, NS:], 1.0, lh[:, 0:NS], ALU.add, ALU.max))
            link(eng.tensor_copy(lohi[:, :], lh[:, :]))
            link(eng.memset(wz[:, :, :], 0.0))
            for r in range(2):
                link(eng.tensor_copy(wz[:, :, :].rearrange("p (c a) n -> p c a n", a=2)[:, :, r, r * DH:(r + 1) * DH],
                                     w_sb[:, :, :].rearrange("p (c a) n -> p c a n", a=2)[:, :, r, :]))
                pv = prod.rearrange("p (h j) -> p h j", h=H)
                link(tt(pv, w_sb[:, :, :], a_bc[:, :, r * DH:(r + 1) * DH], ALU.mult))
                link(eng.tensor_reduce(wa[:, r * H:(r + 1) * H], pv, axis=AX, op=ALU.add))
            for r in range(2):
                pv = prod.rearrange("p (c j) -> p c j", c=HP)
                link(tt(pv, woa[:, :, 0:D], ao_bc[:, r, :].unsqueeze(1).to_broadcast([128, HP, D]), ALU.mult))
                link(eng.tensor_reduce(woa[:, :, D + r], pv, axis=AX, op=ALU.add))
            link(eng.memset(smax[:, :, :], -BIG))
            link(eng.memset(s1col[:, :], float(SN)))
            eng.wait_ge(sp_in, LOADS_T)
            link(eng.tensor_copy(basef[:, :, :].rearrange("p v q -> p (v q)"), basei))
            phase_end(eng, 1)
            S = n_x
            with by_two(eng, NT) as t:
                for u in range(2):
                    eng.wait_ge(S[f"in{u}"], t * 8 + 16)
                    eng.tensor_copy(rowb[:, u, 0:D], xt[:, u, :])
                    eng.wait_ge(S["mps"], t + (u + 3))
                    eng.tensor_copy(rowb[:, u, D:D + H], p_big[0:NP_, u, 0:H]).then_inc(S["row"], 1)
                    eng.tensor_copy(nsc[:, ds(t + u, 1), :].rearrange("p o k -> p (o k)"),
                                    p_big[0:NP_, u, 0:2 * H]).then_inc(S["msb"], 1)
            eng.wait_ge(S["msb"], NT + 2)
            dve_max(H, nsc[:, :, 0:H], 1, 1)
            window_rows(H)
            phase_end(eng, 2)
            clear_sums(True)
            dve_pass(eng, G0, nb, nw, nl, bases)
            phase_end(eng, 3)
            dve_max(H, smax[:, :, :], 2, 0)
            eng.sem_inc(m_ready, 1)

            def reciprocals(S, h, c, dens):
                for u in range(2):
                    eng.wait_ge(S["add"], c + (u + 1))
                    e = e8[0:h, u, :]
                    eng.scalar_tensor_tensor(r8[0:h, u, :], e, SLOPE, e, ALU.mult, ALU.max).then_inc(S["bound"], 1)
                for u in range(2):
                    own = Links(eng, S["own"], (c + u) * 3)
                    eng.wait_ge(S["expd"], c + (u + 1))
                    own(eng.scalar_tensor_tensor(d8[0:h, u, :], e8[0:h, u, :], DEN_EPS, dens(u), ALU.mult, ALU.add))
                    own(ts(d8[0:h, u, :], d8[0:h, u, :], TINY, None, ALU.max))
                    own(eng.reciprocal(r8[0:h, u, :], d8[0:h, u, :]))
                    eng.sem_inc(S["rec"], 1)

            S = n_bn
            with by_two(eng, NC) as c:
                reciprocals(S, H, c, lambda u: d8[:, u, :])
                for u in range(2):
                    eng.wait_ge(S["bc"], c + (u + 1))
                    yv = y1[:, u, :, :].rearrange("p (a b) n -> p a (b n)", a=2)
                    tt(yv, yv, (p_big, p_oht)[u][:, :, 0:2 * CH], ALU.mult).then_inc(S["row"], 1)
                    eng.wait_ge(S["row"], c + (u + 1))
                    for p in range(HP):
                        last = eng.bn_stats(stats[:, p, ds(c + u, 1), :].rearrange("p o k -> p (o k)"), y1[:, u, p, :])
                    last.then_inc(S["stat"], 1)
            eng.drain().then_inc(dve_l, 1)
            link.k += 1
            eng.wait_ge(dve_l, link.k)

            def inverse_sqrt(out_, var, eps, k):
                link(ts(out_, var, eps, None, ALU.add))
                eng.sem_inc(sqrt_arg, 1)
                eng.wait_ge(sqrt_done, k)
                link(eng.reciprocal(out_, out_))

            def batch_norm(n, gamma, beta, k):
                for p in range(n):
                    link(eng.bn_aggr(mv[:, p, :], stats[:, p, :, :].rearrange("p c k -> p (c k)")))
                inverse_sqrt(scl[:, 0:n], mv[:, 0:n, 1], BN_EPS, k)
                link(tt(scl[:, 0:n], scl[:, 0:n], gamma, ALU.mult))
                link(tt(shf[:, 0:n], mv[:, 0:n, 0], scl[:, 0:n], ALU.mult))
                link(tt(shf[:, 0:n], beta, shf[:, 0:n], ALU.subtract))
            batch_norm(HP, gh[:, :], bh[:, :], 1)
            for p in range(HP):
                link(ts(wob[:, p, :], woa[:, p, :], scl[:, p:p + 1], None, ALU.mult))
            eng.sem_inc(bn_ready, 1)
            eng.wait_ge(bias_ps, 1)
            link(eng.tensor_copy(brow[:, :], p_den[0:1, 0:D + 2]))
            phase_end(eng, 4)
            S = n_msg
            with by_two(eng, NC) as c:
                for u in range(2):
                    for i in range(2):
                        eng.wait_ge(S["row"], c * 2 + (2 * u + i + 3))
                        ts(nsc[:, ds(c * 2 + (2 * u + i), 1), 0:2].rearrange("p o k -> p (o k)"),
                           rowb[:, i, D:D + 2], 1.0, None, ALU.mult).then_inc(S["msb"], 1)
                    eng.wait_ge(S["used"], c + (u + 3))
                    ts(den[0:1, ds((c + u) * CH, CH)], bank[u][0:1, 0:CH], 1.0, None, ALU.mult).then_inc(S["dsb"], 1)
            eng.wait_ge(S["msb"], NT + 2)
            dve_max(1, nsc[:, :, 0:1], 3, 2)
            eng.wait_ge(S["dsb"], NC + 2)
            window_rows(1)
            phase_end(eng, 5)
            clear_sums(True)
            link(eng.memset(smax[:, :, :], -BIG))
            link(eng.memset(s1col[:, :], float(N)))
            dve_pass(eng, G1, nb, nw, nl, bases)
            phase_end(eng, 6)
            dve_max(1, smax[:, :, 0:1], 4, 0)
            eng.sem_inc(m_ready, 1)
            S = n_gn
            with by_two(eng, NC) as c:
                reciprocals(S, 1, c, lambda u: den[0:1, ds((c + u) * CH, CH)])
                for u in range(2):
                    eng.wait_ge(S["bc"], c + (u + 1))
                    cols = acc[:, ds((c + u) * CH, CH)]
                    tt(cols, cols, p_big[:, u, 0:CH], ALU.mult).then_inc(S["row"], 1)
                    eng.wait_ge(S["row"], c + (u + 3))
                    eng.bn_stats(stats[:, 0, ds(c + u, 1), :].rearrange("p o k -> p (o k)"), cols)
            eng.drain().then_inc(dve_l, 1)
            link.k += 1
            eng.wait_ge(dve_l, link.k)
            batch_norm(1, go[:, :], bo[:, :], 2)
            phase_end(eng, 7)

            def layer_norm(S, t):
                for u in range(2):
                    own = Links(eng, S["own"], (t + u) * 4 + t * 2)
                    eng.wait_ge(S["mps"], t + (u + 3))
                    eng.wait_ge(S["stored"], t + (u + 1))
                    z = zt[:, u, :]
                    own(tt(z, p_big[0:NP_, u, 0:D], xt[:, u, :], ALU.add))
                    eng.sem_inc(S["msb"], 1)
                    own(eng.bn_stats(lnst[:, u, :], z))
                    eng.sem_inc(alone, 1)
                    own(eng.bn_aggr(lnmv[:, u, :], lnst[:, u, :]))
                    own(ts(lnr[:, u:u + 1], lnmv[:, u, 1:2], LN_EPS, None, ALU.add))
                    eng.sem_inc(S["var"], 1)
                for u in range(2):
                    own = Links(eng, S["own"], (t + u) * 2 + (t + 2) * 4)
                    z = zt[:, u, :]
                    eng.wait_ge(S["std"], t + (u + 1))
                    own(eng.reciprocal(lnr[:, u:u + 1], lnr[:, u:u + 1]))
                    own(ts(z, z, lnmv[:, u, 0:1], lnr[:, u:u + 1], ALU.subtract, ALU.mult))
                    eng.sem_inc(S["row"], 1)
            with by_two(eng, NT) as t:
                layer_norm(n_fin[0], t)
            phase_end(eng, 8)
            clear_sums(True)
            dve_pass(eng, S0, nb, nw, nl, bases)
            phase_end(eng, 9)

            def neighbour_means(S, first):
                with by_two(eng, NC) as c:
                    for u in range(2):
                        own = Links(eng, S["own"], (c + u) * (3 if first else 1))
                        cnt = den[0:1, ds((c + u) * CH, CH)]
                        if first:
                            own(ts(d8[0:1, u, :], cnt, 1.0, None, ALU.max))
                            own(eng.reciprocal(r8[0:1, u, :], d8[0:1, u, :]))
                            own(ts(cnt, r8[0:1, u, :], 1.0, None, ALU.mult))
                        else:
                            own(ts(r8[0:1, u, :], cnt, 1.0, None, ALU.mult))
                        eng.sem_inc(S["rec"], 1)
                    for u in range(2):
                        eng.wait_ge(S["bc"], c + (u + 1))
                        cols = acc[:, ds((c + u) * CH, CH)]
                        tt(cols, cols, p_big[:, u, 0:CH], ALU.mult)

            def fold(loads, k):
                eng.wait_ge(sp_in, loads)
                b_, g_, be_, rm_, rv_ = (vrow[:, i, :] for i in range(5))
                inverse_sqrt(rv_, rv_, BN_EPS, k)
                link(tt(g_, g_, rv_, ALU.mult))
                link(tt(w_a[:, :], w_a[:, :], g_, ALU.mult))
                link(tt(w_b[:, :], w_b[:, :], g_, ALU.mult))
                link(tt(b_, b_, rm_, ALU.subtract))
                link(tt(b_, b_, g_, ALU.mult))
                link(tt(brow[:, 0:D], b_[0:1, :], be_[0:1, :], ALU.add))
            neighbour_means(n_c[0], True)
            fold(LOADS_10, 3)
            phase_end(eng, 10)
            S = n_fin[1]
            with by_two(eng, NT) as t:
                for u in range(2):
                    eng.wait_ge(S["mps"], t + (u + 3))
                    eng.wait_ge(S["stored"], t + (u + 1))
                    ts(zt[:, u, :], p_big[0:NP_, u, 0:D], 0.0, None, ALU.max).then_inc(S["row"], 1)
                    eng.wait_ge(S["row"], t + (u + 1))
                    eng.sem_inc(S["msb"], 1)
            phase_end(eng, 11)
            clear_sums(False)
            dve_pass(eng, S1, nb, nw, nl, bases)
            phase_end(eng, 12)
            neighbour_means(n_c[1], False)
            fold(LOADS_13, 4)
            phase_end(eng, 13)
            with by_two(eng, NT) as t:
                layer_norm(n_fin[2], t)
            phase_end(eng, 14)


def kernel(x, src, dst, **weights):
    import concourse.bacc as bacc
    from concourse.bass_utils import run_bass_kernel_spmd

    def by_tile(a):
        return np.ascontiguousarray(np.asarray(a).reshape(ET, EP).T)

    w = {k.split("gnn_")[0] + k.split("gnn_")[1]: np.asarray(v) for k, v in weights.items()}
    arrays = {
        "x": np.asarray(x), "src_t": by_tile(src), "dst_t": by_tile(dst), "dst": np.asarray(dst),
        "W_heads": w["L0_W_heads"], "a_heads": w["L0_a_heads"], "gamma_h": w["L0_gamma_h"], "beta_h": w["L0_beta_h"],
        "W_out": w["L0_W_out"], "a_out": w["L0_a_out"], "gamma_o": w["L0_gamma_o"], "beta_o": w["L0_beta_o"],
        "W_res": w["L0_W_res"], "b_res": w["L0_b_res"],
    }
    for i in range(2):
        arrays[f"Wl{i}"] = w[f"L1_Wl{i}"].T
        arrays[f"Wr{i}"] = w[f"L1_Wr{i}"].T
        for k in ("b", "g", "be", "rm", "rv"):
            arrays[f"{k}{i}"] = w[f"L1_{k}{i}"]
    nc = bacc.Bacc("TRN2", target_bir_lowering=False, num_devices=1)
    feeds, args = {}, {}
    for name, a in arrays.items():
        a = np.ascontiguousarray(a)
        feeds[f"in_{name}"] = a
        args[name] = nc.dram_tensor(f"in_{name}", a.shape, mybir.dt.from_np(a.dtype), kind="ExternalInput").ap()
    args["out"] = nc.dram_tensor("out_0", (N, D), F32, kind="ExternalOutput").ap()
    gnn_kernel(nc, **args)
    return run_bass_kernel_spmd(nc, [feeds], core_ids=[0]).results[0]["out_0"]
```

```python
from contextlib import ExitStack

import numpy as np
import concourse.bass as bass
from concourse import mybir

F32 = mybir.dt.float32
I32 = mybir.dt.int32
I16 = mybir.dt.int16
BF16 = mybir.dt.bfloat16
ALU = mybir.AluOpType
ACT = mybir.ActivationFunctionType
AX = mybir.AxisListType.X
ds = bass.ds

N = 12500
E = 200000
D = 128
H = 8
DH = 64
NP_ = 125
NT = N // NP_
TC = 4
CH = TC * NP_
NC = N // CH
EP = 125
ET = E // EP
TH = 8
PAIRS = TH // 2
SB = ET // (2 * TH)
NPAIR = ET // 2
WIN = 22
NS = 5
SN = N // NS
NV = NS + 1
WHOLE = NS
SW = SN + WIN
NW = N + WIN
HP = H // 2
NFC = SN // CH
K0 = 2 * H + 1
K1 = 3
ROW0 = D + H
ROW1 = D + 1
SLOPE = 0.2
BN_EPS = 1e-5
LN_EPS = 1e-5
DEN_EPS = 1e-10
TINY = 1.2e-38
BIG = 1e30


class Links:

    def __init__(self, eng, sem, base=0):
        self.eng, self.sem, self.base, self.k = eng, sem, base, 0

    def __call__(self, ins):
        self.k += 1
        ins.then_inc(self.sem, 1)
        self.eng.wait_ge(self.sem, self.base + self.k)


def by_chunk(eng, *stages):
    with eng.Fori(0, NC // 2) as i:
        for stage in stages:
            for u in range(2):
                stage(i * 2, u)
    for stage in stages[:len(stages) * (NC % 2)]:
        stage(NC - 1, 0)


def gnn_kernel(nc, x, src_t, dst_t, dst, W_heads, a_heads, gamma_h, beta_h, W_out, a_out, gamma_o, beta_o,
               W_res, b_res, Wl0, Wr0, b0, g0, be0, rm0, rv0, Wl1, Wr1, b1, g1, be1, rm1, rv1, out):
    ctx = ExitStack()
    with ctx:
        def sb(name, shape, dt=F32):
            return ctx.enter_context(nc.sbuf_tensor(name, shape, dt))

        def psb(name, shape):
            return ctx.enter_context(nc.psum_tensor(name, shape, F32))

        def part(buf, p, at, *dims):
            n = int(np.prod(dims))
            names = "abc"[:len(dims)]
            v = buf[0:p, at:at + n]
            if len(dims) == 1:
                return v
            return v.rearrange(f"p ({' '.join(names)}) -> p {' '.join(names)}", **dict(zip(names, dims)))

        def sem(name):
            return ctx.enter_context(nc.semaphore(name))

        def dram(name, shape, dt=F32):
            return nc.dram_tensor(name, shape, dt).ap()

        t_gat0 = dram("t_gat0", (N, ROW0))
        t_gat1 = dram("t_gat1", (N, ROW1))
        t_sage0 = dram("t_sage0", (N, D))
        t_sage1 = dram("t_sage1", (N, D))
        win0_d = dram("win0_d", (3, NW, K0), BF16)
        win1_d = dram("win1_d", (3, NW, K1), BF16)
        dsc0_d = dram("dsc0_d", (H, N))
        dsc1_d = dram("dsc1_d", (1, N))
        den0_d = dram("den0_d", (H, N))
        y1_d = dram("y1_d", (HP, D, N))
        base_d = dram("base_d", (NV, NPAIR), I32)
        baser_d = dram("baser_d", (NV, NPAIR), I32)

        acc = sb("acc", [128, H * SW])
        den = sb("den", [H, NW])
        acc8 = acc[:, :].rearrange("p (h n) -> p h n", h=H)
        dstf = sb("dstf", [EP, ET], I16)
        dsti = acc[0:EP, 0:ET].bitcast(I32)
        basef = sb("basef", [EP, NV, NPAIR], I16)
        basei = acc[0:EP, 2048:2048 + NV * NPAIR].bitcast(I32)
        baser = sb("baser", [1, NV * NPAIR], I32)
        lohi = sb("lohi", [1, 2 * NS + NV], I32)
        rows_all = sb("rows", [EP, 2 * TH * ROW0])
        rows = rows_all[:, :].rearrange("p (t k) -> p t k", t=2 * TH)
        idx = sb("idx", [EP, 2 * TH], I32)
        adw = sb("adw", [3 * WIN, 2, PAIRS, K0], BF16)
        cur = sb("cur", [EP, PAIRS])
        rel = sb("rel", [EP, TH])
        oh = sb("oh", [EP, 2, TH, WIN])
        ohb = sb("ohb", [EP, 2, TH, 3 * WIN], BF16)
        oht = sb("oht", [3 * WIN, TH, EP], BF16)
        s_t = sb("s_t", [EP, TH, H])
        s_l = sb("s_l", [EP, TH, H])
        s_m = sb("s_m", [EP, TH, H])
        s_d = sb("s_d", [EP, TH, H])
        pen = sb("pen", [EP, TH])
        smax = sb("smax", [EP, TH, H])
        wgt = sb("wgt", [EP, 2, TH, H])
        rhs = sb("rhs", [EP, 2, TH, H * WIN])
        s1col = sb("s1col", [EP, 1])
        roff = sb("roff", [EP, 1])
        ident = sb("ident", [128, 128])
        identb = sb("identb", [128, 128], BF16)
        iota_w = sb("iota_w", [EP, WIN])
        ones = sb("ones", [128, CH])
        zeros = sb("zeros", [128, 128])
        sel = sb("sel", [H, HP, 128])
        w_sb = acc[:, 14400:14400 + H * DH].rearrange("p (h j) -> p h j", h=H)
        wz = sb("wz", [128, H, 128])
        a_bc = acc[:, 16384:16384 + 2 * H * DH].rearrange("p (h j) -> p h j", h=H)
        wa = sb("wa", [128, 2 * H])
        prod = acc[:, 0:HP * D]
        woa = sb("woa", [128, HP, D + 2])
        wob = part(acc, 128, 16768, HP, D + 2)
        ao_bc = acc[:, 17500:17500 + 2 * D].rearrange("p (r j) -> p r j", r=2)
        gh = sb("gh", [128, HP])
        bh = sb("bh", [128, HP])
        stats = acc[:, H * SW - HP * NC * 6:].rearrange("p (h c k) -> p h c k", h=HP, c=NC)
        mv = sb("mv", [128, HP, 2])
        scl = sb("scl", [128, HP])
        shf = sb("shf", [128, HP])
        go = sb("go", [128, 1])
        bo = sb("bo", [128, 1])
        brow = sb("brow", [1, D + 2])
        bres = sb("bres", [1, D])
        w_a = sb("w_a", [128, D])
        w_b = sb("w_b", [128, D])
        stg = sb("stg", [128, 2, CH])
        vrow = stg[:, :, :].rearrange("p u n -> p (u n)")[:, 0:5 * D].rearrange("p (i n) -> p i n", i=5)
        col1 = sb("col1", [128, 2 * H])
        amax = sb("amax", [128, H])
        a8 = sb("a8", [H, 1])
        m8 = sb("m8", [H, 1])
        t8 = sb("t8", [H, H])
        big8 = sb("big8", [H, 128])
        nsc = part(acc, NP_, 0, NT, 2 * H)
        nwin = part(acc, NP_, 2048, NT, K0)
        nlr = part(acc, NP_, 4096, NT, H)
        nres = part(acc, NP_, 5120, NT, K0)
        nw3 = acc[0:NP_, 7168:7168 + NT * 3 * K0 // 2].bitcast(BF16).rearrange("p (t k) -> p t k", t=NT)
        pairs_i = acc[0:SB, 8192:8192 + 2 * TH * EP].bitcast(I32)
        pairs_f = acc[0:SB, 12288:12288 + 2 * TH * EP]
        gmin = sb("gmin", [SB, 2 * PAIRS])
        gmax = sb("gmax", [SB, 2 * PAIRS])
        tb_b, tb_r, tb_e, tb_bi, tb_ri = (part(acc, SB, 7168 + i * NV * 2 * PAIRS, NV, 2 * PAIRS) for i in range(5))
        tb_bi, tb_ri = (t.bitcast(I32) for t in (tb_bi, tb_ri))
        bmn = sb("bmn", [SB, 2])
        tch = sb("tch", [SB, 3])
        pidx = sb("pidx", [SB, 2])
        NCAND = 2 * NS + NV
        cand = sb("cand", [SB, NCAND])
        ccol = sb("ccol", [NCAND, 1])
        lh = sb("lh", [1, NCAND])
        xt = part(acc, NP_, 12544, 2, TC, D)
        ht = part(acc, NP_, 12544 + 2 * TC * D, 2, TC, D)
        zt = part(acc, NP_, 12544 + 4 * TC * D, 2, TC, D)
        rowb = part(acc, NP_, 12544 + 4 * TC * D, 2, TC, ROW0)
        xT = part(acc, 128, 16768, 2, CH)
        aT = part(acc, 128, 16768 + 2 * CH, 2, CH)
        y1 = part(acc, 128, 8192, 2, HP, CH)
        d8, q8, e8, r8 = (part(acc, H, 12544 + 2 * CH * i, 2, CH) for i in range(4))
        lnst = sb("lnst", [NP_, 2, TC, 6])
        lnmv = sb("lnmv", [NP_, 2, TC, 2])
        lnr = sb("lnr", [NP_, 2, TC])

        psa = psb("psa", [128, 4, 512])
        psc = psb("psc", [128, 4, 512])
        p_oht = psc[:, 0, :].bitcast(BF16).rearrange("p (t n) -> p t n", t=TH)
        p_adx = psc[:, 1, :]
        p_den = psc[:, 2, :]
        p_dens = (psc[:, 2, :], psc[:, 3, :])

        cst = sem("cst")
        cst_l = sem("cst_l")
        alone = sem("alone")
        phase = sem("phase")
        sp_in = sem("sp_in")
        sp_out = sem("sp_out")
        dve_l = sem("dve_l")
        cand_ready = sem("cand_ready")
        cand_t = sem("cand_t")
        lh_col = sem("lh_col")
        lh_row = sem("lh_row")
        tables = sem("tables")
        mx_part = sem("mx_part")
        mx_t = sem("mx_t")
        mx_diag = sem("mx_diag")
        mx_bc = sem("mx_bc")
        win_ready = sem("win_ready")
        sqrt_arg = sem("sqrt_arg")
        sqrt_done = sem("sqrt_done")
        m_ready = sem("m_ready")
        bn_ready = sem("bn_ready")
        bias_ps = sem("bias_ps")
        bias_sb = sem("bias_sb")
        idx_in = [sem(f"idx_in{i}") for i in range(2)]
        rows_in = [sem(f"rows_in{i}") for i in range(2)]
        adw_in = [sem(f"adw_in{i}") for i in range(2)]
        ohb_ready = sem("ohb_ready")
        oh_ready = sem("oh_ready")
        oht_ps = sem("oht_ps")
        oht_sb = sem("oht_sb")
        adx_ready = sem("adx_ready")
        exp_arg = sem("exp_arg")
        wgt_ready = sem("wgt_ready")
        den_ps = sem("den_ps")
        rhs_ready = sem("rhs_ready")
        sums_ps = sem("sums_ps")
        sums_used = sem("sums_used")
        dve_w = sem("dve_w")
        dve_r = sem("dve_r")
        fl_ps = sem("fl_ps")
        fl_sb = sem("fl_sb")
        fl_out = [sem(f"fl_out{i}") for i in range(2)]
        fl_free = sem("fl_free")
        rng_done = sem("rng_done")
        den_out = sem("den_out")

        def phase_sems(name, plain, primed=()):
            S = {k: sem(f"{name}_{k}") for k in tuple(plain) + tuple(primed)}
            S["primed"] = [S[k] for k in primed]
            return S

        n_x = phase_sems("n_x", ("in0", "in1", "xps", "row", "out0", "out1"), ("xsb", "mps", "msb", "asb", "stored"))
        n_bn = phase_sems("n_bn", ("in0", "in1", "add", "bound", "expd", "rec", "bc", "row", "stat", "own", "out0", "out1"))
        n_msg = phase_sems("n_msg", ("in0", "in1", "out0", "out1"), ("mps", "row", "msb", "dsb", "used", "stored"))
        n_gn = phase_sems("n_gn", ("in0", "in1", "add", "bound", "expd", "rec", "bc", "own"), ("row",))
        n_c = [phase_sems(f"n_c{k}", ("rec", "bc", "own")) for k in range(2)]
        n_fin = [phase_sems(f"n_f{k}", ("in0", "in1", "xps", "acp", "var", "std", "row", "own_a", "own_b", "out0", "out1"),
                            ("xsb", "mps", "msb", "stored")) for k in range(3)]

        block = ctx.enter_context(nc.Block())
        ENGINES = 5

        def phase_end(eng, k):
            eng.drain().then_inc(phase, 1)
            eng.wait_ge(phase, ENGINES * k)

        def node_ranges(eng, spec, run, after=None):
            def rounds(s0, v, lo, hi):
                longest = eng.value_load(lohi[0:1, ds(v + 2 * NS, 1)], min_val=1, max_val=N)
                with eng.Fori(0, longest, WIN) as w0:
                    run(s0, v, lo, hi, w0)
            if spec["parts"]:
                with eng.Fori(0, NS) as s:
                    lo = eng.value_load(lohi[0:1, ds(s + NS, 1)], min_val=0, max_val=SB - 1)
                    hi = eng.value_load(lohi[0:1, ds(s, 1)], min_val=1, max_val=SB)
                    rounds(s * SN, s, lo, hi)
                    if after:
                        after(s)
            else:
                rounds(0, WHOLE, 0, SB)

        def halves(eng, lo, hi, nxt, front, main):
            front(lo, 0, True)
            with eng.Fori(lo, hi) as b:
                main(b, 0, lambda: front(b, 1, False))
                eng.reg_mov(nxt, b + 1)
                eng.reg_alu(nxt, nxt, SB - 1, ALU.min)
                ahead = eng.snap(nxt, min_val=0, max_val=SB - 1)
                main(b, 1, lambda: front(ahead, 0, False))

        MAX_ROUNDS = NS * (SN // WIN + 1) + 3 * (N // WIN + 1)
        MAX_BLOCKS = (SB + 1) * MAX_ROUNDS
        MAX_HALVES = 2 * MAX_BLOCKS

        def count(eng, reg, most):
            eng.reg_add(reg, reg, 1)
            return eng.snap(reg, min_val=1, max_val=most)

        def value(eng, reg, most=MAX_HALVES):
            return eng.snap(reg, min_val=1, max_val=most)

        G0 = dict(table=t_gat0, width=ROW0, heads=H, weighted=True, parts=True, window=win0_d, k=K0, cols=SN, count=True)
        G1 = dict(table=t_gat1, width=ROW1, heads=1, weighted=True, parts=False, window=win1_d, k=K1, cols=N, count=True)
        S0 = dict(table=t_sage0, width=D, heads=1, weighted=False, parts=False, cols=N, count=True)
        S1 = dict(table=t_sage1, width=D, heads=1, weighted=False, parts=False, cols=N, count=False)

        def acc_view(spec):
            return acc8 if spec["heads"] == H else acc[:, 0:NW].rearrange("p (h n) -> p h n", h=1)

        def sums(q, h):
            return psa[:, q, 0:h * WIN]

        NCHUNK = HP * NFC

        def rows_of(table, c):
            return table[ds(c * CH, CH), :].rearrange("(t p) w -> p t w", p=NP_)

        def pool_pass(eng, spec, ni, nk):
            def run(s0, v, lo, hi, w0):
                with eng.Fori(lo, hi):
                    i = count(eng, ni, MAX_BLOCKS)
                    for half in range(2):
                        k = count(eng, nk, MAX_HALVES)
                        eng.wait_ge(idx_in[half], i * 16)
                        for j in range(half * TH, half * TH + TH):
                            if j % 2 == 0:
                                eng.wait_ge(sums_ps, k * PAIRS + (j % TH // 2 + 1))
                                eng.sem_inc(alone, 1)
                            eng.indirect_dma_start(rows[:, j, 0:spec["width"]], None, spec["table"],
                                                   bass.IndirectOffsetOnAxis(ap=idx[:, j:j + 1], axis=0)
                                                   ).then_inc(rows_in[half], 16)
                eng.reg_add(ni, ni, 1)
                eng.reg_add(nk, nk, 1)
            node_ranges(eng, spec, run)

        def pool_store(eng, S, primed, src, table, width):
            def store(e, u):
                eng.wait_ge(S["row"], e + (u + 1 + primed))
                eng.dma_start(rows_of(table, e + u), src[:, u, :, 0:width]).then_inc(S[f"out{u}"], 16)

            def stored(e, u):
                eng.wait_ge(S[f"out{u}"], e * 8 + 16)
                eng.sem_inc(S["stored"], 1)
            by_chunk(eng, store, stored)

        @block.gpsimd
        def _(eng):
            ni, nk = (eng.alloc_register(f"{n}_pool") for n in ("ni", "nk"))
            eng.reg_mov(ni, 0)
            eng.reg_mov(nk, 0)
            link = Links(eng, cst_l)
            eng.memset(ones[:, :], 1.0).then_inc(cst, 1)
            eng.memset(zeros[:, :], 0.0).then_inc(cst, 1)
            link(eng.memset(ident[:, :], 0.0))
            link(eng.memset(sel[:, :, :], 0.0))
            eng.affine_select(out=ident[:, :], in_=ident[:, :], compare_op=ALU.not_equal, fill=1.0, base=0,
                              pattern=[[-1, 128]], channel_multiplier=1).then_inc(cst, 1)
            for r in range(2):
                v = sel[:, :, r * DH:(r + 1) * DH]
                eng.affine_select(out=v, in_=v, compare_op=ALU.not_equal, fill=1.0, base=-r,
                                  pattern=[[-2, HP], [0, DH]], channel_multiplier=1).then_inc(cst, 1)
            eng.iota(iota_w[:, :], pattern=[[1, WIN]], base=0, channel_multiplier=0,
                     allow_small_or_imprecise_dtypes=True).then_inc(cst, 1)
            eng.iota(pidx[:, 0:1], pattern=[[0, 1]], base=1, channel_multiplier=1,
                     allow_small_or_imprecise_dtypes=True).then_inc(cst, 1)
            eng.iota(pidx[:, 1:2], pattern=[[0, 1]], base=SB, channel_multiplier=-1,
                     allow_small_or_imprecise_dtypes=True).then_inc(cst, 1)
            eng.sem_inc(adx_ready, 2)
            eng.sem_inc(sums_ps, 2 * PAIRS)
            eng.sem_inc(sums_used, 2 * PAIRS)
            eng.sem_inc(rhs_ready, PAIRS)
            eng.sem_inc(den_ps, 1)
            eng.sem_inc(fl_sb, 2)
            eng.sem_inc(fl_free, 2)
            for S in (n_x, n_bn, n_msg, n_gn, *n_fin):
                for s_ in S["primed"]:
                    eng.sem_inc(s_, 2)
            phase_end(eng, 1)
            pool_store(eng, n_x, 0, rowb, t_gat0, ROW0)
            phase_end(eng, 2)
            pool_pass(eng, G0, ni, nk)
            phase_end(eng, 3)
            phase_end(eng, 4)
            pool_store(eng, n_msg, 2, rowb, t_gat1, ROW1)
            phase_end(eng, 5)
            pool_pass(eng, G1, ni, nk)
            phase_end(eng, 6)
            phase_end(eng, 7)
            pool_store(eng, n_fin[0], 0, zt, t_sage0, D)
            phase_end(eng, 8)
            pool_pass(eng, S0, ni, nk)
            phase_end(eng, 9)
            phase_end(eng, 10)
            pool_store(eng, n_fin[1], 0, zt, t_sage1, D)
            phase_end(eng, 11)
            pool_pass(eng, S1, ni, nk)
            phase_end(eng, 12)
            phase_end(eng, 13)
            pool_store(eng, n_fin[2], 0, zt, out, D)
            phase_end(eng, 14)

        def sp_pass(eng, spec, regs, bases):
            nb, ni, nf, nxt = regs
            k = spec.get("k")

            def load_idx(half, block_):
                eng.dma_start(idx[:, half * TH:half * TH + TH],
                              src_t[:, ds(block_ * (2 * TH) + half * TH, TH)]).then_inc(idx_in[half], 16)

            def run(s0, v, lo, hi, w0):
                def front(blk, half, first):
                    if not spec["weighted"]:
                        return
                    f = count(eng, nf, MAX_HALVES)
                    eng.load(bases, baser[0:1, ds(v * NPAIR + blk * (2 * PAIRS) + half * PAIRS, PAIRS)])
                    eng.wait_ge(adx_ready, f + 1 if first else f)
                    for q in range(PAIRS):
                        eng.reg_add(bases[q], bases[q], w0)
                        eng.reg_alu(bases[q], bases[q], spec["cols"], ALU.min)
                        at = eng.snap(bases[q], min_val=0, max_val=spec["cols"])
                        eng.dma_start(adw[:, half, q, 0:k], spec["window"][:, ds(at + s0, WIN), :]).then_inc(adw_in[half], 16)

                def main(blk, half, next_front):
                    if half == 0:
                        count(eng, nb, MAX_BLOCKS)
                        eng.reg_add(ni, ni, 1)
                    next_front()
                    eng.reg_mov(nxt[1], blk + 1)
                    eng.reg_alu(nxt[1], nxt[1], SB - 1, ALU.min)
                    eng.wait_ge(rows_in[half], value(eng, nb) * (16 * TH))
                    load_idx(half, eng.snap(nxt[1], min_val=0, max_val=SB - 1))
                eng.reg_add(ni, ni, 1)
                for half in range(2):
                    load_idx(half, lo)
                halves(eng, lo, hi, nxt[0], front, main)
                for half in range(2):
                    eng.wait_ge(idx_in[half], value(eng, ni) * 16)
                eng.sem_inc(alone, 1)

            def after(s):
                eng.wait_ge(rng_done, s + 1)
                eng.dma_start(den0_d[:, ds(s * SN, SN)], den[:, 0:SN]).then_inc(den_out, 16)
                for i in range(NCHUNK):
                    p, ck, u = i % HP, i // HP, i % 2
                    eng.wait_ge(fl_sb, s * NCHUNK + (i + 1 + 2))
                    eng.dma_start(y1_d[p, :, ds(s * SN + ck * CH, CH)], stg[:, u, :]).then_inc(fl_out[u], 16)
                    for k in ([i - 1] if i else []) + ([i] if i == NCHUNK - 1 else []):
                        eng.wait_ge(fl_out[k % 2], s * (16 * NCHUNK // 2) + 16 * (k // 2 + 1))
                        eng.sem_inc(fl_free, 1)
            node_ranges(eng, spec, run, after)

        def sp_node(eng, S, first, second=None):
            def load(e, u):
                eng.wait_ge(S["stored"], e + (u + 1))
                eng.dma_start(xt[:, u, :, :], rows_of(first, e + u)).then_inc(S[f"in{u}"], 16)
                if second is not None:
                    eng.dma_start(ht[:, u, :, :], rows_of(second, e + u)).then_inc(S[f"in{u}"], 16)
            by_chunk(eng, load)

        def chunk(src, at):
            return src[:, :, ds(at, CH)].rearrange("c p n -> p c n")

        @block.sync
        def _(eng):
            regs = [eng.alloc_register(f"{n}_sp") for n in ("nb", "ni", "nf")]
            bases = [eng.alloc_register(f"base_sp{q}") for q in range(PAIRS)]
            for r in regs:
                eng.reg_mov(r, 0)
            regs.append([eng.alloc_register(f"nxt_sp{i}") for i in range(2)])
            n_in, n_out = [0], [0]

            def load(dst_, src_, **kw):
                eng.dma_start(dst_, src_, **kw).then_inc(sp_in, 16)
                n_in[0] += 1

            def store(dst_, src_):
                eng.dma_start(dst_, src_).then_inc(sp_out, 16)
                n_out[0] += 1

            def store_windows(table, k):
                for r in range(3):
                    store(table[r, 0:N, :].rearrange("(t p) c -> p t c", p=NP_), nw3[:, :, r * k:(r + 1) * k])
                    store(table[r, N:NW, :], nw3[0:WIN, 0, r * k:(r + 1) * k])

            load(pairs_i, dst.rearrange("(p n) -> p n", p=SB))
            load(dsti, dst_t)
            load(w_sb[:, :, :], W_heads.rearrange("h k j -> k h j"))
            load(a_bc[:, :, :], a_heads.rearrange("(o h) j -> o h j", o=1).to_broadcast([128, H, 2 * DH]))
            load(woa[:, :, 0:D], W_out.rearrange("(c p) n -> p c n", p=128))
            load(ao_bc[:, :, :], a_out.rearrange("(o r j) -> o r j", o=1, r=2).to_broadcast([128, 2, D]))
            load(gh[:, :], gamma_h.rearrange("(c a) j -> (a j) c", a=2), allow_slow_non_contiguous=True)
            load(bh[:, :], beta_h.rearrange("(c a) j -> (a j) c", a=2), allow_slow_non_contiguous=True)
            load(go[:, :], gamma_o.rearrange("(p o) -> p o", o=1))
            load(bo[:, :], beta_o.rearrange("(p o) -> p o", o=1))
            load(bres[:, :], b_res.rearrange("(o n) -> o n", o=1))
            eng.wait_ge(tables, 1)
            store(base_d.rearrange("v (p q) -> p v q", p=SB), tb_bi[:, :, :])
            store(baser_d.rearrange("v (p q) -> p v q", p=SB), tb_ri[:, :, :])
            eng.wait_ge(sp_out, 16 * n_out[0])
            load(basei, base_d.rearrange("(o v) q -> o (v q)", o=1).to_broadcast([EP, NV * NPAIR]))
            load(baser[:, :], baser_d.rearrange("(o v) q -> o (v q)", o=1))
            eng.wait_ge(sp_in, 16 * n_in[0])
            phase_end(eng, 1)
            sp_node(eng, n_x, x)
            eng.wait_ge(win_ready, 1)
            store_windows(win0_d, K0)
            eng.wait_ge(n_x["asb"], NC + 2)
            store(dsc0_d, den[:, 0:N])
            eng.wait_ge(sp_out, 16 * n_out[0])
            phase_end(eng, 2)
            sp_pass(eng, G0, regs, bases)
            eng.wait_ge(den_out, 16 * NS)
            phase_end(eng, 3)
            S = n_bn

            def load_chunk(e, u):
                eng.dma_start(y1[:, u, :, :], chunk(y1_d, (e + u) * CH)).then_inc(S[f"in{u}"], 16)
                eng.dma_start(d8[:, u, :], den0_d[:, ds((e + u) * CH, CH)]).then_inc(S[f"in{u}"], 16)
                eng.dma_start(q8[:, u, :], dsc0_d[:, ds((e + u) * CH, CH)]).then_inc(S[f"in{u}"], 16)

            def store_chunk(e, u):
                eng.wait_ge(S["row"], e + (u + 1))
                eng.dma_start(chunk(y1_d, (e + u) * CH), y1[:, u, :, :]).then_inc(S[f"out{u}"], 16)

            def chunk_free(e, u):
                eng.wait_ge(S["stat"], e + (u + 1))
                eng.wait_ge(S[f"out{u}"], e * 8 + 16)
                eng.sem_inc(alone, 1)
            by_chunk(eng, load_chunk, store_chunk, chunk_free)
            phase_end(eng, 4)
            def load_again(e, u):
                eng.wait_ge(n_msg["used"], e + (u + 1))
                eng.dma_start(y1[:, u, :, :], chunk(y1_d, (e + u) * CH)).then_inc(n_msg[f"in{u}"], 16)
            by_chunk(eng, load_again)
            eng.wait_ge(win_ready, 2)
            store_windows(win1_d, K1)
            store(dsc1_d, den[0:1, 0:N])
            eng.wait_ge(sp_out, 16 * n_out[0])
            phase_end(eng, 5)
            sp_pass(eng, G1, regs, bases)
            phase_end(eng, 6)
            load(w_a[:, :], W_res)

            def load_scores(e, u):
                eng.wait_ge(n_gn["row"], e + (u + 1))
                eng.dma_start(q8[0:1, u, :], dsc1_d[:, ds((e + u) * CH, CH)]).then_inc(n_gn[f"in{u}"], 16)
            by_chunk(eng, load_scores)
            eng.wait_ge(sp_in, 16 * n_in[0])
            phase_end(eng, 7)
            sp_node(eng, n_fin[0], x)
            phase_end(eng, 8)
            sp_pass(eng, S0, regs, bases)
            phase_end(eng, 9)

            def sage_weights(Wl, Wr, vectors):
                load(w_a[:, :], Wl)
                load(w_b[:, :], Wr)
                for i, vec in enumerate(vectors):
                    load(vrow[:, i, :], vec.rearrange("(o n) -> o n", o=1).to_broadcast([128, D]))
                eng.wait_ge(sp_in, 16 * n_in[0])
            sage_weights(Wl0, Wr0, (b0, g0, be0, rm0, rv0))
            phase_end(eng, 10)
            sp_node(eng, n_fin[1], t_sage0)
            phase_end(eng, 11)
            sp_pass(eng, S1, regs, bases)
            phase_end(eng, 12)
            sage_weights(Wl1, Wr1, (b1, g1, be1, rm1, rv1))
            phase_end(eng, 13)
            sp_node(eng, n_fin[2], t_sage0, t_sage1)
            phase_end(eng, 14)

        LOADS_1 = 16 * 11
        LOADS_T = 16 * 13
        LOADS_10 = LOADS_T + 16 + 16 * 7
        LOADS_13 = LOADS_10 + 16 * 7

        def act_pass(eng, spec, nf, nm, nxt):
            h = spec["heads"]

            def front(blk, half, first):
                f = count(eng, nf, MAX_HALVES)
                eng.wait_ge(oht_ps, f)
                eng.activation(oht[:, :, :], p_oht[0:3 * WIN, :, 0:EP], ACT.Copy).then_inc(oht_sb, 1)

            def main(blk, half, next_front):
                m = count(eng, nm, MAX_HALVES)
                eng.wait_ge(exp_arg, m)
                eng.activation(wgt[:, half, :, 0:h], s_d[:, :, 0:h], ACT.Exp).then_inc(wgt_ready, 1)
                next_front()

            def after(s):
                for i in range(NCHUNK):
                    u = i % 2
                    eng.wait_ge(fl_ps, s * NCHUNK + (i + 1))
                    eng.wait_ge(fl_free, s * NCHUNK + (i + 1))
                    eng.activation(stg[:, u, :], psa[:, u, 0:CH], ACT.Copy).then_inc(fl_sb, 1)
            node_ranges(eng, spec, lambda s0, v, lo, hi, w0: halves(eng, lo, hi, nxt, front, main), after)

        def act_bound(eng, S, h, loads):
            eng.wait_ge(m_ready, 1 if h == H else 2)

            def add(e, u):
                eng.wait_ge(S[f"in{u}"], e * (8 * loads) + 16 * loads)
                eng.activation(e8[0:h, u, :], q8[0:h, u, :], ACT.Identity, bias=a8[0:h, 0:1]).then_inc(S["add"], 1)

            def exponential(e, u):
                eng.wait_ge(S["bound"], e + (u + 1))
                eng.activation(e8[0:h, u, :], r8[0:h, u, :], ACT.Exp, bias=m8[0:h, 0:1], scale=-1.0).then_inc(S["expd"], 1)
            by_chunk(eng, add, exponential)

        def act_node(eng, S, affine, norm):
            def copies(e, u):
                eng.wait_ge(S["mps"], e + (u + 1))
                cols = acc[:, ds((e + u) * CH, CH)]
                if affine:
                    ins = eng.activation(aT[:, u, :], cols, ACT.Identity, bias=shf[:, 0:1], scale=scl[:, 0:1])
                else:
                    ins = eng.activation(aT[:, u, :], cols, ACT.Copy)
                ins.then_inc(S["acp"], 1)
                eng.wait_ge(S["xps"], e + (u + 1))
                eng.activation(xT[:, u, :], psc[:, u, 0:CH], ACT.Copy).then_inc(S["xsb"], 1)

            def deviation(e, u):
                eng.wait_ge(S["var"], e + (u + 1))
                eng.activation(lnr[:, u, :], lnr[:, u, :], ACT.Sqrt).then_inc(S["std"], 1)
            by_chunk(eng, copies, *([deviation] if norm else []))

        def act_sqrt(eng, ap, k):
            eng.wait_ge(sqrt_arg, k)
            eng.activation(ap, ap, ACT.Sqrt).then_inc(sqrt_done, 1)

        @block.scalar
        def _(eng):
            nf, nm, nxt = (eng.alloc_register(f"{n}_act") for n in ("nf", "nm", "nxt"))
            eng.reg_mov(nf, 0)
            eng.reg_mov(nm, 0)
            eng.wait_ge(cst, 8)
            eng.activation(identb[:, :], ident[:, :], ACT.Copy)
            phase_end(eng, 1)
            S = n_x

            def copy_x(e, u):
                eng.wait_ge(S["mps"], e + (u + 1))
                eng.wait_ge(S["xps"], e + (u + 1))
                eng.activation(xT[:, u, :], psc[:, u, 0:CH], ACT.Copy).then_inc(S["xsb"], 1)

            def copy_scores(e, u):
                eng.wait_ge(S["mps"], e + (u + 3))
                eng.activation(den[:, ds((e + u) * CH, CH)], psc[0:H, 2 + u, 0:CH], ACT.Copy).then_inc(S["asb"], 1)
            by_chunk(eng, copy_x, copy_scores)
            phase_end(eng, 2)
            act_pass(eng, G0, nf, nm, nxt)
            phase_end(eng, 3)
            act_bound(eng, n_bn, H, 3)
            act_sqrt(eng, scl[:, :], 1)
            phase_end(eng, 4)
            S = n_msg

            def copy_rows(e, u):
                eng.wait_ge(S["mps"], e + (u + 3))
                eng.wait_ge(S["stored"], e + (u + 1))
                eng.wait_ge(S["msb"], e + (u + 1))
                eng.activation(rowb[:, u, :, 0:D + 2].rearrange("p (a b) k -> p a b k", a=2),
                               psa[0:NP_, 2 * u:2 * u + 2, 0:2 * (D + 2)].rearrange("p a (b k) -> p a b k", b=2),
                               ACT.Copy).then_inc(S["row"], 1)
            by_chunk(eng, copy_rows)
            phase_end(eng, 5)
            act_pass(eng, G1, nf, nm, nxt)
            phase_end(eng, 6)
            act_bound(eng, n_gn, 1, 1)
            act_sqrt(eng, scl[:, 0:1], 2)
            phase_end(eng, 7)
            act_node(eng, n_fin[0], True, True)
            phase_end(eng, 8)
            phase_end(eng, 9)
            act_sqrt(eng, vrow[:, 4, :], 3)
            phase_end(eng, 10)
            act_node(eng, n_fin[1], False, False)
            phase_end(eng, 11)
            phase_end(eng, 12)
            act_sqrt(eng, vrow[:, 4, :], 4)
            phase_end(eng, 13)
            act_node(eng, n_fin[2], False, True)
            phase_end(eng, 14)

        nwins = []

        def pe_pass(eng, spec, regs):
            nb, nf, nm, nk, nxt = regs
            h, k = spec["heads"], spec.get("k")

            def front(blk, half, first):
                count(eng, nf, MAX_HALVES)
                if not spec["weighted"]:
                    return
                eng.wait_ge(ohb_ready, value(eng, nf))
                for j in range(TH):
                    last = eng.transpose(p_oht[0:3 * WIN, j, 0:EP], ohb[:, half, j, :], identb[0:EP, 0:EP])
                last.then_inc(oht_ps, 1)
                if first:
                    scores(half)

            def scores(half):
                f = value(eng, nf)
                eng.wait_ge(oht_sb, f)
                count(eng, nwins[half], MAX_HALVES)
                eng.wait_ge(adw_in[half], value(eng, nwins[half]) * (16 * PAIRS))
                for j in range(TH):
                    last = eng.matmul(p_adx[0:EP, j * k:(j + 1) * k], oht[:, j, :], adw[:, half, j // 2, 0:k],
                                      start=True, stop=True)
                last.then_inc(adx_ready, 1)

            def main(blk, half, next_front):
                if half == 0:
                    count(eng, nb, MAX_BLOCKS)
                m = count(eng, nm, MAX_HALVES)
                kk = count(eng, nk, MAX_HALVES)
                if spec["weighted"]:
                    eng.wait_ge(wgt_ready, m)
                else:
                    eng.wait_ge(oh_ready, value(eng, nf))
                    eng.wait_ge(rows_in[half], value(eng, nb) * (16 * TH))
                if spec["count"]:
                    for j in range(TH):
                        left = wgt[:, half, j, 0:h] if spec["weighted"] else ones[0:EP, 0:1]
                        last = eng.matmul(p_dens[half][0:h, (j // 2) * WIN:(j // 2 + 1) * WIN], left,
                                          oh[:, half, j, :], start=(j % 2 == 0), stop=(j % 2 == 1))
                    if spec["weighted"]:
                        last.then_inc(den_ps, 1)
                next_front()
                for q in range(PAIRS):
                    if q == PAIRS // 2 and spec["weighted"]:
                        scores(1 - half)
                    if spec["weighted"]:
                        eng.wait_ge(rhs_ready, m * PAIRS + (q + 1))
                    eng.wait_ge(sums_used, kk * PAIRS + (q + 1))
                    for j in (2 * q, 2 * q + 1):
                        right = rhs[:, half, j, 0:h * WIN] if spec["weighted"] else oh[:, half, j, :]
                        last = eng.matmul(sums(q, h), rows[:, half * TH + j, 0:D], right,
                                          start=(j == 2 * q), stop=(j == 2 * q + 1))
                    last.then_inc(sums_ps, 1)

            def after(s):
                eng.wait_ge(rng_done, s + 1)
                for i in range(NCHUNK):
                    p, ck, u = i % HP, i // HP, i % 2
                    eng.wait_ge(fl_sb, s * NCHUNK + (i + 1))
                    for r in range(2):
                        last = eng.matmul(psa[:, u, 0:CH], wz[:, 2 * p + r, :],
                                          acc8[:, 2 * p + r, ck * CH:(ck + 1) * CH], start=(r == 0), stop=(r == 1))
                    last.then_inc(fl_ps, 1)
                eng.wait_ge(fl_sb, (s + 1) * NCHUNK + 2)

            def run(s0, v, lo, hi, w0):
                kk = count(eng, nk, MAX_HALVES)
                eng.wait_ge(sums_used, kk * PAIRS + PAIRS)
                if spec["count"]:
                    eng.matmul(p_dens[1][0:h, 0:PAIRS * WIN], zeros[:, 0:h], ones[:, 0:PAIRS * WIN],
                               start=True, stop=True)
                for q in range(PAIRS):
                    eng.matmul(sums(q, h), zeros[:, :], ones[:, 0:h * WIN], start=True, stop=True).then_inc(sums_ps, 1)
                halves(eng, lo, hi, nxt, front, main)
            node_ranges(eng, spec, run, after)

        def pe_max(eng, h, k, spread):
            eng.wait_ge(mx_part, k)
            eng.transpose(p_den[0:h, 0:EP], col1[0:EP, 0:h], ident[0:EP, 0:EP]).then_inc(mx_t, 1)
            if spread:
                eng.wait_ge(mx_diag, spread)
                eng.matmul(p_adx[:, 0:h], ones[0:h, 0:128], t8[0:h, 0:h], start=True, stop=True).then_inc(mx_bc, 1)

        def pe_transpose(eng, S, tile, loads):
            def stage(e, u):
                eng.wait_ge(S[f"in{u}"], e * (8 * loads) + 16 * loads)
                eng.wait_ge(S["xsb"], e + (u + 1))
                for t in range(TC):
                    last = eng.transpose(psc[:, u, t * NP_:(t + 1) * NP_], tile[:, u, t, :], ident[0:NP_, 0:NP_])
                last.then_inc(S["xps"], 1)
            return stage

        def pe_node(eng, S, tile, loads, left_w, right_w, bias):
            def products(e, u):
                eng.wait_ge(S["msb"], e + (u + 1))
                eng.wait_ge(S["acp"], e + (u + 1))
                eng.wait_ge(S["xsb"], e + (u + 3))
                for t in range(TC):
                    o = psa[0:NP_, u, t * D:(t + 1) * D]
                    cols = slice(t * NP_, (t + 1) * NP_)
                    eng.matmul(o, aT[:, u, cols], left_w, start=True, stop=False)
                    eng.matmul(o, xT[:, u, cols], right_w, start=False, stop=False)
                    last = eng.matmul(o, ones[0:1, 0:NP_], bias, start=False, stop=True)
                last.then_inc(S["mps"], 1)
            by_chunk(eng, pe_transpose(eng, S, tile, loads), products)

        @block.tensor
        def _(eng):
            regs = [eng.alloc_register(f"{n}_pe") for n in ("nb", "nf", "nm", "nk", "nxt")]
            nwins.extend(eng.alloc_register(f"nwin{i}_pe") for i in range(2))
            for r in regs + nwins:
                eng.reg_mov(r, 0)
            eng.wait_ge(cst, 8)
            eng.wait_ge(cand_ready, 1)
            eng.transpose(p_den[0:NCAND, 0:SB], cand[:, :], ident[0:SB, 0:SB]).then_inc(cand_t, 1)
            eng.wait_ge(lh_col, 1)
            eng.matmul(p_adx[0:1, 0:NCAND], ccol[:, 0:1], ident[0:NCAND, 0:NCAND], start=True, stop=True).then_inc(lh_row, 1)
            phase_end(eng, 1)
            S = n_x

            def node_scores(e, u):
                eng.wait_ge(S["msb"], e + (u + 1))
                eng.wait_ge(S["asb"], e + (u + 1))
                eng.wait_ge(S["xsb"], e + (u + 3))
                for t in range(TC):
                    eng.matmul(psa[0:NP_, u, t * 2 * H:(t + 1) * 2 * H], xT[:, u, t * NP_:(t + 1) * NP_], wa[:, :],
                               start=True, stop=True)
                eng.matmul(psc[0:H, 2 + u, 0:CH], wa[:, H:2 * H], xT[:, u, :], start=True, stop=True).then_inc(S["mps"], 1)
            by_chunk(eng, pe_transpose(eng, S, xt, 1), node_scores)
            eng.wait_ge(S["asb"], NC + 2)
            pe_max(eng, H, 1, 1)
            phase_end(eng, 2)
            pe_pass(eng, G0, regs)
            phase_end(eng, 3)
            pe_max(eng, H, 2, 0)
            S = n_bn

            def spread_heads(e, u):
                eng.wait_ge(S["rec"], e + (u + 1))
                for p in range(HP):
                    last = eng.matmul((psa, psc)[u][:, p, 0:CH], sel[:, p, :], r8[:, u, :], start=True, stop=True)
                last.then_inc(S["bc"], 1)
            by_chunk(eng, spread_heads)
            eng.wait_ge(bn_ready, 1)
            for p in range(HP):
                last = eng.matmul(p_den[0:1, 0:D + 2], shf[:, p:p + 1], woa[:, p, :], start=(p == 0), stop=(p == HP - 1))
            last.then_inc(bias_ps, 1)
            phase_end(eng, 4)
            S = n_msg

            def messages(e, u):
                eng.wait_ge(S[f"in{u}"], e * 8 + 16)
                eng.wait_ge(S["row"], e + (u + 1))
                for t in range(TC):
                    o = psa[0:NP_, 2 * u + t // 2, (t % 2) * (D + 2):(t % 2 + 1) * (D + 2)]
                    for p in range(HP):
                        eng.matmul(o, y1[:, u, p, t * NP_:(t + 1) * NP_], wob[:, p, :], start=(p == 0), stop=False)
                    last = eng.matmul(o, ones[0:1, 0:NP_], brow[:, :], start=False, stop=True)
                last.then_inc(S["mps"], 1)
                eng.wait_ge(S["dsb"], e + (u + 1))
                o = psc[0:1, u, 0:CH]
                for p in range(HP):
                    eng.matmul(o, wob[:, p, D + 1:D + 2], y1[:, u, p, :], start=(p == 0), stop=False)
                eng.matmul(o, brow[:, D + 1:D + 2], ones[0:1, 0:CH], start=False, stop=True).then_inc(S["used"], 1)
            by_chunk(eng, messages)
            eng.wait_ge(S["dsb"], NC + 2)
            pe_max(eng, 1, 3, 2)
            phase_end(eng, 5)
            pe_pass(eng, G1, regs)
            phase_end(eng, 6)
            pe_max(eng, 1, 4, 0)

            def spread_row(S):
                def spread(e, u):
                    eng.wait_ge(S["rec"], e + (u + 1))
                    eng.matmul(psa[:, u, 0:CH], ones[0:1, 0:128], r8[0:1, u, :], start=True, stop=True).then_inc(S["bc"], 1)
                by_chunk(eng, spread)
            spread_row(n_gn)
            phase_end(eng, 7)
            pe_node(eng, n_fin[0], xt, 1, ident[:, :], w_a[:, :], bres[:, :])
            phase_end(eng, 8)
            pe_pass(eng, S0, regs)
            phase_end(eng, 9)
            spread_row(n_c[0])
            phase_end(eng, 10)
            pe_node(eng, n_fin[1], xt, 1, w_a[:, :], w_b[:, :], brow[:, 0:D])
            phase_end(eng, 11)
            pe_pass(eng, S1, regs)
            phase_end(eng, 12)
            spread_row(n_c[1])
            phase_end(eng, 13)
            pe_node(eng, n_fin[2], ht, 2, w_a[:, :], w_b[:, :], brow[:, 0:D])
            phase_end(eng, 14)

        class DynLinks:

            def __init__(self, eng, sem_, reg):
                self.eng, self.sem, self.reg, self.k = eng, sem_, reg, 0
                self.base = eng.snap(reg, min_val=0, max_val=16 * MAX_HALVES)

            def __call__(self, ins):
                self.k += 1
                ins.then_inc(self.sem, 1)
                self.eng.wait_ge(self.sem, self.base + self.k)

            def end(self):
                self.eng.reg_add(self.reg, self.reg, self.k)

        def dve_pass(eng, spec, regs, bases):
            nb, nf, nm, nk, nxt, nl = regs
            h, acc_v, weighted = spec["heads"], acc_view(spec), spec["weighted"]
            basef_v = basef[:, :, :].rearrange("p v q -> p (v q)")

            def pairs(ap):
                return ap.rearrange("p (q i) -> p q i", i=2)

            def run(s0, v, lo, hi, w0):
                def base_at(blk, half):
                    return ds(v * NPAIR + blk * (2 * PAIRS) + half * PAIRS, PAIRS)

                def front(blk, half, first):
                    f = count(eng, nf, MAX_HALVES)
                    link = DynLinks(eng, dve_w, nl)
                    if first and weighted:
                        eng.wait_ge(adx_ready, f + 1)
                    link(eng.tensor_scalar(cur[:, :], basef_v[:, base_at(blk, half)], roff[:, 0:1], s1col[:, 0:1],
                                           ALU.add, ALU.min))
                    link(eng.tensor_tensor(pairs(rel[:, :]), pairs(dstf[:, ds(blk * (2 * TH) + half * TH, TH)]),
                                           cur[:, :].unsqueeze(2).to_broadcast([EP, PAIRS, 2]), ALU.subtract))
                    if weighted:
                        eng.tensor_tensor(ohb[:, half, :, :].rearrange("p t (r n) -> p t r n", r=3),
                                          iota_w[:, :].unsqueeze(1).unsqueeze(1).to_broadcast([EP, TH, 3, WIN]),
                                          rel[:, :].unsqueeze(2).unsqueeze(2).to_broadcast([EP, TH, 3, WIN]),
                                          ALU.is_equal).then_inc(ohb_ready, 1)
                    eng.tensor_tensor(oh[:, half, :, :], iota_w[:, :].unsqueeze(1).to_broadcast([EP, TH, WIN]),
                                      rel[:, :].unsqueeze(2).to_broadcast([EP, TH, WIN]),
                                      ALU.is_equal).then_inc(oh_ready, 1)
                    link.end()

                def main(blk, half, next_front):
                    if half == 0:
                        count(eng, nb, MAX_BLOCKS)
                    m = count(eng, nm, MAX_HALVES)
                    if weighted:
                        link = DynLinks(eng, dve_w, nl)
                        eng.wait_ge(adx_ready, value(eng, nf) + 2)
                        eng.wait_ge(rows_in[half], value(eng, nb) * (16 * TH))
                        adx = p_adx[0:EP, 0:TH * (2 * h + 1)].rearrange("p (t k) -> p t k", t=TH)
                        t_, l_, m_, d_ = (a[:, :, 0:h] for a in (s_t, s_l, s_m, s_d))
                        eng.tensor_scalar(pen[:, :], adx[:, :, 2 * h], -1.0, BIG, ALU.add, ALU.mult)
                        link(eng.tensor_tensor(t_, rows[:, half * TH:half * TH + TH, D:D + h], adx[:, :, 0:h], ALU.add))
                        link(eng.scalar_tensor_tensor(l_, t_, SLOPE, t_, ALU.mult, ALU.max))
                        link(eng.tensor_tensor(m_, l_, pen[:, :].unsqueeze(2).to_broadcast([EP, TH, h]), ALU.add))
                        eng.tensor_tensor(d_, m_, adx[:, :, h:2 * h], ALU.subtract).then_inc(exp_arg, 1)
                        link(eng.tensor_tensor(smax[:, :, 0:h], smax[:, :, 0:h], m_, ALU.max))
                        link.end()
                    if not weighted:
                        add_sums(1 - half)
                        next_front()
                        set_bases(blk, half)
                        return
                    if spec["count"]:
                        eng.wait_ge(den_ps, m)
                        eng.sem_inc(alone, 1)
                    next_front()

                    def weighted_onehots(q):
                        if q == 0:
                            eng.wait_ge(wgt_ready, m)
                        two = slice(2 * q, 2 * q + 2)
                        eng.tensor_tensor(rhs[:, half, two, 0:h * WIN].rearrange("p t (h j) -> p t h j", h=h),
                                          oh[:, half, two, :].unsqueeze(2).to_broadcast([EP, 2, h, WIN]),
                                          wgt[:, half, two, 0:h].unsqueeze(3).to_broadcast([EP, 2, h, WIN]),
                                          ALU.mult).then_inc(rhs_ready, 1)
                    add_sums(1 - half, weighted_onehots)
                    set_bases(blk, half)

                def set_bases(blk, half):
                    eng.load(bases, baser[0:1, base_at(blk, half)])
                    for q in range(PAIRS):
                        eng.reg_add(bases[q], bases[q], w0)
                        eng.reg_alu(bases[q], bases[q], spec["cols"], ALU.min)

                def add_sums(half, before=None):
                    kk = count(eng, nk, MAX_HALVES)
                    link = DynLinks(eng, dve_w, nl)
                    for q in range(PAIRS):
                        if before:
                            before(q)
                        at = eng.snap(bases[q], min_val=0, max_val=spec["cols"])
                        a = acc_v[:, :, ds(at, WIN)]
                        eng.wait_ge(sums_ps, kk * PAIRS + (q + 1 + PAIRS))
                        if spec["count"]:
                            dn = den[0:h, ds(at, WIN)]
                            eng.tensor_tensor(dn, dn, p_dens[half][0:h, q * WIN:(q + 1) * WIN],
                                              ALU.add).then_inc(dve_w, 1)
                            link.k += 1
                        link(eng.tensor_tensor(a, a, sums(q, h).rearrange("p (h j) -> p h j", h=h), ALU.add))
                        eng.sem_inc(sums_used, 1)
                    link.end()

                for q in range(PAIRS):
                    eng.reg_mov(bases[q], spec["cols"])
                halves(eng, lo, hi, nxt, front, main)
                add_sums(1)
                link = DynLinks(eng, dve_w, nl)
                link(eng.tensor_scalar(roff[:, :], roff[:, :], float(WIN), None, ALU.add))
                link.end()

            def after(s):
                link = Links(eng, dve_r, s * (NCHUNK + 3))
                link(eng.tensor_scalar(s1col[:, :], s1col[:, :], float(SN), None, ALU.add))
                link(eng.memset(roff[:, :], 0.0))
                eng.sem_inc(rng_done, 1)
                for i in range(NCHUNK):
                    p, ck = i % HP, i // HP
                    eng.wait_ge(fl_ps, s * NCHUNK + (i + 1))
                    end = SW if ck == NFC - 1 else (ck + 1) * CH
                    link(eng.memset(acc8[:, 2 * p:2 * p + 2, ck * CH:end], 0.0))
                eng.wait_ge(den_out, s * 16 + 16)
                link(eng.memset(den[:, 0:SW], 0.0))
                eng.sem_inc(alone, 1)
            node_ranges(eng, spec, run, after)

        @block.vector
        def _(eng):
            regs = [eng.alloc_register(f"{n}_dve") for n in ("nb", "nf", "nm", "nk", "nxt", "nl")]
            bases = [eng.alloc_register(f"base_dve{q}") for q in range(PAIRS)]
            for r in regs:
                eng.reg_mov(r, 0)
            link = Links(eng, dve_l)
            ts, tt = eng.tensor_scalar, eng.tensor_tensor

            def dve_max(h, src, k, spread):
                eng.tensor_reduce(col1[0:EP, 0:h], src.rearrange("p m h -> p h m"), axis=AX, op=ALU.max).then_inc(mx_part, 1)
                eng.wait_ge(mx_t, k)
                top = a8 if spread else m8
                link(eng.tensor_reduce(top[0:h, :], p_den[0:h, 0:EP], axis=AX, op=ALU.max))
                if spread:
                    ts(t8[0:h, 0:h], ident[0:h, 0:h], a8[0:h, 0:1], None, ALU.mult).then_inc(mx_diag, 1)
                    eng.wait_ge(mx_bc, spread)
                    link(eng.tensor_copy(amax[:, 0:h], p_adx[:, 0:h]))

            def window_rows(h):
                sc, k = nsc[:, :, h:2 * h], 2 * h + 1
                link(tt(nlr[:, :, 0:h], sc, amax[0:NP_, 0:h].unsqueeze(1).to_broadcast([NP_, NT, h]), ALU.add))
                link(eng.scalar_tensor_tensor(nwin[:, :, h:2 * h], nlr[:, :, 0:h], SLOPE, nlr[:, :, 0:h], ALU.mult, ALU.max))
                link(eng.tensor_copy(nwin[:, :, 0:h], sc))
                link(eng.memset(nwin[:, :, 2 * h:2 * h + 1], 1.0))
                rest = nwin[:, :, 0:k]
                for r in range(3):
                    link(eng.tensor_copy(nw3[:, :, r * k:(r + 1) * k], rest))
                    if r < 2:
                        link(tt(nres[:, :, 0:k], rest, nw3[:, :, r * k:(r + 1) * k], ALU.subtract))
                        rest = nres[:, :, 0:k]
                eng.sem_inc(win_ready, 1)

            def clear_sums(cols_den):
                link(eng.memset(acc[:, :], 0.0))
                if cols_den:
                    link(eng.memset(den[:, :], 0.0))

            eng.wait_ge(cst, 8)
            eng.wait_ge(sp_in, LOADS_1)
            link(eng.tensor_copy(dstf[:, :], dsti))
            link(eng.tensor_copy(pairs_f, pairs_i))
            by_pair = pairs_f.rearrange("p (q n) -> p q n", n=2 * EP)
            link(eng.tensor_reduce(gmin[:, :], by_pair, axis=AX, op=ALU.min))
            link(eng.tensor_reduce(gmax[:, :], by_pair, axis=AX, op=ALU.max))
            for v in range(NV):
                s0, s1 = (0, N) if v == WHOLE else (v * SN, (v + 1) * SN)
                link(ts(tb_b[:, v, :], gmin[:, :], float(s0), float(s1), ALU.max, ALU.min))
                link(ts(tb_r[:, v, :], tb_b[:, v, :], float(-s0), None, ALU.add))
                link(ts(tb_e[:, v, :], gmax[:, :], float(s1 - 1), None, ALU.min))
                link(tt(tb_e[:, v, :], tb_e[:, v, :], tb_b[:, v, :], ALU.subtract))
                link(eng.tensor_reduce(cand[:, 2 * NS + v:2 * NS + v + 1], tb_e[:, v, :], axis=AX, op=ALU.max))
            link(eng.tensor_copy(tb_bi[:, :, :], tb_b[:, :, :]))
            link(eng.tensor_copy(tb_ri[:, :, :], tb_r[:, :, :]))
            eng.sem_inc(tables, 1)
            link(eng.tensor_reduce(bmn[:, 0:1], gmin[:, :], axis=AX, op=ALU.min))
            link(eng.tensor_reduce(bmn[:, 1:2], gmax[:, :], axis=AX, op=ALU.max))
            for s in range(NS):
                link(ts(tch[:, 0:1], bmn[:, 1:2], float(s * SN), None, ALU.is_ge))
                link(ts(tch[:, 1:2], bmn[:, 0:1], float((s + 1) * SN), None, ALU.is_lt))
                link(tt(tch[:, 2:3], tch[:, 0:1], tch[:, 1:2], ALU.mult))
                for i in range(2):
                    link(tt(cand[:, i * NS + s:i * NS + s + 1], tch[:, 2:3], pidx[:, i:i + 1], ALU.mult))
            eng.sem_inc(cand_ready, 1)
            eng.wait_ge(cand_t, 1)
            eng.tensor_reduce(ccol[:, :], p_den[0:NCAND, 0:SB], axis=AX, op=ALU.max).then_inc(lh_col, 1)
            eng.wait_ge(lh_row, 1)
            link(eng.tensor_copy(lh[:, :], p_adx[0:1, 0:NCAND]))
            lo = lh[:, NS:2 * NS]
            link(ts(lo, lo, -1.0, float(SB), ALU.mult, ALU.add))
            link(ts(lo, lo, float(SB - 1), None, ALU.min))
            link(eng.scalar_tensor_tensor(lh[:, 0:NS], lo, 1.0, lh[:, 0:NS], ALU.add, ALU.max))
            link(ts(lh[:, 2 * NS:], lh[:, 2 * NS:], 1.0, 1.0, ALU.add, ALU.max))
            link(eng.tensor_copy(lohi[:, :], lh[:, :]))
            link(eng.memset(wz[:, :, :], 0.0))
            for r in range(2):
                link(eng.tensor_copy(wz[:, :, :].rearrange("p (c a) n -> p c a n", a=2)[:, :, r, r * DH:(r + 1) * DH],
                                     w_sb[:, :, :].rearrange("p (c a) n -> p c a n", a=2)[:, :, r, :]))
                pv = prod.rearrange("p (h j) -> p h j", h=H)
                link(tt(pv, w_sb[:, :, :], a_bc[:, :, r * DH:(r + 1) * DH], ALU.mult))
                link(eng.tensor_reduce(wa[:, r * H:(r + 1) * H], pv, axis=AX, op=ALU.add))
            for r in range(2):
                pv = prod.rearrange("p (c j) -> p c j", c=HP)
                link(tt(pv, woa[:, :, 0:D], ao_bc[:, r, :].unsqueeze(1).to_broadcast([128, HP, D]), ALU.mult))
                link(eng.tensor_reduce(woa[:, :, D + r], pv, axis=AX, op=ALU.add))
            link(eng.memset(smax[:, :, :], -BIG))
            link(eng.memset(s1col[:, :], float(SN)))
            link(eng.memset(roff[:, :], 0.0))
            eng.wait_ge(sp_in, LOADS_T)
            link(eng.tensor_copy(basef[:, :, :].rearrange("p v q -> p (v q)"), basei))
            phase_end(eng, 1)
            S = n_x

            def score_rows(e, u):
                eng.wait_ge(S[f"in{u}"], e * 8 + 16)
                eng.tensor_copy(rowb[:, u, :, 0:D], xt[:, u, :, :])
                eng.wait_ge(S["mps"], e + (u + 3))
                sc = psa[0:NP_, u, 0:TC * 2 * H].rearrange("p (t k) -> p t k", t=TC)
                eng.tensor_copy(rowb[:, u, :, D:D + H], sc[:, :, 0:H]).then_inc(S["row"], 1)
                eng.tensor_copy(nsc[:, ds((e + u) * TC, TC), :], sc).then_inc(S["msb"], 1)
            by_chunk(eng, score_rows)
            eng.wait_ge(S["msb"], NC + 2)
            dve_max(H, nsc[:, :, 0:H], 1, 1)
            window_rows(H)
            phase_end(eng, 2)
            clear_sums(True)
            dve_pass(eng, G0, regs, bases)
            phase_end(eng, 3)
            dve_max(H, smax[:, :, :], 2, 0)
            eng.sem_inc(m_ready, 1)

            def reciprocals(S, h, dens):
                def bound(e, u):
                    eng.wait_ge(S["add"], e + (u + 1))
                    a = e8[0:h, u, :]
                    eng.scalar_tensor_tensor(r8[0:h, u, :], a, SLOPE, a, ALU.mult, ALU.max).then_inc(S["bound"], 1)

                def inverse(e, u):
                    own = Links(eng, S["own"], (e + u) * 3)
                    eng.wait_ge(S["expd"], e + (u + 1))
                    own(eng.scalar_tensor_tensor(d8[0:h, u, :], e8[0:h, u, :], DEN_EPS, dens(e, u), ALU.mult, ALU.add))
                    own(ts(d8[0:h, u, :], d8[0:h, u, :], TINY, None, ALU.max))
                    own(eng.reciprocal(r8[0:h, u, :], d8[0:h, u, :]))
                    eng.sem_inc(S["rec"], 1)
                return bound, inverse

            def normalise_heads(e, u):
                S = n_bn
                eng.wait_ge(S["bc"], e + (u + 1))
                yv = y1[:, u, :, :]
                tt(yv, yv, (psa, psc)[u][:, :, 0:CH], ALU.mult).then_inc(S["row"], 1)
                eng.wait_ge(S["row"], e + (u + 1))
                for p in range(HP):
                    last = eng.bn_stats(stats[:, p, ds(e + u, 1), :].rearrange("p o k -> p (o k)"), y1[:, u, p, :])
                last.then_inc(S["stat"], 1)
            by_chunk(eng, *reciprocals(n_bn, H, lambda e, u: d8[:, u, :]), normalise_heads)
            eng.drain().then_inc(dve_l, 1)
            link.k += 1
            eng.wait_ge(dve_l, link.k)

            def inverse_sqrt(out_, var, eps, k):
                link(ts(out_, var, eps, None, ALU.add))
                eng.sem_inc(sqrt_arg, 1)
                eng.wait_ge(sqrt_done, k)
                link(eng.reciprocal(out_, out_))

            def batch_norm(n, gamma, beta, k):
                for p in range(n):
                    link(eng.bn_aggr(mv[:, p, :], stats[:, p, :, :].rearrange("p c k -> p (c k)")))
                inverse_sqrt(scl[:, 0:n], mv[:, 0:n, 1], BN_EPS, k)
                link(tt(scl[:, 0:n], scl[:, 0:n], gamma, ALU.mult))
                link(tt(shf[:, 0:n], mv[:, 0:n, 0], scl[:, 0:n], ALU.mult))
                link(tt(shf[:, 0:n], beta, shf[:, 0:n], ALU.subtract))
            batch_norm(HP, gh[:, :], bh[:, :], 1)
            for p in range(HP):
                link(ts(wob[:, p, :], woa[:, p, :], scl[:, p:p + 1], None, ALU.mult))
            eng.sem_inc(bn_ready, 1)
            eng.wait_ge(bias_ps, 1)
            link(eng.tensor_copy(brow[:, :], p_den[0:1, 0:D + 2]))
            phase_end(eng, 4)
            S = n_msg

            def keep_scores(e, u):
                eng.wait_ge(S["row"], e + (u + 3))
                ts(nsc[:, ds((e + u) * TC, TC), 0:2], rowb[:, u, :, D:D + 2], 1.0, None, ALU.mult).then_inc(S["msb"], 1)
                eng.wait_ge(S["used"], e + (u + 3))
                ts(den[0:1, ds((e + u) * CH, CH)], psc[0:1, u, 0:CH], 1.0, None, ALU.mult).then_inc(S["dsb"], 1)
            by_chunk(eng, keep_scores)
            eng.wait_ge(S["msb"], NC + 2)
            dve_max(1, nsc[:, :, 0:1], 3, 2)
            eng.wait_ge(S["dsb"], NC + 2)
            window_rows(1)
            phase_end(eng, 5)
            clear_sums(True)
            link(eng.memset(smax[:, :, :], -BIG))
            link(eng.memset(s1col[:, :], float(N)))
            link(eng.memset(roff[:, :], 0.0))
            dve_pass(eng, G1, regs, bases)
            phase_end(eng, 6)
            dve_max(1, smax[:, :, 0:1], 4, 0)
            eng.sem_inc(m_ready, 1)
            def normalise(e, u):
                S = n_gn
                eng.wait_ge(S["bc"], e + (u + 1))
                cols = acc[:, ds((e + u) * CH, CH)]
                tt(cols, cols, psa[:, u, 0:CH], ALU.mult).then_inc(S["row"], 1)
                eng.wait_ge(S["row"], e + (u + 3))
                eng.bn_stats(stats[:, 0, ds(e + u, 1), :].rearrange("p o k -> p (o k)"), cols)
            by_chunk(eng, *reciprocals(n_gn, 1, lambda e, u: den[0:1, ds((e + u) * CH, CH)]), normalise)
            eng.drain().then_inc(dve_l, 1)
            link.k += 1
            eng.wait_ge(dve_l, link.k)
            batch_norm(1, go[:, :], bo[:, :], 2)
            phase_end(eng, 7)

            def layer_norm(S):
                def centre(e, u):
                    own = Links(eng, S["own_a"], (e + u) * 4)
                    eng.wait_ge(S["mps"], e + (u + 3))
                    eng.wait_ge(S["stored"], e + (u + 1))
                    z = zt[:, u, :, :]
                    own(tt(z, psa[0:NP_, u, 0:TC * D].rearrange("p (t n) -> p t n", t=TC), xt[:, u, :, :], ALU.add))
                    eng.sem_inc(S["msb"], 1)
                    for t in range(TC):
                        last = eng.bn_stats(lnst[:, u, t, :], zt[:, u, t, :])
                    own(last)
                    eng.sem_inc(alone, 1)
                    for t in range(TC):
                        last = eng.bn_aggr(lnmv[:, u, t, :], lnst[:, u, t, :])
                    own(last)
                    own(ts(lnr[:, u, :], lnmv[:, u, :, 1], LN_EPS, None, ALU.add))
                    eng.sem_inc(S["var"], 1)

                def scale(e, u):
                    own = Links(eng, S["own_b"], (e + u) * 2)
                    eng.wait_ge(S["std"], e + (u + 1))
                    own(eng.reciprocal(lnr[:, u, :], lnr[:, u, :]))
                    for t in range(TC):
                        z = zt[:, u, t, :]
                        last = ts(z, z, lnmv[:, u, t, 0:1], lnr[:, u, t:t + 1], ALU.subtract, ALU.mult)
                    own(last)
                    eng.sem_inc(S["row"], 1)
                by_chunk(eng, centre, scale)
            layer_norm(n_fin[0])
            phase_end(eng, 8)
            clear_sums(True)
            link(eng.memset(roff[:, :], 0.0))
            dve_pass(eng, S0, regs, bases)
            phase_end(eng, 9)

            def neighbour_means(S, first):
                def inverse(e, u):
                    own = Links(eng, S["own"], (e + u) * (3 if first else 1))
                    cnt = den[0:1, ds((e + u) * CH, CH)]
                    if first:
                        own(ts(d8[0:1, u, :], cnt, 1.0, None, ALU.max))
                        own(eng.reciprocal(r8[0:1, u, :], d8[0:1, u, :]))
                        own(ts(cnt, r8[0:1, u, :], 1.0, None, ALU.mult))
                    else:
                        own(ts(r8[0:1, u, :], cnt, 1.0, None, ALU.mult))
                    eng.sem_inc(S["rec"], 1)

                def scale(e, u):
                    eng.wait_ge(S["bc"], e + (u + 1))
                    cols = acc[:, ds((e + u) * CH, CH)]
                    tt(cols, cols, psa[:, u, 0:CH], ALU.mult)
                by_chunk(eng, inverse, scale)

            def fold(loads, k):
                eng.wait_ge(sp_in, loads)
                b_, g_, be_, rm_, rv_ = (vrow[:, i, :] for i in range(5))
                inverse_sqrt(rv_, rv_, BN_EPS, k)
                link(tt(g_, g_, rv_, ALU.mult))
                link(tt(w_a[:, :], w_a[:, :], g_, ALU.mult))
                link(tt(w_b[:, :], w_b[:, :], g_, ALU.mult))
                link(tt(b_, b_, rm_, ALU.subtract))
                link(tt(b_, b_, g_, ALU.mult))
                link(tt(brow[:, 0:D], b_[0:1, :], be_[0:1, :], ALU.add))
            neighbour_means(n_c[0], True)
            fold(LOADS_10, 3)
            phase_end(eng, 10)
            S = n_fin[1]

            def relu(e, u):
                eng.wait_ge(S["mps"], e + (u + 3))
                eng.wait_ge(S["stored"], e + (u + 1))
                ts(zt[:, u, :, :], psa[0:NP_, u, 0:TC * D].rearrange("p (t n) -> p t n", t=TC), 0.0, None,
                   ALU.max).then_inc(S["row"], 1)
                eng.wait_ge(S["row"], e + (u + 1))
                eng.sem_inc(S["msb"], 1)
            by_chunk(eng, relu)
            phase_end(eng, 11)
            clear_sums(False)
            link(eng.memset(roff[:, :], 0.0))
            dve_pass(eng, S1, regs, bases)
            phase_end(eng, 12)
            neighbour_means(n_c[1], False)
            fold(LOADS_13, 4)
            phase_end(eng, 13)
            layer_norm(n_fin[2])
            phase_end(eng, 14)


def kernel(x, src, dst, **weights):
    import concourse.bacc as bacc
    from concourse.bass_utils import run_bass_kernel_spmd

    def by_tile(a):
        return np.ascontiguousarray(np.asarray(a).reshape(ET, EP).T)

    w = {k.split("gnn_")[0] + k.split("gnn_")[1]: np.asarray(v) for k, v in weights.items()}
    arrays = {
        "x": np.asarray(x), "src_t": by_tile(src), "dst_t": by_tile(dst), "dst": np.asarray(dst),
        "W_heads": w["L0_W_heads"], "a_heads": w["L0_a_heads"], "gamma_h": w["L0_gamma_h"], "beta_h": w["L0_beta_h"],
        "W_out": w["L0_W_out"], "a_out": w["L0_a_out"], "gamma_o": w["L0_gamma_o"], "beta_o": w["L0_beta_o"],
        "W_res": w["L0_W_res"], "b_res": w["L0_b_res"],
    }
    for i in range(2):
        arrays[f"Wl{i}"] = w[f"L1_Wl{i}"].T
        arrays[f"Wr{i}"] = w[f"L1_Wr{i}"].T
        for k in ("b", "g", "be", "rm", "rv"):
            arrays[f"{k}{i}"] = w[f"L1_{k}{i}"]
    nc = bacc.Bacc("TRN2", target_bir_lowering=False, num_devices=1)
    feeds, args = {}, {}
    for name, a in arrays.items():
        a = np.ascontiguousarray(a)
        feeds[f"in_{name}"] = a
        args[name] = nc.dram_tensor(f"in_{name}", a.shape, mybir.dt.from_np(a.dtype), kind="ExternalInput").ap()
    args["out"] = nc.dram_tensor("out_0", (N, D), F32, kind="ExternalOutput").ap()
    gnn_kernel(nc, **args)
    return run_bass_kernel_spmd(nc, [feeds], core_ids=[0]).results[0]["out_0"]
```

```python
from contextlib import ExitStack

import numpy as np
import concourse.bass as bass
from concourse import mybir

F32 = mybir.dt.float32
I32 = mybir.dt.int32
I16 = mybir.dt.int16
BF16 = mybir.dt.bfloat16
ALU = mybir.AluOpType
ACT = mybir.ActivationFunctionType
AX = mybir.AxisListType.X
ds = bass.ds

N = 12500
E = 200000
D = 128
H = 8
DH = 64
NP = 125
NT = N // NP
TC = 4
CH = TC * NP
NC = N // CH
EP = 128
TH = 8
PAIRS = TH // 2
SB = -(-E // (2 * TH * EP))
ET = SB * 2 * TH
NOWHERE = 2 * N
NPAIR = ET // 2
WIN = 22
NS = 5
SN = N // NS
NV = NS + 1
WHOLE = NS
SW = SN + WIN
NW = N + WIN
HP = H // 2
NFC = SN // CH
K0 = 2 * H + 1
K1 = 3
ROW0 = D + H
ROW1 = D + 1
SLOPE = 0.2
BN_EPS = 1e-5
LN_EPS = 1e-5
DEN_EPS = 1e-10
TINY = 1.2e-38
BIG = 1e30


class Links:

    def __init__(self, eng, sem, base=0):
        self.eng, self.sem, self.base, self.k = eng, sem, base, 0

    def __call__(self, ins):
        self.k += 1
        ins.then_inc(self.sem, 1)
        self.eng.wait_ge(self.sem, self.base + self.k)


def by_chunk(eng, *stages):
    with eng.Fori(0, NC // 2) as i:
        for stage in stages:
            for u in range(2):
                stage(i * 2, u)
    for stage in stages[:len(stages) * (NC % 2)]:
        stage(NC - 1, 0)


def by_four(eng, *stages):
    with eng.Fori(0, NC // 4) as i:
        for first in (0, 2):
            for stage in stages:
                for u in (first, first + 1):
                    stage(i * 4, u)
    for first in range(0, NC % 4, 2):
        for stage in stages:
            for u in range(first, min(first + 2, NC % 4)):
                stage(NC // 4 * 4, u)


def gnn_kernel(nc, x, src_t, dst_t, dst, W_heads, a_heads, gamma_h, beta_h, W_out, a_out, gamma_o, beta_o,
               W_res, b_res, Wl0, Wr0, b0, g0, be0, rm0, rv0, Wl1, Wr1, b1, g1, be1, rm1, rv1, out):
    ctx = ExitStack()
    with ctx:
        def sb(name, shape, dt=F32):
            return ctx.enter_context(nc.sbuf_tensor(name, shape, dt))

        def psb(name, shape):
            return ctx.enter_context(nc.psum_tensor(name, shape, F32))

        def part(buf, p, at, *dims):
            n = int(np.prod(dims))
            names = "abc"[:len(dims)]
            v = buf[0:p, at:at + n]
            if len(dims) == 1:
                return v
            return v.rearrange(f"p ({' '.join(names)}) -> p {' '.join(names)}", **dict(zip(names, dims)))

        def sem(name):
            return ctx.enter_context(nc.semaphore(name))

        def dram(name, shape, dt=F32):
            return nc.dram_tensor(name, shape, dt).ap()

        t_gat0 = dram("t_gat0", (N, ROW0))
        t_gat1 = dram("t_gat1", (N, ROW1))
        t_sage0 = dram("t_sage0", (N, D))
        t_sage1 = dram("t_sage1", (N, D))
        win0_d = dram("win0_d", (3, NW, K0), BF16)
        win1_d = dram("win1_d", (3, NW, K1), BF16)
        bnd0_d = dram("bnd0_d", (NP, NT * H))
        bnd1_d = dram("bnd1_d", (NP, NT))
        y1_d = dram("y1_d", (HP, D, N))
        base_d = dram("base_d", (NV, NPAIR), I32)
        baser_d = dram("baser_d", (NV, NPAIR), I32)

        acc = sb("acc", [128, H * SW])
        den = sb("den", [3 * H, NW])
        recT = den[:, :].bitcast(BF16)
        acc8 = acc[:, :].rearrange("p (h n) -> p h n", h=H)
        dstf = sb("dstf", [EP, ET], I16)
        dsti = acc[0:EP, 0:ET].bitcast(I32)
        basef = sb("basef", [EP, NV, NPAIR], I16)
        basei = acc[0:EP, 2048:2048 + NV * NPAIR].bitcast(I32)
        baser = sb("baser", [1, NV * NPAIR], I32)
        lohi = sb("lohi", [1, 2 * NS + NV], I32)
        rows = sb("rows", [EP, 2 * TH, ROW0])
        idx = sb("idx", [EP, 2 * TH], I32)
        adw = sb("adw", [3 * WIN, 2, PAIRS, K0], BF16)
        cur = sb("cur", [EP, PAIRS])
        rel = sb("rel", [EP, TH])
        oh = sb("oh", [EP, 2, TH, WIN])
        ohb = sb("ohb", [EP, 2, TH, 3 * WIN], BF16)
        oht = sb("oht", [3 * WIN, TH, EP], BF16)
        s_t = sb("s_t", [EP, TH, H])
        s_l = sb("s_l", [EP, TH, H])
        s_m = sb("s_m", [EP, TH, H])
        s_d = sb("s_d", [EP, TH, H])
        pen = sb("pen", [EP, TH])
        smax = sb("smax", [EP, TH, H])
        wgt = sb("wgt", [EP, 2, TH, H])
        rhs = sb("rhs", [EP, 2, TH, H * WIN])
        s1col = sb("s1col", [EP, 1])
        roff = sb("roff", [EP, 1])
        ident = sb("ident", [128, 128])
        identb = sb("identb", [128, 128], BF16)
        iota_w = sb("iota_w", [EP, WIN])
        ones = sb("ones", [128, CH])
        zeros = sb("zeros", [128, 128])
        sel = part(acc, 3 * H, 17800, HP, 128)
        selb = sb("selb", [3 * H, HP, 128], BF16)
        onesb = sb("onesb", [3, 128], BF16)
        rcnt = sb("rcnt", [NP, NT])
        w_sb = acc[:, 14400:14400 + H * DH].rearrange("p (h j) -> p h j", h=H)
        wz = sb("wz", [128, H, 128])
        a_bc = acc[:, 16384:16384 + 2 * H * DH].rearrange("p (h j) -> p h j", h=H)
        wa = sb("wa", [128, 2 * H])
        prod = acc[:, 0:HP * D]
        woa = sb("woa", [128, HP, D + 2])
        wob = part(acc, 128, 16768, HP, D + 2)
        ao_bc = acc[:, 17500:17500 + 2 * D].rearrange("p (r j) -> p r j", r=2)
        gh = sb("gh", [128, HP])
        bh = sb("bh", [128, HP])
        stats = acc[:, H * SW - HP * NC * 6:].rearrange("p (h c k) -> p h c k", h=HP, c=NC)
        mv = sb("mv", [128, HP, 2])
        scl = sb("scl", [128, HP])
        shf = sb("shf", [128, HP])
        go = sb("go", [128, 1])
        bo = sb("bo", [128, 1])
        brow = sb("brow", [1, D + 2])
        bres = sb("bres", [1, D])
        w_a = sb("w_a", [128, D])
        w_b = sb("w_b", [128, D])
        stg = sb("stg", [128, 2, CH])
        vrow = stg[:, :, :].rearrange("p u n -> p (u n)")[:, 0:5 * D].rearrange("p (i n) -> p i n", i=5)
        col1 = sb("col1", [128, 2 * H])
        amax = sb("amax", [128, H])
        a8 = sb("a8", [H, 1])
        t8 = sb("t8", [H, H])
        nsc = part(acc, NP, 0, NT, 2 * H)
        nwin = part(acc, NP, 2048, NT, K0)
        nlr = part(acc, NP, 4096, NT, H)
        nres = part(acc, NP, 5120, NT, K0)
        nw3 = acc[0:NP, 7168:7168 + NT * 3 * K0 // 2].bitcast(BF16).rearrange("p (t k) -> p t k", t=NT)
        pairs_i = acc[0:SB, 8192:8192 + 2 * TH * EP].bitcast(I32)
        pairs_f = acc[0:SB, 12288:12288 + 2 * TH * EP]
        gmin = sb("gmin", [SB, 2 * PAIRS])
        gmax = sb("gmax", [SB, 2 * PAIRS])
        tb_b, tb_r, tb_e, tb_bi, tb_ri = (part(acc, SB, 7168 + i * NV * 2 * PAIRS, NV, 2 * PAIRS) for i in range(5))
        tb_bi, tb_ri = (t.bitcast(I32) for t in (tb_bi, tb_ri))
        bmn = sb("bmn", [SB, 2])
        tch = sb("tch", [SB, 3])
        pidx = sb("pidx", [SB, 2])
        NCAND = 2 * NS + NV
        cand = sb("cand", [SB, NCAND])
        ccol = sb("ccol", [NCAND, 1])
        lh = sb("lh", [1, NCAND])
        xt = part(acc, NP, 12544, 4, TC, D)
        ht = part(acc, NP, 12544 + 4 * TC * D, 4, TC, D)
        zt = part(acc, NP, 12544 + 8 * TC * D, 2, TC, D)
        rowb = part(acc, NP, 12544 + 4 * TC * D, 2, TC, ROW0)
        xT = part(acc, 128, 17664, 2, CH)
        aT = part(acc, 128, 17664 + 2 * CH, 2, CH)
        y1 = part(acc, 128, 8192, 2, HP, CH)
        dslot = part(acc, H, 12544, 2, CH)
        bnode, dnode, rest = (part(acc, NP, at, NT * H) for at in (13600, 18488, 15700))
        rparts = acc[0:NP, 17288:17288 + NT * 3 * H // 2].bitcast(BF16).rearrange("p (t k) -> p t k", t=NT)
        rslot = acc[0:NP, 16600:16600 + TC * 3 * H].bitcast(BF16).rearrange("p (u t k) -> p u t k", u=2, t=TC)
        lnst = sb("lnst", [NP, 2, TC, 6])
        lnmv = sb("lnmv", [NP, 2, TC, 2])
        lnr = sb("lnr", [NP, 2, TC])
        lnb = sb("lnb", [NP, 2, TC])

        psa = psb("psa", [128, 4, 512])
        psc = psb("psc", [128, 4, 512])
        p_oht = psc[:, 0, :].bitcast(BF16).rearrange("p (t n) -> p t n", t=TH)
        p_turn = [psc[:, u, :].bitcast(BF16).rearrange("p (t n) -> p t n", t=2 * TC) for u in range(2)]
        p_adx = psc[:, 1, :]
        p_den = psc[:, 2, :]
        p_dens = (psc[:, 2, :], psc[:, 3, :])

        cst = sem("cst")
        cst_l = sem("cst_l")
        alone = sem("alone")
        phase = sem("phase")
        sp_in = sem("sp_in")
        sp_out = sem("sp_out")
        dve_l = sem("dve_l")
        cand_ready = sem("cand_ready")
        cand_t = sem("cand_t")
        lh_col = sem("lh_col")
        lh_row = sem("lh_row")
        tables = sem("tables")
        mx_part = sem("mx_part")
        mx_t = sem("mx_t")
        mx_diag = sem("mx_diag")
        mx_bc = sem("mx_bc")
        win_ready = sem("win_ready")
        sqrt_arg = sem("sqrt_arg")
        sqrt_done = sem("sqrt_done")
        bn_ready = sem("bn_ready")
        bias_ps = sem("bias_ps")
        idx_in = [sem(f"idx_in{i}") for i in range(2)]
        rows_in = [sem(f"rows_in{i}") for i in range(2)]
        adw_in = [sem(f"adw_in{i}") for i in range(2)]
        ohb_ready = sem("ohb_ready")
        oh_ready = sem("oh_ready")
        oht_ps = sem("oht_ps")
        oht_sb = sem("oht_sb")
        adx_ready = sem("adx_ready")
        exp_arg = sem("exp_arg")
        wgt_ready = sem("wgt_ready")
        den_ps = sem("den_ps")
        rhs_ready = sem("rhs_ready")
        sums_ps = sem("sums_ps")
        sums_used = sem("sums_used")
        dve_w = sem("dve_w")
        dve_r = sem("dve_r")
        fl_ps = sem("fl_ps")
        fl_sb = sem("fl_sb")
        fl_out = [sem(f"fl_out{i}") for i in range(2)]
        fl_free = sem("fl_free")
        den_clear = sem("den_clear")
        rng_done = sem("rng_done")

        def phase_sems(name, plain, primed=()):
            S = {k: sem(f"{name}_{k}") for k in tuple(plain) + tuple(primed)}
            S["primed"] = [S[k] for k in primed]
            return S

        n_x = phase_sems("n_x", ("in0", "in1", "in2", "in3", "xps", "row", "out0", "out1"), ("xsb", "mps", "msb", "stored"))
        n_bn = phase_sems("n_bn", ("in0", "in1", "bc"), ("row", "stat"))
        n_msg = phase_sems("n_msg", ("in0", "in1", "bc", "out0", "out1"), ("nrm", "mps", "row", "msb", "stored"))
        n_gn = phase_sems("n_gn", ("bc",), ("row",))
        n_den = [phase_sems(f"n_d{k}", ("cp", "dif", "ex", "parts", "rs"), ("ps", "dn", "tps", "rt")) for k in range(2)]
        n_den.append(phase_sems("n_d2", ("cp",), ("ps", "dn")))
        node_plain = ("in0", "in1", "in2", "in3", "xps", "acp", "row", "own_a", "out0", "out1")
        norm_plain = node_plain + ("var", "std", "norm", "own_b")
        n_fin = [phase_sems(f"n_f{k}", plain, ("xsb", "mps", "msb", "stored"))
                 for k, plain in enumerate((norm_plain, node_plain, norm_plain))]

        block = ctx.enter_context(nc.Block())
        ENGINES = 5

        def phase_end(eng, k):
            eng.drain().then_inc(phase, 1)
            eng.wait_ge(phase, ENGINES * k)

        def node_ranges(eng, spec, run, after=None):
            def rounds(s0, v, lo, hi):
                longest = eng.value_load(lohi[0:1, ds(v + 2 * NS, 1)], min_val=1, max_val=N)
                with eng.Fori(0, longest, WIN) as w0:
                    run(s0, v, lo, hi, w0)
            if spec["parts"]:
                with eng.Fori(0, NS) as s:
                    lo = eng.value_load(lohi[0:1, ds(s + NS, 1)], min_val=0, max_val=SB - 1)
                    hi = eng.value_load(lohi[0:1, ds(s, 1)], min_val=1, max_val=SB)
                    rounds(s * SN, s, lo, hi)
                    if after:
                        after(s)
            else:
                rounds(0, WHOLE, 0, SB)

        def halves(eng, lo, hi, nxt, front, main):
            front(lo, 0, True)
            with eng.Fori(lo, hi) as b:
                main(b, 0, lambda: front(b, 1, False))
                eng.reg_mov(nxt, b + 1)
                eng.reg_alu(nxt, nxt, SB - 1, ALU.min)
                ahead = eng.snap(nxt, min_val=0, max_val=SB - 1)
                main(b, 1, lambda: front(ahead, 0, False))

        MAX_ROUNDS = NS * (SN // WIN + 1) + 3 * (N // WIN + 1)
        MAX_BLOCKS = (SB + 1) * MAX_ROUNDS
        MAX_HALVES = 2 * MAX_BLOCKS

        def count(eng, reg, most):
            eng.reg_add(reg, reg, 1)
            return eng.snap(reg, min_val=1, max_val=most)

        def value(eng, reg, most=MAX_HALVES):
            return eng.snap(reg, min_val=1, max_val=most)

        G0 = dict(table=t_gat0, width=ROW0, heads=H, weighted=True, parts=True, window=win0_d, k=K0, cols=SN, count=True)
        G1 = dict(table=t_gat1, width=ROW1, heads=1, weighted=True, parts=False, window=win1_d, k=K1, cols=N, count=True)
        S0 = dict(table=t_sage0, width=D, heads=1, weighted=False, parts=False, cols=N, count=True)
        S1 = dict(table=t_sage1, width=D, heads=1, weighted=False, parts=False, cols=N, count=False)

        def acc_view(spec):
            return acc8 if spec["heads"] == H else acc[:, 0:NW].rearrange("p (h n) -> p h n", h=1)

        def sums(q, h):
            return psa[:, q, 0:h * WIN]

        NCHUNK = HP * NFC

        def rows_of(table, c):
            return table[ds(c * CH, CH), :].rearrange("(t p) w -> p t w", p=NP)

        def pool_pass(eng, spec, ni, nk, fst):
            def run(s0, v, lo, hi, w0):
                eng.reg_mov(fst, 1)
                with eng.Fori(lo, hi):
                    i = count(eng, ni, MAX_BLOCKS)
                    for half in range(2):
                        k = eng.snap(nk, min_val=0, max_val=MAX_HALVES)
                        eng.reg_add(nk, nk, 1)
                        eng.wait_ge(idx_in[half], i * 16)
                        for j in range(half * TH, half * TH + TH):
                            if j % 2 == 0:
                                eng.wait_ge(sums_ps, k * PAIRS + (j % TH // 2 + 1))
                                eng.sem_inc(alone, 1)
                            eng.indirect_dma_start(rows[:, j, 0:spec["width"]], None, spec["table"],
                                                   bass.IndirectOffsetOnAxis(ap=idx[:, j:j + 1], axis=0)
                                                   ).then_inc(rows_in[half], 16)
                    eng.reg_add(nk, nk, fst)
                    eng.reg_mov(fst, 0)
                eng.reg_add(ni, ni, 1)
            node_ranges(eng, spec, run)
            eng.reg_add(ni, ni, 1)

        def pool_store(eng, S, primed, src, table, width):
            def store(e, u):
                eng.wait_ge(S["row"], e + (u + 1 + primed))
                eng.dma_start(rows_of(table, e + u), src[:, u % 2, :, 0:width]).then_inc(S[f"out{u % 2}"], 16)

            def stored(e, u):
                eng.wait_ge(S[f"out{u % 2}"], e * 8 + 16 * (u // 2 + 1))
                eng.sem_inc(S["stored"], 1)
            by_four(eng, store, stored)

        @block.gpsimd
        def _(eng):
            ni, nk, fst = (eng.alloc_register(f"{n}_pool") for n in ("ni", "nk", "fst"))
            eng.reg_mov(ni, 0)
            eng.reg_mov(nk, 0)
            link = Links(eng, cst_l)
            eng.memset(ones[:, :], 1.0).then_inc(cst, 1)
            eng.memset(zeros[:, :], 0.0).then_inc(cst, 1)
            link(eng.memset(ident[:, :], 0.0))
            link(eng.memset(sel[:, :, :], 0.0))
            eng.affine_select(out=ident[:, :], in_=ident[:, :], compare_op=ALU.not_equal, fill=1.0, base=0,
                              pattern=[[-1, 128]], channel_multiplier=1).then_inc(cst, 1)
            for r in range(2):
                v = sel[:, :, r * DH:(r + 1) * DH]
                for k in range(3):
                    ins = eng.affine_select(out=v, in_=v, compare_op=ALU.not_equal, fill=1.0, base=-H * k - r,
                                            pattern=[[-2, HP], [0, DH]], channel_multiplier=1)
                    if k < 2:
                        link(ins)
                ins.then_inc(cst, 1)
            eng.iota(iota_w[:, :], pattern=[[1, WIN]], base=0, channel_multiplier=0,
                     allow_small_or_imprecise_dtypes=True).then_inc(cst, 1)
            eng.iota(pidx[:, 0:1], pattern=[[0, 1]], base=1, channel_multiplier=1,
                     allow_small_or_imprecise_dtypes=True).then_inc(cst, 1)
            eng.iota(pidx[:, 1:2], pattern=[[0, 1]], base=SB, channel_multiplier=-1,
                     allow_small_or_imprecise_dtypes=True).then_inc(cst, 1)
            eng.sem_inc(adx_ready, 2)
            eng.sem_inc(sums_ps, 2 * PAIRS)
            eng.sem_inc(sums_used, 2 * PAIRS)
            eng.sem_inc(rhs_ready, PAIRS)
            eng.sem_inc(den_ps, 1)
            eng.sem_inc(fl_sb, 2)
            eng.sem_inc(fl_free, 2)
            for S in (n_x, n_bn, n_msg, n_gn, *n_den, *n_fin):
                for s_ in S["primed"]:
                    eng.sem_inc(s_, 2)
            for S in (n_x, *n_fin):
                eng.sem_inc(S["msb"], 2)
            phase_end(eng, 1)
            pool_store(eng, n_x, 0, rowb, t_gat0, ROW0)
            phase_end(eng, 2)
            pool_pass(eng, G0, ni, nk, fst)
            phase_end(eng, 3)
            phase_end(eng, 4)
            pool_store(eng, n_msg, 2, rowb, t_gat1, ROW1)
            phase_end(eng, 5)
            pool_pass(eng, G1, ni, nk, fst)
            phase_end(eng, 6)
            phase_end(eng, 7)
            pool_store(eng, n_fin[0], 0, zt, t_sage0, D)
            phase_end(eng, 8)
            pool_pass(eng, S0, ni, nk, fst)
            phase_end(eng, 9)
            phase_end(eng, 10)
            pool_store(eng, n_fin[1], 0, zt, t_sage1, D)
            phase_end(eng, 11)
            pool_pass(eng, S1, ni, nk, fst)
            phase_end(eng, 12)
            phase_end(eng, 13)
            pool_store(eng, n_fin[2], 0, zt, out, D)
            phase_end(eng, 14)

        def sp_pass(eng, spec, regs, bases):
            nb, ni, nf, nxt = regs
            k = spec.get("k")

            def load_idx(half, block_):
                eng.dma_start(idx[:, half * TH:half * TH + TH],
                              src_t[:, ds(block_ * (2 * TH) + half * TH, TH)]).then_inc(idx_in[half], 16)

            def choose(out_, at, end, yes, no):
                eng.reg_mov(nxt[2], at)
                eng.reg_alu(nxt[2], nxt[2], end, ALU.min)
                eng.reg_mov(nxt[3], end)
                eng.reg_alu(nxt[3], nxt[3], nxt[2], ALU.subtract)
                eng.reg_alu(nxt[3], nxt[3], 1, ALU.min)
                eng.reg_mov(nxt[2], 1)
                eng.reg_alu(nxt[2], nxt[2], nxt[3], ALU.subtract)
                eng.reg_alu(nxt[2], nxt[2], no, ALU.mult)
                eng.reg_alu(nxt[3], nxt[3], yes, ALU.mult)
                eng.reg_mov(out_, nxt[2])
                eng.reg_add(out_, out_, nxt[3])

            def first_of_next(v, lo, w0):
                if not spec["parts"]:
                    return 0
                eng.reg_mov(nxt[4], v + 1)
                eng.reg_alu(nxt[4], nxt[4], NS - 1, ALU.min)
                after_s = eng.snap(nxt[4], min_val=0, max_val=NS - 1)
                next_lo = eng.value_load(lohi[0:1, ds(after_s + NS, 1)], min_val=0, max_val=SB - 1)
                longest = eng.value_load(lohi[0:1, ds(v + 2 * NS, 1)], min_val=1, max_val=N)
                choose(nxt[4], w0 + WIN, longest, lo, next_lo)
                return eng.snap(nxt[4], min_val=0, max_val=SB - 1)

            def run(s0, v, lo, hi, w0):
                def front(blk, half, first):
                    if not spec["weighted"]:
                        return
                    f = count(eng, nf, MAX_HALVES)
                    eng.load(bases, baser[0:1, ds(v * NPAIR + blk * (2 * PAIRS) + half * PAIRS, PAIRS)])
                    eng.wait_ge(adx_ready, f + 1 if first else f)
                    for q in range(PAIRS):
                        eng.reg_add(bases[q], bases[q], w0)
                        eng.reg_alu(bases[q], bases[q], spec["cols"], ALU.min)
                        at = eng.snap(bases[q], min_val=0, max_val=spec["cols"])
                        eng.dma_start(adw[:, half, q, 0:k], spec["window"][:, ds(at + s0, WIN), :]
                                      ).then_inc(adw_in[half], 16)

                def main(blk, half, next_front):
                    if half == 0:
                        count(eng, nb, MAX_BLOCKS)
                        eng.reg_add(ni, ni, 1)
                    next_front()
                    eng.reg_mov(nxt[1], blk + 1)
                    eng.reg_alu(nxt[1], nxt[1], SB - 1, ALU.min)
                    eng.wait_ge(rows_in[half], value(eng, nb) * (16 * TH))
                    load_idx(half, eng.snap(nxt[1], min_val=0, max_val=SB - 1))

                halves(eng, lo, hi, nxt[0], front, main)
                following = first_of_next(v, lo, w0)
                for half in range(2):
                    eng.wait_ge(idx_in[half], value(eng, ni) * 16)
                    load_idx(half, following)
                eng.reg_add(ni, ni, 1)

            def after(s):
                for i in range(NCHUNK):
                    p, ck, u = i % HP, i // HP, i % 2
                    eng.wait_ge(fl_sb, s * NCHUNK + (i + 1 + 2))
                    eng.dma_start(y1_d[p, :, ds(s * SN + ck * CH, CH)], stg[:, u, :]).then_inc(fl_out[u], 16)
                    for k in ([i - 1] if i else []) + ([i] if i == NCHUNK - 1 else []):
                        eng.wait_ge(fl_out[k % 2], s * (16 * NCHUNK // 2) + 16 * (k // 2 + 1))
                        eng.sem_inc(fl_free, 1)
            eng.reg_add(ni, ni, 1)
            first = eng.value_load(lohi[0:1, NS:NS + 1], min_val=0, max_val=SB - 1) if spec["parts"] else 0
            for half in range(2):
                load_idx(half, first)
            node_ranges(eng, spec, run, after)
            for half in range(2):
                eng.wait_ge(idx_in[half], value(eng, ni) * 16)
            eng.sem_inc(alone, 1)

        def sp_node(eng, S, first, second=None):
            def load(e, u):
                eng.wait_ge(S["msb"], e + (u + 1))
                eng.dma_start(xt[:, u, :, :], rows_of(first, e + u)).then_inc(S[f"in{u}"], 16)
                if second is not None:
                    eng.dma_start(ht[:, u, :, :], rows_of(second, e + u)).then_inc(S[f"in{u}"], 16)
            by_four(eng, load)

        def chunk(src, at):
            return src[:, :, ds(at, CH)].rearrange("c p n -> p c n")

        @block.sync
        def _(eng):
            regs = [eng.alloc_register(f"{n}_sp") for n in ("nb", "ni", "nf")]
            bases = [eng.alloc_register(f"base_sp{q}") for q in range(PAIRS)]
            for r in regs:
                eng.reg_mov(r, 0)
            regs.append([eng.alloc_register(f"nxt_sp{i}") for i in range(5)])
            n_in, n_out = [0], [0]

            def load(dst_, src_, **kw):
                eng.dma_start(dst_, src_, **kw).then_inc(sp_in, 16)
                n_in[0] += 1

            def store(dst_, src_):
                eng.dma_start(dst_, src_).then_inc(sp_out, 16)
                n_out[0] += 1

            def store_windows(table, k):
                for r in range(3):
                    store(table[r, 0:N, :].rearrange("(t p) c -> p t c", p=NP), nw3[:, :, r * k:(r + 1) * k])
                    store(table[r, N:NW, :], nw3[0:WIN, 0, r * k:(r + 1) * k])

            load(pairs_i, dst.rearrange("(p n) -> p n", p=SB))
            load(dsti, dst_t)
            load(w_sb[:, :, :], W_heads.rearrange("h k j -> k h j"))
            load(a_bc[:, :, :], a_heads.rearrange("(o h) j -> o h j", o=1).to_broadcast([128, H, 2 * DH]))
            load(woa[:, :, 0:D], W_out.rearrange("(c p) n -> p c n", p=128))
            load(ao_bc[:, :, :], a_out.rearrange("(o r j) -> o r j", o=1, r=2).to_broadcast([128, 2, D]))
            load(gh[:, :], gamma_h.rearrange("(c a) j -> (a j) c", a=2), allow_slow_non_contiguous=True)
            load(bh[:, :], beta_h.rearrange("(c a) j -> (a j) c", a=2), allow_slow_non_contiguous=True)
            load(go[:, :], gamma_o.rearrange("(p o) -> p o", o=1))
            load(bo[:, :], beta_o.rearrange("(p o) -> p o", o=1))
            load(bres[:, :], b_res.rearrange("(o n) -> o n", o=1))
            eng.wait_ge(tables, 1)
            store(base_d.rearrange("v (p q) -> p v q", p=SB), tb_bi[:, :, :])
            store(baser_d.rearrange("v (p q) -> p v q", p=SB), tb_ri[:, :, :])
            eng.wait_ge(sp_out, 16 * n_out[0])
            load(basei, base_d.rearrange("(o v) q -> o (v q)", o=1).to_broadcast([EP, NV * NPAIR]))
            load(baser[:, :], baser_d.rearrange("(o v) q -> o (v q)", o=1))
            eng.wait_ge(sp_in, 16 * n_in[0])
            phase_end(eng, 1)
            sp_node(eng, n_x, x)
            eng.wait_ge(win_ready, 1)
            store_windows(win0_d, K0)
            store(bnd0_d, bnode)
            eng.wait_ge(sp_out, 16 * n_out[0])
            phase_end(eng, 2)
            sp_pass(eng, G0, regs, bases)
            phase_end(eng, 3)
            load(bnode[:, :], bnd0_d)

            def load_chunk(e, u):
                eng.wait_ge(n_bn["stat"], e + (u + 1))
                eng.dma_start(y1[:, u, :, :], chunk(y1_d, (e + u) * CH)).then_inc(n_bn[f"in{u}"], 16)
            by_chunk(eng, load_chunk)
            eng.wait_ge(sp_in, 16 * n_in[0])
            phase_end(eng, 4)
            def load_again(e, u):
                eng.wait_ge(n_msg["mps"], e + (u + 1))
                eng.dma_start(y1[:, u, :, :], chunk(y1_d, (e + u) * CH)).then_inc(n_msg[f"in{u}"], 16)
            by_chunk(eng, load_again)
            eng.wait_ge(win_ready, 2)
            store_windows(win1_d, K1)
            store(bnd1_d, bnode[:, 0:NT])
            eng.wait_ge(sp_out, 16 * n_out[0])
            phase_end(eng, 5)
            sp_pass(eng, G1, regs, bases)
            phase_end(eng, 6)
            load(bnode[:, 0:NT], bnd1_d)
            load(w_a[:, :], W_res)
            eng.wait_ge(sp_in, 16 * n_in[0])
            phase_end(eng, 7)
            sp_node(eng, n_fin[0], x)
            phase_end(eng, 8)
            sp_pass(eng, S0, regs, bases)
            phase_end(eng, 9)

            def sage_weights(Wl, Wr, vectors):
                load(w_a[:, :], Wl)
                load(w_b[:, :], Wr)
                for i, vec in enumerate(vectors):
                    load(vrow[:, i, :], vec.rearrange("(o n) -> o n", o=1).to_broadcast([128, D]))
                eng.wait_ge(sp_in, 16 * n_in[0])
            sage_weights(Wl0, Wr0, (b0, g0, be0, rm0, rv0))
            phase_end(eng, 10)
            sp_node(eng, n_fin[1], t_sage0)
            phase_end(eng, 11)
            sp_pass(eng, S1, regs, bases)
            phase_end(eng, 12)
            sage_weights(Wl1, Wr1, (b1, g1, be1, rm1, rv1))
            phase_end(eng, 13)
            sp_node(eng, n_fin[2], t_sage0, t_sage1)
            phase_end(eng, 14)

        LOADS_1 = 16 * 11
        LOADS_T = 16 * 13
        LOADS_4 = LOADS_T + 16
        LOADS_7 = LOADS_4 + 16 * 2
        LOADS_10 = LOADS_7 + 16 * 7
        LOADS_13 = LOADS_10 + 16 * 7

        def act_pass(eng, spec, nf, nm, nxt):
            h = spec["heads"]

            def front(blk, half, first):
                f = count(eng, nf, MAX_HALVES)
                eng.wait_ge(oht_ps, f)
                eng.activation(oht[:, :, :], p_oht[0:3 * WIN, :, 0:EP], ACT.Copy).then_inc(oht_sb, 1)

            def main(blk, half, next_front):
                m = count(eng, nm, MAX_HALVES)
                eng.wait_ge(exp_arg, m)
                eng.activation(wgt[:, half, :, 0:h], s_d[:, :, 0:h], ACT.Exp).then_inc(wgt_ready, 1)
                next_front()

            def after(s):
                for i in range(NCHUNK):
                    u = i % 2
                    eng.wait_ge(fl_ps, s * NCHUNK + (i + 1))
                    eng.wait_ge(fl_free, s * NCHUNK + (i + 1))
                    eng.activation(stg[:, u, :], psa[:, u, 0:CH], ACT.Copy).then_inc(fl_sb, 1)
            node_ranges(eng, spec, lambda s0, v, lo, hi, w0: halves(eng, lo, hi, nxt, front, main), after)

        def act_clear(eng, h):
            eng.activation(den[0:h, :], zeros[0:h, 0:1].to_broadcast([h, NW]), ACT.Copy).then_inc(den_clear, 1)

        def act_den(eng, S, h):
            def copy(e, u):
                eng.wait_ge(S["ps"], e + (u + 1))
                eng.activation(dslot[0:h, u, :], den[0:h, ds((e + u) * CH, CH)], ACT.Copy).then_inc(S["cp"], 1)
            by_chunk(eng, copy)

        def act_reciprocals(eng, S, h):
            eng.wait_ge(S["dif"], 1)
            eng.activation(rest[:, 0:NT * h], rest[:, 0:NT * h], ACT.Exp, scale=-1.0).then_inc(S["ex"], 1)
            eng.wait_ge(S["parts"], 1)

            def chunk_parts(e, u):
                eng.wait_ge(S["tps"], e + (u + 1))
                eng.activation(rslot[:, u, :, 0:3 * h], rparts[:, ds((e + u) * TC, TC), 0:3 * h],
                               ACT.Copy).then_inc(S["rs"], 1)

            def turned(e, u):
                eng.wait_ge(S["tps"], e + (u + 3))
                eng.activation(recT[0:3 * h, ds((e + u) * CH, CH)].rearrange("p (t n) -> p t n", t=TC),
                               p_turn[u][0:3 * h, 0:TC, 0:NP], ACT.Copy).then_inc(S["rt"], 1)
            by_chunk(eng, chunk_parts, turned)

        def act_node(eng, S, affine, norm):
            def copies(e, u):
                eng.wait_ge(S["mps"], e + (u + 1))
                cols = acc[:, ds((e + u) * CH, CH)]
                if affine:
                    ins = eng.activation(aT[:, u % 2, :], cols, ACT.Identity, bias=shf[:, 0:1], scale=scl[:, 0:1])
                else:
                    ins = eng.activation(aT[:, u % 2, :], cols, ACT.Copy)
                ins.then_inc(S["acp"], 1)
                eng.wait_ge(S["xps"], e + (u + 1))
                eng.activation(xT[:, u % 2, :], psc[:, u % 2, 0:CH], ACT.Copy).then_inc(S["xsb"], 1)

            def deviation(e, u):
                eng.wait_ge(S["var"], e + (u + 1))
                eng.activation(lnr[:, u % 2, :], lnr[:, u % 2, :], ACT.Sqrt).then_inc(S["std"], 1)

            def finish(e, u):
                eng.wait_ge(S["norm"], e + (u + 1))
                for t in range(TC):
                    z = zt[:, u % 2, t, :]
                    last = eng.activation(z, z, ACT.Identity, bias=lnb[:, u % 2, t:t + 1], scale=lnr[:, u % 2, t:t + 1])
                last.then_inc(S["row"], 1)

            def pair(stages, e, chunks):
                for stage in stages:
                    for u in chunks:
                        stage(e, u)
            if not norm:
                by_four(eng, copies)
                return
            pair([copies], 0, (0, 1))
            with eng.Fori(0, NC // 2 - 1) as i:
                pair([copies], i * 2, (2, 3))
                pair([deviation, finish], i * 2, (0, 1))
            pair([copies], NC - 1, range(NC % 2))
            pair([deviation, finish], NC // 2 * 2 - 2, (0, 1))
            pair([deviation, finish], NC - 1, range(NC % 2))

        def act_sqrt(eng, ap, k):
            eng.wait_ge(sqrt_arg, k)
            eng.activation(ap, ap, ACT.Sqrt).then_inc(sqrt_done, 1)

        @block.scalar
        def _(eng):
            nf, nm, nxt = (eng.alloc_register(f"{n}_act") for n in ("nf", "nm", "nxt"))
            eng.reg_mov(nf, 0)
            eng.reg_mov(nm, 0)
            eng.wait_ge(cst, 8)
            eng.activation(identb[:, :], ident[:, :], ACT.Copy)
            eng.activation(selb[:, :, :], sel[:, :, :], ACT.Copy)
            eng.activation(onesb[:, :], ones[0:3, 0:128], ACT.Copy)
            phase_end(eng, 1)
            S = n_x

            def copy_x(e, u):
                eng.wait_ge(S["mps"], e + (u + 1))
                eng.wait_ge(S["xps"], e + (u + 1))
                eng.activation(xT[:, u % 2, :], psc[:, u % 2, 0:CH], ACT.Copy).then_inc(S["xsb"], 1)

            by_four(eng, copy_x)
            phase_end(eng, 2)
            act_clear(eng, H)
            act_pass(eng, G0, nf, nm, nxt)
            phase_end(eng, 3)
            act_den(eng, n_den[0], H)
            act_reciprocals(eng, n_den[0], H)
            act_sqrt(eng, scl[:, :], 1)
            phase_end(eng, 4)
            S = n_msg

            def copy_rows(e, u):
                eng.wait_ge(S["mps"], e + (u + 3))
                eng.wait_ge(S["stored"], e + (u + 1))
                products = psa[0:NP, 2 * u:2 * u + 2, 0:2 * (D + 2)].rearrange("p a (b k) -> p a b k", b=2)
                eng.activation(nsc[:, ds((e + u) * TC, TC), 0:2].rearrange("p (a b) k -> p a b k", a=2),
                               products[:, :, :, D:D + 2], ACT.Copy).then_inc(S["msb"], 1)
                eng.activation(rowb[:, u, :, 0:D + 1].rearrange("p (a b) k -> p a b k", a=2),
                               products[:, :, :, 0:D + 1], ACT.Copy).then_inc(S["row"], 1)
            by_chunk(eng, copy_rows)
            phase_end(eng, 5)
            act_clear(eng, 1)
            act_pass(eng, G1, nf, nm, nxt)
            phase_end(eng, 6)
            act_den(eng, n_den[1], 1)
            act_reciprocals(eng, n_den[1], 1)
            act_sqrt(eng, scl[:, 0:1], 2)
            phase_end(eng, 7)
            act_node(eng, n_fin[0], True, True)
            phase_end(eng, 8)
            act_clear(eng, 1)
            phase_end(eng, 9)
            act_den(eng, n_den[2], 1)
            act_sqrt(eng, vrow[:, 4, :], 3)
            phase_end(eng, 10)
            act_node(eng, n_fin[1], False, False)
            phase_end(eng, 11)
            phase_end(eng, 12)
            act_sqrt(eng, vrow[:, 4, :], 4)
            phase_end(eng, 13)
            act_node(eng, n_fin[2], False, True)
            phase_end(eng, 14)

        nwins = []

        def pe_pass(eng, spec, regs):
            nb, nf, nm, nk, nxt = regs
            h, k = spec["heads"], spec.get("k")

            def front(blk, half, first):
                count(eng, nf, MAX_HALVES)
                if not spec["weighted"]:
                    return
                eng.wait_ge(ohb_ready, value(eng, nf))
                for j in range(TH):
                    last = eng.transpose(p_oht[0:3 * WIN, j, 0:EP], ohb[:, half, j, :], identb[0:EP, 0:EP])
                last.then_inc(oht_ps, 1)
                if first:
                    scores(half)

            def scores(half):
                f = value(eng, nf)
                eng.wait_ge(oht_sb, f)
                count(eng, nwins[half], MAX_HALVES)
                eng.wait_ge(adw_in[half], value(eng, nwins[half]) * (16 * PAIRS))
                for j in range(TH):
                    last = eng.matmul(p_adx[0:EP, j * k:(j + 1) * k], oht[:, j, :], adw[:, half, j // 2, 0:k],
                                      start=True, stop=True)
                last.then_inc(adx_ready, 1)

            def main(blk, half, next_front):
                if half == 0:
                    count(eng, nb, MAX_BLOCKS)
                m = count(eng, nm, MAX_HALVES)
                kk = count(eng, nk, MAX_HALVES)
                if spec["weighted"]:
                    eng.wait_ge(wgt_ready, m)
                else:
                    eng.wait_ge(oh_ready, value(eng, nf))
                    eng.wait_ge(rows_in[half], value(eng, nb) * (16 * TH))
                if spec["count"]:
                    for j in range(TH):
                        left = wgt[:, half, j, 0:h] if spec["weighted"] else ones[0:EP, 0:1]
                        last = eng.matmul(p_dens[half][0:h, (j // 2) * WIN:(j // 2 + 1) * WIN], left,
                                          oh[:, half, j, :], start=(j % 2 == 0), stop=(j % 2 == 1))
                    if spec["weighted"]:
                        last.then_inc(den_ps, 1)
                next_front()
                for q in range(PAIRS):
                    if q == PAIRS // 2 and spec["weighted"]:
                        scores(1 - half)
                    if spec["weighted"]:
                        eng.wait_ge(rhs_ready, m * PAIRS + (q + 1))
                    eng.wait_ge(sums_used, kk * PAIRS + (q + 1))
                    for j in (2 * q, 2 * q + 1):
                        right = rhs[:, half, j, 0:h * WIN] if spec["weighted"] else oh[:, half, j, :]
                        last = eng.matmul(sums(q, h), rows[:, half * TH + j, 0:D], right,
                                          start=(j == 2 * q), stop=(j == 2 * q + 1))
                    last.then_inc(sums_ps, 1)

            def after(s):
                eng.wait_ge(rng_done, s + 1)
                for i in range(NCHUNK):
                    p, ck, u = i % HP, i // HP, i % 2
                    eng.wait_ge(fl_sb, s * NCHUNK + (i + 1))
                    for r in range(2):
                        last = eng.matmul(psa[:, u, 0:CH], wz[:, 2 * p + r, :],
                                          acc8[:, 2 * p + r, ck * CH:(ck + 1) * CH], start=(r == 0), stop=(r == 1))
                    last.then_inc(fl_ps, 1)
                eng.wait_ge(fl_sb, (s + 1) * NCHUNK + 2)

            def run(s0, v, lo, hi, w0):
                kk = count(eng, nk, MAX_HALVES)
                eng.wait_ge(sums_used, kk * PAIRS + PAIRS)
                if spec["count"]:
                    eng.matmul(p_dens[1][0:h, 0:PAIRS * WIN], zeros[:, 0:h], ones[:, 0:PAIRS * WIN],
                               start=True, stop=True)
                for q in range(PAIRS):
                    eng.matmul(sums(q, h), zeros[:, :], ones[:, 0:h * WIN], start=True, stop=True).then_inc(sums_ps, 1)
                halves(eng, lo, hi, nxt, front, main)
            node_ranges(eng, spec, run, after)

        def pe_max(eng, h, k, parts):
            eng.wait_ge(mx_part, k)
            eng.transpose(p_den[0:h, 0:parts], col1[0:parts, 0:h], ident[0:parts, 0:parts]).then_inc(mx_t, 1)
            eng.wait_ge(mx_diag, k)
            eng.matmul(p_adx[:, 0:h], ones[0:h, 0:128], t8[0:h, 0:h], start=True, stop=True).then_inc(mx_bc, 1)

        def pe_den(eng, S, h):
            def turn(e, u):
                eng.wait_ge(S["dn"], e + (u + 1))
                eng.wait_ge(S["cp"], e + (u + 1))
                eng.sem_inc(alone, 1)
                for t in range(TC):
                    last = eng.transpose(psa[0:NP, u, t * h:(t + 1) * h], dslot[0:h, u, t * NP:(t + 1) * NP],
                                         ident[0:h, 0:h])
                last.then_inc(S["ps"], 1)
            by_chunk(eng, turn)

        def pe_reciprocals(eng, S, h):
            def turn(e, u):
                eng.wait_ge(S["rt"], e + (u + 1))
                eng.wait_ge(S["rs"], e + (u + 1))
                for t in range(TC):
                    last = eng.transpose(p_turn[u][0:3 * h, t, 0:NP], rslot[:, u, t, 0:3 * h], identb[0:NP, 0:NP])
                last.then_inc(S["tps"], 1)
            by_chunk(eng, turn)
            eng.wait_ge(S["rt"], NC + 2)
            eng.sem_inc(alone, 1)

        def pe_transpose(eng, S, tile, loads):
            def stage(e, u):
                eng.wait_ge(S[f"in{u}"], e * (4 * loads) + 16 * loads)
                eng.wait_ge(S["xsb"], e + (u + 1))
                for t in range(TC):
                    last = eng.transpose(psc[:, u % 2, t * NP:(t + 1) * NP], tile[:, u, t, :], ident[0:NP, 0:NP])
                last.then_inc(S["xps"], 1)
            return stage

        def pe_node(eng, S, tile, loads, left_w, right_w, bias, split):
            def products(e, u):
                eng.wait_ge(S["msb"], e + (u + 3))
                eng.wait_ge(S["acp"], e + (u + 1))
                eng.wait_ge(S["xsb"], e + (u + 3))
                for t in range(TC):
                    o = psa[0:NP, u % 2, t * D:(t + 1) * D]
                    cols = slice(t * NP, (t + 1) * NP)
                    left_o = psa[0:NP, 2 + u % 2, t * D:(t + 1) * D] if split else o
                    eng.matmul(left_o, aT[:, u % 2, cols], left_w, start=True, stop=split)
                    eng.matmul(o, xT[:, u % 2, cols], right_w, start=split, stop=False)
                    last = eng.matmul(o, ones[0:1, 0:NP], bias, start=False, stop=True)
                last.then_inc(S["mps"], 1)
            by_four(eng, pe_transpose(eng, S, tile, loads), products)

        @block.tensor
        def _(eng):
            regs = [eng.alloc_register(f"{n}_pe") for n in ("nb", "nf", "nm", "nk", "nxt")]
            nwins.extend(eng.alloc_register(f"nwin{i}_pe") for i in range(2))
            for r in regs + nwins:
                eng.reg_mov(r, 0)
            eng.wait_ge(cst, 8)
            eng.wait_ge(cand_ready, 1)
            eng.transpose(p_den[0:NCAND, 0:SB], cand[:, :], ident[0:SB, 0:SB]).then_inc(cand_t, 1)
            eng.wait_ge(lh_col, 1)
            eng.matmul(p_adx[0:1, 0:NCAND], ccol[:, 0:1], ident[0:NCAND, 0:NCAND], start=True, stop=True).then_inc(lh_row, 1)
            phase_end(eng, 1)
            S = n_x

            def node_scores(e, u):
                eng.wait_ge(S["msb"], e + (u + 3))
                eng.wait_ge(S["xsb"], e + (u + 3))
                for t in range(TC):
                    last = eng.matmul(psa[0:NP, u % 2, t * 2 * H:(t + 1) * 2 * H], xT[:, u % 2, t * NP:(t + 1) * NP],
                                      wa[:, :], start=True, stop=True)
                last.then_inc(S["mps"], 1)
            by_four(eng, pe_transpose(eng, S, xt, 1), node_scores)
            eng.wait_ge(S["xsb"], NC + 2)
            pe_max(eng, H, 1, NP)
            phase_end(eng, 2)
            pe_pass(eng, G0, regs)
            phase_end(eng, 3)
            pe_max(eng, H, 2, EP)
            pe_den(eng, n_den[0], H)
            pe_reciprocals(eng, n_den[0], H)

            def spread_chunk(banks, e, u):
                for p in range(HP):
                    last = eng.matmul(banks[:, p, 0:CH], selb[:, p, :], recT[:, ds((e + u) * CH, CH)],
                                      start=True, stop=True)
                return last

            def spread_heads(e, u):
                eng.wait_ge(n_bn["row"], e + (u + 1))
                spread_chunk((psa, psc)[u], e, u).then_inc(n_bn["bc"], 1)
            by_chunk(eng, spread_heads)
            eng.wait_ge(bn_ready, 1)
            for p in range(HP):
                last = eng.matmul(p_den[0:1, 0:D + 2], shf[:, p:p + 1], woa[:, p, :], start=(p == 0), stop=(p == HP - 1))
            last.then_inc(bias_ps, 1)
            phase_end(eng, 4)
            S = n_msg

            def spread_again(e, u):
                eng.wait_ge(S["nrm"], e + (u + 2))
                spread_chunk(psc, e, u).then_inc(S["bc"], 1)

            def messages(e, u):
                eng.wait_ge(S["nrm"], e + (u + 3))
                eng.wait_ge(S["row"], e + (u + 1))
                for t in range(TC):
                    o = psa[0:NP, 2 * u + t // 2, (t % 2) * (D + 2):(t % 2 + 1) * (D + 2)]
                    for p in range(HP):
                        eng.matmul(o, y1[:, u, p, t * NP:(t + 1) * NP], wob[:, p, :], start=(p == 0), stop=False)
                    last = eng.matmul(o, ones[0:1, 0:NP], brow[:, :], start=False, stop=True)
                last.then_inc(S["mps"], 1)
            by_chunk(eng, spread_again, messages)
            pe_max(eng, 1, 3, NP)
            phase_end(eng, 5)
            pe_pass(eng, G1, regs)
            phase_end(eng, 6)
            pe_max(eng, 1, 4, EP)
            pe_den(eng, n_den[1], 1)
            pe_reciprocals(eng, n_den[1], 1)

            def spread_row(e, u):
                eng.wait_ge(n_gn["row"], e + (u + 1))
                eng.matmul(psa[:, u, 0:CH], onesb[:, :], recT[0:3, ds((e + u) * CH, CH)],
                           start=True, stop=True).then_inc(n_gn["bc"], 1)
            by_chunk(eng, spread_row)
            phase_end(eng, 7)
            pe_node(eng, n_fin[0], xt, 1, ident[:, :], w_a[:, :], bres[:, :], False)
            phase_end(eng, 8)
            pe_pass(eng, S0, regs)
            phase_end(eng, 9)
            pe_den(eng, n_den[2], 1)
            phase_end(eng, 10)
            pe_node(eng, n_fin[1], xt, 1, w_a[:, :], w_b[:, :], brow[:, 0:D], True)
            phase_end(eng, 11)
            pe_pass(eng, S1, regs)
            phase_end(eng, 12)
            phase_end(eng, 13)
            pe_node(eng, n_fin[2], ht, 2, w_a[:, :], w_b[:, :], brow[:, 0:D], True)
            phase_end(eng, 14)

        class DynLinks:

            def __init__(self, eng, sem_, reg):
                self.eng, self.sem, self.reg, self.k = eng, sem_, reg, 0
                self.base = eng.snap(reg, min_val=0, max_val=16 * MAX_HALVES)

            def __call__(self, ins):
                self.k += 1
                ins.then_inc(self.sem, 1)
                self.eng.wait_ge(self.sem, self.base + self.k)

            def end(self):
                self.eng.reg_add(self.reg, self.reg, self.k)

        def dve_pass(eng, spec, regs, bases):
            nb, nf, nm, nk, nxt, nl = regs
            h, acc_v, weighted = spec["heads"], acc_view(spec), spec["weighted"]
            basef_v = basef[:, :, :].rearrange("p v q -> p (v q)")

            def pairs(ap):
                return ap.rearrange("p (q i) -> p q i", i=2)

            def run(s0, v, lo, hi, w0):
                def base_at(blk, half):
                    return ds(v * NPAIR + blk * (2 * PAIRS) + half * PAIRS, PAIRS)

                def front(blk, half, first):
                    f = count(eng, nf, MAX_HALVES)
                    link = DynLinks(eng, dve_w, nl)
                    if first and weighted:
                        eng.wait_ge(adx_ready, f + 1)
                    link(eng.tensor_scalar(cur[:, :], basef_v[:, base_at(blk, half)], roff[:, 0:1], s1col[:, 0:1],
                                           ALU.add, ALU.min))
                    link(eng.tensor_tensor(pairs(rel[:, :]), pairs(dstf[:, ds(blk * (2 * TH) + half * TH, TH)]),
                                           cur[:, :].unsqueeze(2).to_broadcast([EP, PAIRS, 2]), ALU.subtract))
                    if weighted:
                        eng.tensor_tensor(ohb[:, half, :, :].rearrange("p t (r n) -> p t r n", r=3),
                                          iota_w[:, :].unsqueeze(1).unsqueeze(1).to_broadcast([EP, TH, 3, WIN]),
                                          rel[:, :].unsqueeze(2).unsqueeze(2).to_broadcast([EP, TH, 3, WIN]),
                                          ALU.is_equal).then_inc(ohb_ready, 1)
                    eng.tensor_tensor(oh[:, half, :, :], iota_w[:, :].unsqueeze(1).to_broadcast([EP, TH, WIN]),
                                      rel[:, :].unsqueeze(2).to_broadcast([EP, TH, WIN]),
                                      ALU.is_equal).then_inc(oh_ready, 1)
                    link.end()

                def main(blk, half, next_front):
                    if half == 0:
                        count(eng, nb, MAX_BLOCKS)
                    m = count(eng, nm, MAX_HALVES)
                    if weighted:
                        link = DynLinks(eng, dve_w, nl)
                        eng.wait_ge(adx_ready, value(eng, nf) + 2)
                        eng.wait_ge(rows_in[half], value(eng, nb) * (16 * TH))
                        adx = p_adx[0:EP, 0:TH * (2 * h + 1)].rearrange("p (t k) -> p t k", t=TH)
                        t_, l_, m_, d_ = (a[:, :, 0:h] for a in (s_t, s_l, s_m, s_d))
                        eng.tensor_scalar(pen[:, :], adx[:, :, 2 * h], -1.0, BIG, ALU.add, ALU.mult)
                        link(eng.tensor_tensor(t_, rows[:, half * TH:half * TH + TH, D:D + h], adx[:, :, 0:h], ALU.add))
                        link(eng.scalar_tensor_tensor(l_, t_, SLOPE, t_, ALU.mult, ALU.max))
                        link(eng.tensor_tensor(m_, l_, pen[:, :].unsqueeze(2).to_broadcast([EP, TH, h]), ALU.add))
                        eng.tensor_tensor(d_, m_, adx[:, :, h:2 * h], ALU.subtract).then_inc(exp_arg, 1)
                        link(eng.tensor_tensor(smax[:, :, 0:h], smax[:, :, 0:h], m_, ALU.max))
                        link.end()
                    if not weighted:
                        add_sums(1 - half)
                        next_front()
                        set_bases(blk, half)
                        return
                    if spec["count"]:
                        eng.wait_ge(den_ps, m)
                        eng.sem_inc(alone, 1)
                    next_front()

                    def weighted_onehots(q):
                        if q == 0:
                            eng.wait_ge(wgt_ready, m)
                        two = slice(2 * q, 2 * q + 2)
                        eng.tensor_tensor(rhs[:, half, two, 0:h * WIN].rearrange("p t (h j) -> p t h j", h=h),
                                          oh[:, half, two, :].unsqueeze(2).to_broadcast([EP, 2, h, WIN]),
                                          wgt[:, half, two, 0:h].unsqueeze(3).to_broadcast([EP, 2, h, WIN]),
                                          ALU.mult).then_inc(rhs_ready, 1)
                    add_sums(1 - half, weighted_onehots)
                    set_bases(blk, half)

                def set_bases(blk, half):
                    eng.load(bases, baser[0:1, base_at(blk, half)])
                    for q in range(PAIRS):
                        eng.reg_add(bases[q], bases[q], w0)
                        eng.reg_alu(bases[q], bases[q], spec["cols"], ALU.min)

                def add_sums(half, before=None):
                    kk = count(eng, nk, MAX_HALVES)
                    link = DynLinks(eng, dve_w, nl)
                    for q in range(PAIRS):
                        if before:
                            before(q)
                        at = eng.snap(bases[q], min_val=0, max_val=spec["cols"])
                        a = acc_v[:, :, ds(at, WIN)]
                        eng.wait_ge(sums_ps, kk * PAIRS + (q + 1 + PAIRS))
                        if spec["count"]:
                            dn = den[0:h, ds(at + s0, WIN)]
                            eng.tensor_tensor(dn, dn, p_dens[half][0:h, q * WIN:(q + 1) * WIN],
                                              ALU.add).then_inc(dve_w, 1)
                            link.k += 1
                        link(eng.tensor_tensor(a, a, sums(q, h).rearrange("p (h j) -> p h j", h=h), ALU.add))
                        eng.sem_inc(sums_used, 1)
                    link.end()

                for q in range(PAIRS):
                    eng.reg_mov(bases[q], spec["cols"])
                halves(eng, lo, hi, nxt, front, main)
                add_sums(1)
                link = DynLinks(eng, dve_w, nl)
                link(eng.tensor_scalar(roff[:, :], roff[:, :], float(WIN), None, ALU.add))
                link.end()

            def after(s):
                link = Links(eng, dve_r, s * (NCHUNK + 3))
                link(eng.tensor_scalar(s1col[:, :], s1col[:, :], float(SN), None, ALU.add))
                link(eng.memset(roff[:, :], 0.0))
                eng.sem_inc(rng_done, 1)
                for i in range(NCHUNK):
                    p, ck = i % HP, i // HP
                    eng.wait_ge(fl_ps, s * NCHUNK + (i + 1))
                    end = SW if ck == NFC - 1 else (ck + 1) * CH
                    link(eng.memset(acc8[:, 2 * p:2 * p + 2, ck * CH:end], 0.0))
                link(eng.tensor_scalar(den[0:H, ds(s * SN + SN, WIN)], ones[0:H, 0:WIN], 0.0, None, ALU.mult))
                eng.sem_inc(alone, 1)
            node_ranges(eng, spec, run, after)

        @block.vector
        def _(eng):
            regs = [eng.alloc_register(f"{n}_dve") for n in ("nb", "nf", "nm", "nk", "nxt", "nl")]
            bases = [eng.alloc_register(f"base_dve{q}") for q in range(PAIRS)]
            for r in regs:
                eng.reg_mov(r, 0)
            link = Links(eng, dve_l)
            ts, tt = eng.tensor_scalar, eng.tensor_tensor

            def dve_max(h, src, k, parts):
                eng.tensor_reduce(col1[0:parts, 0:h], src.rearrange("p m h -> p h m"), axis=AX, op=ALU.max).then_inc(mx_part, 1)
                eng.wait_ge(mx_t, k)
                link(eng.tensor_reduce(a8[0:h, :], p_den[0:h, 0:parts], axis=AX, op=ALU.max))
                ts(t8[0:h, 0:h], ident[0:h, 0:h], a8[0:h, 0:1], None, ALU.mult).then_inc(mx_diag, 1)
                eng.wait_ge(mx_bc, k)
                link(eng.tensor_copy(amax[:, 0:h], p_adx[:, 0:h]))

            def window_rows(h):
                sc, k = nsc[:, :, h:2 * h], 2 * h + 1
                link(tt(nlr[:, :, 0:h], sc, amax[0:NP, 0:h].unsqueeze(1).to_broadcast([NP, NT, h]), ALU.add))
                link(eng.scalar_tensor_tensor(nwin[:, :, h:2 * h], nlr[:, :, 0:h], SLOPE, nlr[:, :, 0:h], ALU.mult, ALU.max))
                link(eng.tensor_copy(nwin[:, :, 0:h], sc))
                link(eng.tensor_copy(bnode[:, 0:NT * h].rearrange("p (t h) -> p t h", h=h), nwin[:, :, h:2 * h]))
                link(eng.memset(nwin[:, :, 2 * h:2 * h + 1], 1.0))
                rest = nwin[:, :, 0:k]
                for r in range(3):
                    link(eng.tensor_copy(nw3[:, :, r * k:(r + 1) * k], rest))
                    if r < 2:
                        link(tt(nres[:, :, 0:k], rest, nw3[:, :, r * k:(r + 1) * k], ALU.subtract))
                        rest = nres[:, :, 0:k]
                eng.sem_inc(win_ready, 1)

            def clear_sums(columns, k=None):
                link(eng.memset(acc[:, 0:columns], 0.0))
                if k:
                    eng.wait_ge(den_clear, k)
                    eng.sem_inc(alone, 1)

            eng.wait_ge(cst, 8)
            eng.wait_ge(sp_in, LOADS_1)
            link(eng.tensor_copy(dstf[:, :], dsti))
            link(eng.tensor_copy(pairs_f, pairs_i))
            by_pair = pairs_f.rearrange("p (q n) -> p q n", n=2 * EP)
            link(eng.tensor_reduce(gmin[:, :], by_pair, axis=AX, op=ALU.min))
            link(eng.tensor_reduce(gmax[:, :], by_pair, axis=AX, op=ALU.max))
            for v in range(NV):
                s0, s1 = (0, N) if v == WHOLE else (v * SN, (v + 1) * SN)
                link(ts(tb_b[:, v, :], gmin[:, :], float(s0), float(s1), ALU.max, ALU.min))
                link(ts(tb_r[:, v, :], tb_b[:, v, :], float(-s0), None, ALU.add))
                link(ts(tb_e[:, v, :], gmax[:, :], float(s1 - 1), None, ALU.min))
                link(tt(tb_e[:, v, :], tb_e[:, v, :], tb_b[:, v, :], ALU.subtract))
                link(eng.tensor_reduce(cand[:, 2 * NS + v:2 * NS + v + 1], tb_e[:, v, :], axis=AX, op=ALU.max))
            link(eng.tensor_copy(tb_bi[:, :, :], tb_b[:, :, :]))
            link(eng.tensor_copy(tb_ri[:, :, :], tb_r[:, :, :]))
            eng.sem_inc(tables, 1)
            link(eng.tensor_reduce(bmn[:, 0:1], gmin[:, :], axis=AX, op=ALU.min))
            link(eng.tensor_reduce(bmn[:, 1:2], gmax[:, :], axis=AX, op=ALU.max))
            for s in range(NS):
                link(ts(tch[:, 0:1], bmn[:, 1:2], float(s * SN), None, ALU.is_ge))
                link(ts(tch[:, 1:2], bmn[:, 0:1], float((s + 1) * SN), None, ALU.is_lt))
                link(tt(tch[:, 2:3], tch[:, 0:1], tch[:, 1:2], ALU.mult))
                for i in range(2):
                    link(tt(cand[:, i * NS + s:i * NS + s + 1], tch[:, 2:3], pidx[:, i:i + 1], ALU.mult))
            eng.sem_inc(cand_ready, 1)
            eng.wait_ge(cand_t, 1)
            eng.tensor_reduce(ccol[:, :], p_den[0:NCAND, 0:SB], axis=AX, op=ALU.max).then_inc(lh_col, 1)
            eng.wait_ge(lh_row, 1)
            link(eng.tensor_copy(lh[:, :], p_adx[0:1, 0:NCAND]))
            lo = lh[:, NS:2 * NS]
            link(ts(lo, lo, -1.0, float(SB), ALU.mult, ALU.add))
            link(ts(lo, lo, float(SB - 1), None, ALU.min))
            link(eng.scalar_tensor_tensor(lh[:, 0:NS], lo, 1.0, lh[:, 0:NS], ALU.add, ALU.max))
            link(ts(lh[:, 2 * NS:], lh[:, 2 * NS:], 1.0, 1.0, ALU.add, ALU.max))
            link(eng.tensor_copy(lohi[:, :], lh[:, :]))
            link(eng.memset(wz[:, :, :], 0.0))
            for r in range(2):
                link(eng.tensor_copy(wz[:, :, :].rearrange("p (c a) n -> p c a n", a=2)[:, :, r, r * DH:(r + 1) * DH],
                                     w_sb[:, :, :].rearrange("p (c a) n -> p c a n", a=2)[:, :, r, :]))
                pv = prod.rearrange("p (h j) -> p h j", h=H)
                link(tt(pv, w_sb[:, :, :], a_bc[:, :, r * DH:(r + 1) * DH], ALU.mult))
                link(eng.tensor_reduce(wa[:, r * H:(r + 1) * H], pv, axis=AX, op=ALU.add))
            for r in range(2):
                pv = prod.rearrange("p (c j) -> p c j", c=HP)
                link(tt(pv, woa[:, :, 0:D], ao_bc[:, r, :].unsqueeze(1).to_broadcast([128, HP, D]), ALU.mult))
                link(eng.tensor_reduce(woa[:, :, D + r], pv, axis=AX, op=ALU.add))
            link(eng.memset(smax[:, :, :], -BIG))
            link(eng.memset(s1col[:, :], float(SN)))
            link(eng.memset(roff[:, :], 0.0))
            eng.wait_ge(sp_in, LOADS_T)
            link(eng.tensor_copy(basef[:, :, :].rearrange("p v q -> p (v q)"), basei))
            phase_end(eng, 1)
            S = n_x

            def score_rows(e, u):
                eng.wait_ge(S[f"in{u}"], e * 4 + 16)
                eng.wait_ge(S["stored"], e + (u + 1))
                eng.tensor_copy(rowb[:, u % 2, :, 0:D], xt[:, u, :, :])
                eng.wait_ge(S["mps"], e + (u + 3))
                sc = psa[0:NP, u % 2, 0:TC * 2 * H].rearrange("p (t k) -> p t k", t=TC)
                eng.tensor_copy(rowb[:, u % 2, :, D:D + H], sc[:, :, 0:H]).then_inc(S["row"], 1)
                eng.tensor_copy(nsc[:, ds((e + u) * TC, TC), :], sc).then_inc(S["msb"], 1)
            by_four(eng, score_rows)
            eng.wait_ge(S["msb"], NC + 4)
            dve_max(H, nsc[:, :, 0:H], 1, NP)
            window_rows(H)
            phase_end(eng, 2)
            clear_sums(H * SW, 1)
            dve_pass(eng, G0, regs, bases)
            phase_end(eng, 3)
            dve_max(H, smax[:, :, :], 2, EP)

            def denominators(S, h):
                def keep(e, u):
                    eng.wait_ge(S["ps"], e + (u + 3))
                    ts(dnode[:, ds((e + u) * (TC * h), TC * h)], psa[0:NP, u, 0:TC * h], 1.0, None,
                       ALU.mult).then_inc(S["dn"], 1)
                by_chunk(eng, keep)
                eng.wait_ge(S["dn"], NC + 2)
                eng.sem_inc(alone, 1)

            def reciprocals(S, h, loads):
                def by_node(buf):
                    return buf[:, 0:NT * h].rearrange("p (t h) -> p t h", h=h)
                eng.wait_ge(sp_in, loads)
                link(tt(by_node(rest), by_node(bnode), amax[0:NP, 0:h].unsqueeze(1).to_broadcast([NP, NT, h]),
                        ALU.subtract))
                eng.sem_inc(S["dif"], 1)
                eng.wait_ge(S["ex"], 1)
                dn = dnode[:, 0:NT * h]
                link(eng.scalar_tensor_tensor(dn, rest[:, 0:NT * h], DEN_EPS, dn, ALU.mult, ALU.add))
                link(ts(dn, dn, TINY, None, ALU.max))
                link(eng.reciprocal(dn, dn))
                left = by_node(dnode)
                for r in range(3):
                    part_r = rparts[:, :, r * h:(r + 1) * h]
                    link(eng.tensor_copy(part_r, left))
                    if r < 2:
                        link(tt(by_node(rest), left, part_r, ALU.subtract))
                        left = by_node(rest)
                eng.sem_inc(S["parts"], 1)
            denominators(n_den[0], H)
            reciprocals(n_den[0], H, LOADS_4)

            def normalise_heads(e, u):
                S = n_bn
                eng.wait_ge(S[f"in{u}"], e * 8 + 16)
                eng.wait_ge(S["bc"], e + (u + 1))
                yv = y1[:, u, :, :]
                tt(yv, yv, (psa, psc)[u][:, :, 0:CH], ALU.mult).then_inc(S["row"], 1)
                eng.wait_ge(S["row"], e + (u + 3))
                for p in range(HP):
                    last = eng.bn_stats(stats[:, p, ds(e + u, 1), :].rearrange("p o k -> p (o k)"), y1[:, u, p, :])
                last.then_inc(S["stat"], 1)
            by_chunk(eng, normalise_heads)
            eng.drain().then_inc(dve_l, 1)
            link.k += 1
            eng.wait_ge(dve_l, link.k)

            def inverse_sqrt(out_, var, eps, k):
                link(ts(out_, var, eps, None, ALU.add))
                eng.sem_inc(sqrt_arg, 1)
                eng.wait_ge(sqrt_done, k)
                link(eng.reciprocal(out_, out_))

            def batch_norm(n, gamma, beta, k):
                for p in range(n):
                    link(eng.bn_aggr(mv[:, p, :], stats[:, p, :, :].rearrange("p c k -> p (c k)")))
                inverse_sqrt(scl[:, 0:n], mv[:, 0:n, 1], BN_EPS, k)
                link(tt(scl[:, 0:n], scl[:, 0:n], gamma, ALU.mult))
                link(tt(shf[:, 0:n], mv[:, 0:n, 0], scl[:, 0:n], ALU.mult))
                link(tt(shf[:, 0:n], beta, shf[:, 0:n], ALU.subtract))
            batch_norm(HP, gh[:, :], bh[:, :], 1)
            for p in range(HP):
                link(ts(wob[:, p, :], woa[:, p, :], scl[:, p:p + 1], None, ALU.mult))
            eng.sem_inc(bn_ready, 1)
            eng.wait_ge(bias_ps, 1)
            link(eng.tensor_copy(brow[:, :], p_den[0:1, 0:D + 2]))
            phase_end(eng, 4)
            S = n_msg

            def normalise_again(e, u):
                eng.wait_ge(S[f"in{u}"], e * 8 + 16)
                eng.wait_ge(S["bc"], e + (u + 1))
                yv = y1[:, u, :, :]
                tt(yv, yv, psc[:, :, 0:CH], ALU.mult).then_inc(S["nrm"], 1)
            by_chunk(eng, normalise_again)
            eng.wait_ge(S["msb"], NC + 2)
            dve_max(1, nsc[:, :, 0:1], 3, NP)
            window_rows(1)
            phase_end(eng, 5)
            clear_sums(NW, 2)
            link(eng.memset(smax[:, :, :], -BIG))
            link(eng.memset(s1col[:, :], float(N)))
            link(eng.memset(roff[:, :], 0.0))
            dve_pass(eng, G1, regs, bases)
            phase_end(eng, 6)
            dve_max(1, smax[:, :, 0:1], 4, EP)
            denominators(n_den[1], 1)
            reciprocals(n_den[1], 1, LOADS_7)

            def normalise(e, u):
                S = n_gn
                eng.wait_ge(S["bc"], e + (u + 1))
                cols = acc[:, ds((e + u) * CH, CH)]
                tt(cols, cols, psa[:, u, 0:CH], ALU.mult).then_inc(S["row"], 1)
                eng.wait_ge(S["row"], e + (u + 3))
                eng.bn_stats(stats[:, 0, ds(e + u, 1), :].rearrange("p o k -> p (o k)"), cols)
            by_chunk(eng, normalise)
            eng.drain().then_inc(dve_l, 1)
            link.k += 1
            eng.wait_ge(dve_l, link.k)
            batch_norm(1, go[:, :], bo[:, :], 2)
            phase_end(eng, 7)

            def product(bank):
                return psa[0:NP, bank, 0:TC * D].rearrange("p (t n) -> p t n", t=TC)

            def means_and_rest(own, e, u):
                z = zt[:, u % 2, :, :]
                own(tt(z, product(2 + u % 2), rcnt[:, ds((e + u) * TC, TC)].unsqueeze(2).to_broadcast([NP, TC, D]), ALU.mult))
                own(tt(z, z, product(u % 2), ALU.add))

            def layer_norm(S, split):
                def centre(e, u):
                    own = Links(eng, S["own_a"], (e + u) * (6 if split else 4))
                    eng.wait_ge(S["mps"], e + (u + 3))
                    eng.wait_ge(S["stored"], e + (u + 1))
                    z = zt[:, u % 2, :, :]
                    if split:
                        means_and_rest(own, e, u)
                    own(tt(z, z if split else product(u % 2), xt[:, u, :, :], ALU.add))
                    eng.sem_inc(S["msb"], 1)
                    for t in range(TC):
                        last = eng.bn_stats(lnst[:, u % 2, t, :], zt[:, u % 2, t, :])
                    own(last)
                    eng.sem_inc(alone, 1)
                    for t in range(TC):
                        last = eng.bn_aggr(lnmv[:, u % 2, t, :], lnst[:, u % 2, t, :])
                    own(last)
                    own(ts(lnr[:, u % 2, :], lnmv[:, u % 2, :, 1], LN_EPS, None, ALU.add))
                    eng.sem_inc(S["var"], 1)

                def scale(e, u):
                    own = Links(eng, S["own_b"], (e + u) * 2)
                    eng.wait_ge(S["std"], e + (u + 1))
                    own(eng.reciprocal(lnr[:, u % 2, :], lnr[:, u % 2, :]))
                    own(eng.scalar_tensor_tensor(lnb[:, u % 2, :], lnmv[:, u % 2, :, 0], -1.0, lnr[:, u % 2, :],
                                                 ALU.mult, ALU.mult))
                    eng.sem_inc(S["norm"], 1)
                by_four(eng, centre, scale)
            layer_norm(n_fin[0], False)
            phase_end(eng, 8)
            clear_sums(NW, 3)
            link(eng.memset(roff[:, :], 0.0))
            dve_pass(eng, S0, regs, bases)
            phase_end(eng, 9)

            def fold(loads, k):
                eng.wait_ge(sp_in, loads)
                b_, g_, be_, rm_, rv_ = (vrow[:, i, :] for i in range(5))
                inverse_sqrt(rv_, rv_, BN_EPS, k)
                link(tt(g_, g_, rv_, ALU.mult))
                link(tt(w_a[:, :], w_a[:, :], g_, ALU.mult))
                link(tt(w_b[:, :], w_b[:, :], g_, ALU.mult))
                link(tt(b_, b_, rm_, ALU.subtract))
                link(tt(b_, b_, g_, ALU.mult))
                link(tt(brow[:, 0:D], b_[0:1, :], be_[0:1, :], ALU.add))
            denominators(n_den[2], 1)
            link(ts(rcnt[:, :], dnode[:, 0:NT], 1.0, None, ALU.max))
            link(eng.reciprocal(rcnt[:, :], rcnt[:, :]))
            fold(LOADS_10, 3)
            phase_end(eng, 10)
            S = n_fin[1]

            def relu(e, u):
                eng.wait_ge(S["mps"], e + (u + 3))
                eng.wait_ge(S["stored"], e + (u + 1))
                own = Links(eng, S["own_a"], (e + u) * 2)
                means_and_rest(own, e, u)
                eng.sem_inc(S["msb"], 1)
                ts(zt[:, u % 2, :, :], zt[:, u % 2, :, :], 0.0, None, ALU.max).then_inc(S["row"], 1)
            by_four(eng, relu)
            phase_end(eng, 11)
            clear_sums(NW)
            link(eng.memset(roff[:, :], 0.0))
            dve_pass(eng, S1, regs, bases)
            phase_end(eng, 12)
            fold(LOADS_13, 4)
            phase_end(eng, 13)
            layer_norm(n_fin[2], True)
            phase_end(eng, 14)


def kernel(x, src, dst, **weights):
    import concourse.bacc as bacc
    from concourse.bass_utils import run_bass_kernel_spmd

    def whole_blocks(a, filler):
        return np.pad(np.asarray(a), (0, ET * EP - E), constant_values=filler)

    def by_tile(a):
        return np.ascontiguousarray(a.reshape(ET, EP).T)

    src, dst = whole_blocks(src, 0), whole_blocks(dst, NOWHERE)

    w = {k.split("gnn_")[0] + k.split("gnn_")[1]: np.asarray(v) for k, v in weights.items()}
    arrays = {
        "x": np.asarray(x), "src_t": by_tile(src), "dst_t": by_tile(dst), "dst": dst,
        "W_heads": w["L0_W_heads"], "a_heads": w["L0_a_heads"], "gamma_h": w["L0_gamma_h"], "beta_h": w["L0_beta_h"],
        "W_out": w["L0_W_out"], "a_out": w["L0_a_out"], "gamma_o": w["L0_gamma_o"], "beta_o": w["L0_beta_o"],
        "W_res": w["L0_W_res"], "b_res": w["L0_b_res"],
    }
    for i in range(2):
        arrays[f"Wl{i}"] = w[f"L1_Wl{i}"].T
        arrays[f"Wr{i}"] = w[f"L1_Wr{i}"].T
        for k in ("b", "g", "be", "rm", "rv"):
            arrays[f"{k}{i}"] = w[f"L1_{k}{i}"]
    nc = bacc.Bacc("TRN2", target_bir_lowering=False, num_devices=1)
    feeds, args = {}, {}
    for name, a in arrays.items():
        a = np.ascontiguousarray(a)
        feeds[f"in_{name}"] = a
        args[name] = nc.dram_tensor(f"in_{name}", a.shape, mybir.dt.from_np(a.dtype), kind="ExternalInput").ap()
    args["out"] = nc.dram_tensor("out_0", (N, D), F32, kind="ExternalOutput").ap()
    gnn_kernel(nc, **args)
    return run_bass_kernel_spmd(nc, [feeds], core_ids=[0]).results[0]["out_0"]
```
